# Optimizing a Trainium2 kernel written in Bass

```python
import numpy as np
import jax
import jax.numpy as jnp

def _softmax(x, axis=-1):
    return jax.nn.softmax(x, axis=axis)

def _gelu(x):
    return jax.nn.gelu(x, approximate=True)

def _silu(x):
    return jax.nn.silu(x)

def _sigmoid(x):
    return jax.nn.sigmoid(x)

def _layernorm(x, axis=-1, eps=1e-05):
    m = jnp.mean(x, axis=axis, keepdims=True)
    v = jnp.var(x, axis=axis, keepdims=True)
    return (x - m) / jnp.sqrt(v + eps)

def _scatter_add(tgt, idx, src, axis=0):
    return tgt.at[idx].add(src)

def _segment_sum(src, seg, n):
    return jax.ops.segment_sum(src, seg, n)
kernel_name = 'mk_gnn_ffn_d4_gnn_r64_3b1608'

def setup_inputs(seed: int=0):
    np.random.seed(seed)
    _w = jnp.asarray

    def _rec_inputs():
        import jax
        import jax.numpy as jnp
        _gk = jax.random.key(seed)
        x = 7.22e-05 + 1 * jax.random.normal(jax.random.fold_in(_gk, 1), (256, 512), jnp.float32)
        src = jax.random.randint(jax.random.fold_in(_gk, 2), (8192,), 0, 256, jnp.int32)
        dst = jax.random.randint(jax.random.fold_in(_gk, 3), (8192,), 0, 256, jnp.int32)
        _o = jnp.argsort(dst, stable=True)
        src = src[_o]
        dst = dst[_o]
        edge_attr_128 = -0.00010739 + 0.99994 * jax.random.normal(jax.random.fold_in(_gk, 12), (8192, 128), jnp.float32)
        edge_attr_16 = -0.000585658 + 0.999949 * jax.random.normal(jax.random.fold_in(_gk, 13), (8192, 16), jnp.float32)
        edge_attr_4 = 0.00171547 + 0.999346 * jax.random.normal(jax.random.fold_in(_gk, 14), (8192, 4), jnp.float32)
        edge_attr_8 = 0.000126197 + 0.999763 * jax.random.normal(jax.random.fold_in(_gk, 15), (8192, 8), jnp.float32)
        return (x, src, dst, edge_attr_128, edge_attr_16, edge_attr_4, edge_attr_8)
    x, src, dst, edge_attr_128, edge_attr_16, edge_attr_4, edge_attr_8 = _rec_inputs()

    def _L0_gnn_setup():
        import jax, jax.numpy as jnp
        import numpy as np
        B = 32
        N = 512
        HID = 512
        H = 8
        E = 4096
        ED = 16
        key = jax.random.key(seed)
        ks = jax.random.split(key, 12)
        x = jax.random.normal(ks[0], (B * N, HID), jnp.float32)
        batch = jnp.repeat(jnp.arange(B, dtype=jnp.int64), N)
        g = jax.random.randint(ks[1], (E,), 0, B)
        src = g * N + jax.random.randint(ks[2], (E,), 0, N)
        dst = g * N + jax.random.randint(ks[3], (E,), 0, N)
        edge_index = jnp.stack([src, dst]).astype(jnp.int64)
        edge_attr = jax.random.normal(ks[4], (E, ED), jnp.float32)
        s = 1.0 / np.sqrt(HID).astype(np.float32)
        Wq = jax.random.normal(ks[5], (HID, HID), jnp.float32) * s
        Wk = jax.random.normal(ks[6], (HID, HID), jnp.float32) * s
        Wv = jax.random.normal(ks[7], (HID, HID), jnp.float32) * s
        Wo = jax.random.normal(ks[8], (HID, HID), jnp.float32) * s
        We = jax.random.normal(ks[9], (ED, H), jnp.float32) * (1.0 / np.sqrt(ED).astype(np.float32))
        bq = jnp.zeros((HID,), jnp.float32)
        bk = jnp.zeros((HID,), jnp.float32)
        bv = jnp.zeros((HID,), jnp.float32)
        bo = jnp.zeros((HID,), jnp.float32)
        be = jnp.zeros((H,), jnp.float32)
        return dict(x=x, batch=batch, edge_index=edge_index, edge_attr=edge_attr, Wq=Wq, bq=bq, Wk=Wk, bk=bk, Wv=Wv, bv=bv, Wo=Wo, bo=bo, We=We, be=be, num_graphs=B)
    _L0_gnn_all = _L0_gnn_setup()
    _L0_gnn_in = {k: v for k, v in _L0_gnn_all.items() if k in ('Wq', 'bq', 'Wk', 'bk', 'Wv', 'bv', 'Wo', 'bo', 'We', 'be')}
    del _L0_gnn_all

    def _L0_ffn_setup():
        import jax, jax.numpy as jnp
        import numpy as np
        D, E, DR, K, DFF, DSH = (512, 64, 64, 2, 32, 1024)
        TEMP = 0.7
        SHARED_SCALE = 0.25
        EPS = 1e-05

        def _ln(x, g, b):
            m = jnp.mean(x, axis=-1, keepdims=True)
            v = jnp.mean(jnp.square(x - m), axis=-1, keepdims=True)
            return (x - m) * jax.lax.rsqrt(v + EPS) * g + b
        key = jax.random.key(seed)
        ks = jax.random.split(key, 16)
        s = 0.02
        return {'x': jax.random.normal(ks[0], (1, 512, D), dtype=jnp.float32), 'ln1_g': jnp.ones((D,), jnp.float32), 'ln1_b': jnp.zeros((D,), jnp.float32), 'Wr': jax.random.normal(ks[1], (D, DR), jnp.float32) * s, 'codebook': jax.random.normal(ks[2], (E, DR), jnp.float32), 'W1': jax.random.normal(ks[3], (E, D, DFF), jnp.float32) * s, 'b1': jnp.zeros((E, DFF), jnp.float32), 'W2': jax.random.normal(ks[4], (E, DFF, D), jnp.float32) * s, 'b2': jnp.zeros((E, D), jnp.float32), 'Ws1': jax.random.normal(ks[5], (D, DSH), jnp.float32) * s, 'bs1': jnp.zeros((DSH,), jnp.float32), 'Ws2': jax.random.normal(ks[6], (DSH, D), jnp.float32) * s, 'bs2': jnp.zeros((D,), jnp.float32), 'ffln_g': jnp.ones((D,), jnp.float32), 'ffln_b': jnp.zeros((D,), jnp.float32), 'Wf1': jax.random.normal(ks[7], (D, DFF), jnp.float32) * s, 'bf1': jnp.zeros((DFF,), jnp.float32), 'Wf2': jax.random.normal(ks[8], (DFF, D), jnp.float32) * s, 'bf2': jnp.zeros((D,), jnp.float32)}
    _L0_ffn_all = _L0_ffn_setup()
    _L0_ffn_in = {k: v for k, v in _L0_ffn_all.items() if k in ('ln1_g', 'ln1_b', 'Wr', 'codebook', 'W1', 'b1', 'W2', 'b2', 'Ws1', 'bs1', 'Ws2', 'bs2', 'ffln_g', 'ffln_b', 'Wf1', 'bf1', 'Wf2', 'bf2')}
    del _L0_ffn_all

    def _L1_gnn_setup():
        import jax, jax.numpy as jnp
        import numpy as np
        MUL = 128
        N_NODES = 10000
        N_EDGES = 2500
        R_BASIS = 8
        HIDDEN = 64
        W_NUMEL = 4 * MUL
        SQRT3 = 3.0 ** 0.5
        SILU_2MOM = 1.679177
        AVG_NUM_NEIGHBORS = 10.0

        def _lin_irreps(x0, x1, W0, W1):
            y0 = x0 @ W0 / jnp.sqrt(jnp.float32(W0.shape[0]))
            y1 = jnp.einsum('num,uv->nvm', x1, W1) / jnp.sqrt(jnp.float32(W1.shape[0]))
            return (y0, y1)

        def _forward(node_feats, edge_attrs, edge_feats, edge_index, W_up0, W_up1, W_mlp1, W_mlp2, W_mlp3, W_mlp4, W_out0, W_out1):
            num_nodes = node_feats.shape[0]
            sender, receiver = (edge_index[0], edge_index[1])
            x0 = node_feats[:, :MUL]
            x1 = node_feats[:, MUL:].reshape(num_nodes, MUL, 3)
            x0, x1 = _lin_irreps(x0, x1, W_up0, W_up1)
            h = edge_feats
            for W in (W_mlp1, W_mlp2, W_mlp3):
                h = SILU_2MOM * jax.nn.silu(h @ W / jnp.sqrt(jnp.float32(W.shape[0])))
            tpw = h @ W_mlp4 / jnp.sqrt(jnp.float32(W_mlp4.shape[0]))
            w1, w2, w3, w4 = jnp.split(tpw, 4, axis=-1)
            s0 = x0[sender]
            s1 = x1[sender]
            y0 = edge_attrs[:, 0:1]
            y1 = edge_attrs[:, 1:4]
            p1 = w1 * s0 * y0
            p2 = (w2 * s0)[:, :, None] * y1[:, None, :]
            p3 = w3[:, :, None] * s1 * y0[:, None, :]
            p4 = w4 * jnp.einsum('eum,em->eu', s1, y1) / SQRT3
            m0 = jnp.concatenate([p1, p4], axis=-1)
            m1 = jnp.concatenate([p2, p3], axis=1)
            msg0 = jax.ops.segment_sum(m0, receiver, num_segments=num_nodes)
            msg1 = jax.ops.segment_sum(m1, receiver, num_segments=num_nodes)
            o0, o1 = _lin_irreps(msg0, msg1, W_out0, W_out1)
            out = jnp.concatenate([o0, o1.reshape(num_nodes, 3 * MUL)], axis=-1)
            return out / AVG_NUM_NEIGHBORS
        key = jax.random.key(seed)
        ks = jax.random.split(key, 12)
        rn = lambda k, s: jax.random.normal(k, s, dtype=jnp.float32)
        return {'node_feats': rn(ks[0], (N_NODES, 4 * MUL)), 'edge_attrs': rn(ks[1], (N_EDGES, 4)), 'edge_feats': rn(ks[2], (N_EDGES, R_BASIS)), 'edge_index': jax.random.randint(ks[3], (2, N_EDGES), 0, N_NODES), 'W_up0': rn(ks[4], (MUL, MUL)), 'W_up1': rn(ks[5], (MUL, MUL)), 'W_mlp1': rn(ks[6], (R_BASIS, HIDDEN)), 'W_mlp2': rn(ks[7], (HIDDEN, HIDDEN)), 'W_mlp3': rn(ks[8], (HIDDEN, HIDDEN)), 'W_mlp4': rn(ks[9], (HIDDEN, W_NUMEL)), 'W_out0': rn(ks[10], (2 * MUL, MUL)), 'W_out1': rn(ks[11], (2 * MUL, MUL))}
    _L1_gnn_all = _L1_gnn_setup()
    _L1_gnn_in = {k: v for k, v in _L1_gnn_all.items() if k in ('W_up0', 'W_up1', 'W_mlp1', 'W_mlp2', 'W_mlp3', 'W_mlp4', 'W_out0', 'W_out1')}
    del _L1_gnn_all

    def _L1_ffn_setup():
        import jax, jax.numpy as jnp
        import numpy as np
        B, L, H, E, F, C = (8, 128, 512, 8, 1024, 2)
        key = jax.random.key(seed)
        ks = jax.random.split(key, 4)
        x = jax.random.normal(ks[0], (B, L, H), jnp.float32)
        Wg = jax.random.normal(ks[1], (H, E), jnp.float32) * H ** (-0.5)
        W1 = jax.random.normal(ks[2], (E, H, F), jnp.float32) * H ** (-0.5)
        b1 = jnp.zeros((E, F), jnp.float32)
        W2 = jax.random.normal(ks[3], (E, F, H), jnp.float32) * F ** (-0.5)
        b2 = jnp.zeros((E, H), jnp.float32)
        return {'x': x, 'Wg': Wg, 'W1': W1, 'b1': b1, 'W2': W2, 'b2': b2}
    _L1_ffn_all = _L1_ffn_setup()
    _L1_ffn_in = {k: v for k, v in _L1_ffn_all.items() if k in ('Wg', 'W1', 'b1', 'W2', 'b2')}
    del _L1_ffn_all

    def _L2_gnn_setup():
        import jax, jax.numpy as jnp
        import numpy as np
        N_NODES = 20000
        N_EDGES = 100000
        IN = 512
        HID = 512
        OUT = 512
        EF = 128
        NH = 16
        HEAD = OUT // NH

        def _ln(x):
            mu = jnp.mean(x, axis=-1, keepdims=True)
            var = jnp.var(x, axis=-1, keepdims=True)
            return (x - mu) / jnp.sqrt(var + 1e-05)

        def _mlp(x, W1, b1, g, be, W2, b2):
            hdn = x @ W1 + b1
            hdn = _ln(hdn) * g + be
            hdn = jax.nn.relu(hdn)
            return hdn @ W2 + b2
        key = jax.random.key(seed)
        ks = jax.random.split(key, 16)

        def w(k, i, o):
            return jax.random.normal(k, (i, o), jnp.float32) / np.float32(np.sqrt(i))
        inp = {'h': jax.random.normal(ks[0], (N_NODES, IN), jnp.float32), 'edge_feat': jax.random.normal(ks[1], (N_EDGES, EF), jnp.float32), 'edge_index': jax.random.randint(ks[2], (2, N_EDGES), 0, N_NODES, jnp.int32)}
        inp['hk_W1'] = w(ks[3], IN + EF, HID)
        inp['hk_b1'] = jnp.zeros((HID,), jnp.float32)
        inp['hk_g'] = jnp.ones((HID,), jnp.float32)
        inp['hk_be'] = jnp.zeros((HID,), jnp.float32)
        inp['hk_W2'] = w(ks[4], HID, OUT)
        inp['hk_b2'] = jnp.zeros((OUT,), jnp.float32)
        inp['hv_W1'] = w(ks[5], IN + EF, HID)
        inp['hv_b1'] = jnp.zeros((HID,), jnp.float32)
        inp['hv_g'] = jnp.ones((HID,), jnp.float32)
        inp['hv_be'] = jnp.zeros((HID,), jnp.float32)
        inp['hv_W2'] = w(ks[6], HID, OUT)
        inp['hv_b2'] = jnp.zeros((OUT,), jnp.float32)
        inp['hq_W1'] = w(ks[7], IN, HID)
        inp['hq_b1'] = jnp.zeros((HID,), jnp.float32)
        inp['hq_g'] = jnp.ones((HID,), jnp.float32)
        inp['hq_be'] = jnp.zeros((HID,), jnp.float32)
        inp['hq_W2'] = w(ks[8], HID, OUT)
        inp['hq_b2'] = jnp.zeros((OUT,), jnp.float32)
        inp['no_W1'] = w(ks[9], 2 * HID, HID)
        inp['no_b1'] = jnp.zeros((HID,), jnp.float32)
        inp['no_g'] = jnp.ones((HID,), jnp.float32)
        inp['no_be'] = jnp.zeros((HID,), jnp.float32)
        inp['no_W2'] = w(ks[10], HID, HID)
        inp['no_b2'] = jnp.zeros((HID,), jnp.float32)
        return inp
    _L2_gnn_all = _L2_gnn_setup()
    _L2_gnn_in = {k: v for k, v in _L2_gnn_all.items() if k in ('hk_W1', 'hk_b1', 'hk_g', 'hk_be', 'hk_W2', 'hk_b2', 'hv_W1', 'hv_b1', 'hv_g', 'hv_be', 'hv_W2', 'hv_b2', 'hq_W1', 'hq_b1', 'hq_g', 'hq_be', 'hq_W2', 'hq_b2', 'no_W1', 'no_b1', 'no_g', 'no_be', 'no_W2', 'no_b2')}
    del _L2_gnn_all

    def _L2_ffn_setup():
        import jax, jax.numpy as jnp
        import numpy as np
        S, B, D, F, E, K = (1024, 2, 512, 32, 8, 2)
        key = jax.random.key(seed)
        ks = jax.random.split(key, 12)
        s = lambda *sh: 1.0 / np.sqrt(sh[0])
        inp = {'x': jax.random.normal(ks[0], (S, B, D), dtype=jnp.float32), 'Wg': jax.random.normal(ks[1], (D, E), dtype=jnp.float32) * s(D), 'bg': jnp.zeros((E,), dtype=jnp.float32), 'W1': jax.random.normal(ks[2], (E, D, F), dtype=jnp.float32) * s(D), 'b1': jnp.zeros((E, F), dtype=jnp.float32), 'W2': jax.random.normal(ks[3], (E, F, D), dtype=jnp.float32) * s(F), 'b2': jnp.zeros((E, D), dtype=jnp.float32), 'Ws1': jax.random.normal(ks[4], (D, F), dtype=jnp.float32) * s(D), 'bs1': jnp.zeros((F,), dtype=jnp.float32), 'Ws2': jax.random.normal(ks[5], (F, D), dtype=jnp.float32) * s(F), 'bs2': jnp.zeros((D,), dtype=jnp.float32)}
        return inp
    _L2_ffn_all = _L2_ffn_setup()
    _L2_ffn_in = {k: v for k, v in _L2_ffn_all.items() if k in ('Wg', 'bg', 'W1', 'b1', 'W2', 'b2', 'Ws1', 'bs1', 'Ws2', 'bs2')}
    del _L2_ffn_all

    def _L3_gnn_setup():
        import jax, jax.numpy as jnp
        import numpy as np
        N_NODES = 10000
        N_EDGES = 2500
        D_FEAT = 512
        OUT_CH = 512
        key = jax.random.key(seed)
        k1, k2, k3, k4 = jax.random.split(key, 4)
        x = jax.random.normal(k1, (N_NODES, D_FEAT), dtype=jnp.float32)
        edge_index = jax.random.randint(k2, (N_EDGES, 2), 0, N_NODES, dtype=jnp.int64)
        W = jax.random.normal(k3, (OUT_CH, 2 * D_FEAT), dtype=jnp.float32) / np.sqrt(2 * D_FEAT)
        b = jax.random.normal(k4, (OUT_CH,), dtype=jnp.float32) * 0.01
        return {'x': x, 'edge_index': edge_index, 'num_local_nodes': N_NODES, 'W': W, 'b': b}
    _L3_gnn_all = _L3_gnn_setup()
    _L3_gnn_in = {k: v for k, v in _L3_gnn_all.items() if k in ('W', 'b')}
    del _L3_gnn_all

    def _L3_ffn_setup():
        import jax, jax.numpy as jnp
        import numpy as np
        D = 512
        E = 8
        K = 2
        EXP = 4
        LN_EPS = 1e-05
        key = jax.random.key(seed)
        ks = jax.random.split(key, 8)
        B, T = (8, 32)
        Dh = D * EXP
        x = jax.random.normal(ks[0], (B, T, D), dtype=jnp.float32)
        ln_g = jnp.ones((D,), dtype=jnp.float32)
        ln_b = jnp.zeros((D,), dtype=jnp.float32)
        lim_r = np.sqrt(6.0 / (D + E)).astype(np.float32)
        w_r = jax.random.uniform(ks[1], (E, D), dtype=jnp.float32, minval=-lim_r, maxval=lim_r)
        b_r = jnp.zeros((E,), dtype=jnp.float32)
        lim1 = np.sqrt(6.0 / (D + Dh)).astype(np.float32)
        W1 = jax.random.uniform(ks[2], (E, D, Dh), dtype=jnp.float32, minval=-lim1, maxval=lim1)
        b1 = jnp.zeros((E, Dh), dtype=jnp.float32)
        W2 = jax.random.uniform(ks[3], (E, Dh, D), dtype=jnp.float32, minval=-lim1, maxval=lim1)
        b2 = jnp.zeros((E, D), dtype=jnp.float32)
        return {'x': x, 'ln_g': ln_g, 'ln_b': ln_b, 'w_r': w_r, 'b_r': b_r, 'W1': W1, 'b1': b1, 'W2': W2, 'b2': b2}
    _L3_ffn_all = _L3_ffn_setup()
    _L3_ffn_in = {k: v for k, v in _L3_ffn_all.items() if k in ('ln_g', 'ln_b', 'w_r', 'b_r', 'W1', 'b1', 'W2', 'b2')}
    del _L3_ffn_all
    return {'x': x, 'src': src, 'dst': dst, 'edge_attr_128': edge_attr_128, 'edge_attr_16': edge_attr_16, 'edge_attr_4': edge_attr_4, 'edge_attr_8': edge_attr_8, 'L0_gnn_Wq': _L0_gnn_in['Wq'], 'L0_gnn_bq': _L0_gnn_in['bq'], 'L0_gnn_Wk': _L0_gnn_in['Wk'], 'L0_gnn_bk': _L0_gnn_in['bk'], 'L0_gnn_Wv': _L0_gnn_in['Wv'], 'L0_gnn_bv': _L0_gnn_in['bv'], 'L0_gnn_Wo': _L0_gnn_in['Wo'], 'L0_gnn_bo': _L0_gnn_in['bo'], 'L0_gnn_We': _L0_gnn_in['We'], 'L0_gnn_be': _L0_gnn_in['be'], 'L0_ffn_ln1_g': _L0_ffn_in['ln1_g'], 'L0_ffn_ln1_b': _L0_ffn_in['ln1_b'], 'L0_ffn_Wr': _L0_ffn_in['Wr'], 'L0_ffn_codebook': _L0_ffn_in['codebook'], 'L0_ffn_W1': _L0_ffn_in['W1'], 'L0_ffn_b1': _L0_ffn_in['b1'], 'L0_ffn_W2': _L0_ffn_in['W2'], 'L0_ffn_b2': _L0_ffn_in['b2'], 'L0_ffn_Ws1': _L0_ffn_in['Ws1'], 'L0_ffn_bs1': _L0_ffn_in['bs1'], 'L0_ffn_Ws2': _L0_ffn_in['Ws2'], 'L0_ffn_bs2': _L0_ffn_in['bs2'], 'L0_ffn_ffln_g': _L0_ffn_in['ffln_g'], 'L0_ffn_ffln_b': _L0_ffn_in['ffln_b'], 'L0_ffn_Wf1': _L0_ffn_in['Wf1'], 'L0_ffn_bf1': _L0_ffn_in['bf1'], 'L0_ffn_Wf2': _L0_ffn_in['Wf2'], 'L0_ffn_bf2': _L0_ffn_in['bf2'], 'L1_gnn_W_up0': _L1_gnn_in['W_up0'], 'L1_gnn_W_up1': _L1_gnn_in['W_up1'], 'L1_gnn_W_mlp1': _L1_gnn_in['W_mlp1'], 'L1_gnn_W_mlp2': _L1_gnn_in['W_mlp2'], 'L1_gnn_W_mlp3': _L1_gnn_in['W_mlp3'], 'L1_gnn_W_mlp4': _L1_gnn_in['W_mlp4'], 'L1_gnn_W_out0': _L1_gnn_in['W_out0'], 'L1_gnn_W_out1': _L1_gnn_in['W_out1'], 'L1_ffn_Wg': _L1_ffn_in['Wg'], 'L1_ffn_W1': _L1_ffn_in['W1'], 'L1_ffn_b1': _L1_ffn_in['b1'], 'L1_ffn_W2': _L1_ffn_in['W2'], 'L1_ffn_b2': _L1_ffn_in['b2'], 'L2_gnn_hk_W1': _L2_gnn_in['hk_W1'], 'L2_gnn_hk_b1': _L2_gnn_in['hk_b1'], 'L2_gnn_hk_g': _L2_gnn_in['hk_g'], 'L2_gnn_hk_be': _L2_gnn_in['hk_be'], 'L2_gnn_hk_W2': _L2_gnn_in['hk_W2'], 'L2_gnn_hk_b2': _L2_gnn_in['hk_b2'], 'L2_gnn_hv_W1': _L2_gnn_in['hv_W1'], 'L2_gnn_hv_b1': _L2_gnn_in['hv_b1'], 'L2_gnn_hv_g': _L2_gnn_in['hv_g'], 'L2_gnn_hv_be': _L2_gnn_in['hv_be'], 'L2_gnn_hv_W2': _L2_gnn_in['hv_W2'], 'L2_gnn_hv_b2': _L2_gnn_in['hv_b2'], 'L2_gnn_hq_W1': _L2_gnn_in['hq_W1'], 'L2_gnn_hq_b1': _L2_gnn_in['hq_b1'], 'L2_gnn_hq_g': _L2_gnn_in['hq_g'], 'L2_gnn_hq_be': _L2_gnn_in['hq_be'], 'L2_gnn_hq_W2': _L2_gnn_in['hq_W2'], 'L2_gnn_hq_b2': _L2_gnn_in['hq_b2'], 'L2_gnn_no_W1': _L2_gnn_in['no_W1'], 'L2_gnn_no_b1': _L2_gnn_in['no_b1'], 'L2_gnn_no_g': _L2_gnn_in['no_g'], 'L2_gnn_no_be': _L2_gnn_in['no_be'], 'L2_gnn_no_W2': _L2_gnn_in['no_W2'], 'L2_gnn_no_b2': _L2_gnn_in['no_b2'], 'L2_ffn_Wg': _L2_ffn_in['Wg'], 'L2_ffn_bg': _L2_ffn_in['bg'], 'L2_ffn_W1': _L2_ffn_in['W1'], 'L2_ffn_b1': _L2_ffn_in['b1'], 'L2_ffn_W2': _L2_ffn_in['W2'], 'L2_ffn_b2': _L2_ffn_in['b2'], 'L2_ffn_Ws1': _L2_ffn_in['Ws1'], 'L2_ffn_bs1': _L2_ffn_in['bs1'], 'L2_ffn_Ws2': _L2_ffn_in['Ws2'], 'L2_ffn_bs2': _L2_ffn_in['bs2'], 'L3_gnn_W': _L3_gnn_in['W'], 'L3_gnn_b': _L3_gnn_in['b'], 'L3_ffn_ln_g': _L3_ffn_in['ln_g'], 'L3_ffn_ln_b': _L3_ffn_in['ln_b'], 'L3_ffn_w_r': _L3_ffn_in['w_r'], 'L3_ffn_b_r': _L3_ffn_in['b_r'], 'L3_ffn_W1': _L3_ffn_in['W1'], 'L3_ffn_b1': _L3_ffn_in['b1'], 'L3_ffn_W2': _L3_ffn_in['W2'], 'L3_ffn_b2': _L3_ffn_in['b2']}

def reference(x, src, dst, edge_attr_128, edge_attr_16, edge_attr_4, edge_attr_8, L0_gnn_Wq, L0_gnn_bq, L0_gnn_Wk, L0_gnn_bk, L0_gnn_Wv, L0_gnn_bv, L0_gnn_Wo, L0_gnn_bo, L0_gnn_We, L0_gnn_be, L0_ffn_ln1_g, L0_ffn_ln1_b, L0_ffn_Wr, L0_ffn_codebook, L0_ffn_W1, L0_ffn_b1, L0_ffn_W2, L0_ffn_b2, L0_ffn_Ws1, L0_ffn_bs1, L0_ffn_Ws2, L0_ffn_bs2, L0_ffn_ffln_g, L0_ffn_ffln_b, L0_ffn_Wf1, L0_ffn_bf1, L0_ffn_Wf2, L0_ffn_bf2, L1_gnn_W_up0, L1_gnn_W_up1, L1_gnn_W_mlp1, L1_gnn_W_mlp2, L1_gnn_W_mlp3, L1_gnn_W_mlp4, L1_gnn_W_out0, L1_gnn_W_out1, L1_ffn_Wg, L1_ffn_W1, L1_ffn_b1, L1_ffn_W2, L1_ffn_b2, L2_gnn_hk_W1, L2_gnn_hk_b1, L2_gnn_hk_g, L2_gnn_hk_be, L2_gnn_hk_W2, L2_gnn_hk_b2, L2_gnn_hv_W1, L2_gnn_hv_b1, L2_gnn_hv_g, L2_gnn_hv_be, L2_gnn_hv_W2, L2_gnn_hv_b2, L2_gnn_hq_W1, L2_gnn_hq_b1, L2_gnn_hq_g, L2_gnn_hq_be, L2_gnn_hq_W2, L2_gnn_hq_b2, L2_gnn_no_W1, L2_gnn_no_b1, L2_gnn_no_g, L2_gnn_no_be, L2_gnn_no_W2, L2_gnn_no_b2, L2_ffn_Wg, L2_ffn_bg, L2_ffn_W1, L2_ffn_b1, L2_ffn_W2, L2_ffn_b2, L2_ffn_Ws1, L2_ffn_bs1, L2_ffn_Ws2, L2_ffn_bs2, L3_gnn_W, L3_gnn_b, L3_ffn_ln_g, L3_ffn_ln_b, L3_ffn_w_r, L3_ffn_b_r, L3_ffn_W1, L3_ffn_b1, L3_ffn_W2, L3_ffn_b2):
    import jax
    import jax.numpy as jnp

    def _L0_gnn_ref(x, batch, edge_index, edge_attr, Wq, bq, Wk, bk, Wv, bv, Wo, bo, We, be, num_graphs):
        import jax, jax.numpy as jnp
        import numpy as np
        B = 32
        N = 512
        HID = 512
        H = 8
        E = 4096
        ED = 16
        n_total, hid = x.shape
        n = n_total // num_graphs
        hd = hid // H
        scale = 1.0 / jnp.sqrt(jnp.asarray(hd, x.dtype))
        q = (x @ Wq + bq).reshape(num_graphs, n, H, hd)
        k = (x @ Wk + bk).reshape(num_graphs, n, H, hd)
        v = (x @ Wv + bv).reshape(num_graphs, n, H, hd)
        attn = jnp.einsum('bnhd,bmhd->bnmh', q, k) * scale
        eb = edge_attr @ We + be
        b_idx = edge_index[0] // n
        loc_src = edge_index[0] % n
        loc_dst = edge_index[1] % n
        attn = attn.at[b_idx, loc_src, loc_dst].add(eb)
        attn = jax.nn.softmax(attn, axis=2)
        out = jnp.einsum('bnmh,bmhd->bnhd', attn, v).reshape(n_total, hid)
        return out @ Wo + bo

    def _L0_ffn_ref(x, ln1_g, ln1_b, Wr, codebook, W1, b1, W2, b2, Ws1, bs1, Ws2, bs2, ffln_g, ffln_b, Wf1, bf1, Wf2, bf2):
        import jax, jax.numpy as jnp
        import numpy as np
        D, E, DR, K, DFF, DSH = (512, 64, 64, 2, 32, 1024)
        TEMP = 0.7
        SHARED_SCALE = 0.25
        EPS = 1e-05

        def _ln(x, g, b):
            m = jnp.mean(x, axis=-1, keepdims=True)
            v = jnp.mean(jnp.square(x - m), axis=-1, keepdims=True)
            return (x - m) * jax.lax.rsqrt(v + EPS) * g + b
        B, S, _ = x.shape
        T = B * S
        h = _ln(x, ln1_g, ln1_b).reshape(T, D)
        r = h @ Wr
        logits = r @ codebook.T / TEMP
        probs = jax.nn.softmax(logits, axis=-1)
        vals, idx = jax.lax.top_k(probs, K)
        w = vals / jnp.sum(vals, axis=-1, keepdims=True)
        combine = jnp.zeros((T, E), x.dtype).at[jnp.arange(T)[:, None], idx].set(w)
        eh = jax.nn.silu(jnp.einsum('td,edf->tef', h, W1) + b1)
        eo = jnp.einsum('tef,efd->ted', eh, W2) + b2
        moe = jnp.einsum('te,ted->td', combine, eo)
        shared = (jax.nn.silu(h @ Ws1 + bs1) @ Ws2 + bs2) * SHARED_SCALE
        hmoe = (moe + shared).reshape(B, S, D)
        f = _ln(hmoe, ffln_g, ffln_b)
        f = jax.nn.silu(f @ Wf1 + bf1) @ Wf2 + bf2
        return x + hmoe + f

    def _L1_gnn_ref(node_feats, edge_attrs, edge_feats, edge_index, W_up0, W_up1, W_mlp1, W_mlp2, W_mlp3, W_mlp4, W_out0, W_out1):
        import jax, jax.numpy as jnp
        import numpy as np
        MUL = 128
        N_NODES = 10000
        N_EDGES = 2500
        R_BASIS = 8
        HIDDEN = 64
        W_NUMEL = 4 * MUL
        SQRT3 = 3.0 ** 0.5
        SILU_2MOM = 1.679177
        AVG_NUM_NEIGHBORS = 10.0

        def _lin_irreps(x0, x1, W0, W1):
            y0 = x0 @ W0 / jnp.sqrt(jnp.float32(W0.shape[0]))
            y1 = jnp.einsum('num,uv->nvm', x1, W1) / jnp.sqrt(jnp.float32(W1.shape[0]))
            return (y0, y1)

        def _forward(node_feats, edge_attrs, edge_feats, edge_index, W_up0, W_up1, W_mlp1, W_mlp2, W_mlp3, W_mlp4, W_out0, W_out1):
            num_nodes = node_feats.shape[0]
            sender, receiver = (edge_index[0], edge_index[1])
            x0 = node_feats[:, :MUL]
            x1 = node_feats[:, MUL:].reshape(num_nodes, MUL, 3)
            x0, x1 = _lin_irreps(x0, x1, W_up0, W_up1)
            h = edge_feats
            for W in (W_mlp1, W_mlp2, W_mlp3):
                h = SILU_2MOM * jax.nn.silu(h @ W / jnp.sqrt(jnp.float32(W.shape[0])))
            tpw = h @ W_mlp4 / jnp.sqrt(jnp.float32(W_mlp4.shape[0]))
            w1, w2, w3, w4 = jnp.split(tpw, 4, axis=-1)
            s0 = x0[sender]
            s1 = x1[sender]
            y0 = edge_attrs[:, 0:1]
            y1 = edge_attrs[:, 1:4]
            p1 = w1 * s0 * y0
            p2 = (w2 * s0)[:, :, None] * y1[:, None, :]
            p3 = w3[:, :, None] * s1 * y0[:, None, :]
            p4 = w4 * jnp.einsum('eum,em->eu', s1, y1) / SQRT3
            m0 = jnp.concatenate([p1, p4], axis=-1)
            m1 = jnp.concatenate([p2, p3], axis=1)
            msg0 = jax.ops.segment_sum(m0, receiver, num_segments=num_nodes)
            msg1 = jax.ops.segment_sum(m1, receiver, num_segments=num_nodes)
            o0, o1 = _lin_irreps(msg0, msg1, W_out0, W_out1)
            out = jnp.concatenate([o0, o1.reshape(num_nodes, 3 * MUL)], axis=-1)
            return out / AVG_NUM_NEIGHBORS
        return _forward(node_feats, edge_attrs, edge_feats, edge_index, W_up0, W_up1, W_mlp1, W_mlp2, W_mlp3, W_mlp4, W_out0, W_out1)

    def _L1_ffn_ref(x, Wg, W1, b1, W2, b2):
        import jax, jax.numpy as jnp
        import numpy as np
        B, L, H, E, F, C = (8, 128, 512, 8, 1024, 2)
        b, l, h = x.shape
        e = Wg.shape[1]
        k = min(max(int(l * C / e), 1), l)
        S = jax.nn.softmax(x @ Wg, axis=-1)
        St = jnp.swapaxes(S, 1, 2)
        G, I = jax.lax.top_k(St, k)
        ex = jnp.take_along_axis(x[:, None], I[..., None], axis=2)
        hmid = jax.nn.gelu(jnp.einsum('bekh,ehf->bekf', ex, W1) + b1[None, :, None, :], approximate=False)
        out = jnp.einsum('bekf,efh->bekh', hmid, W2) + b2[None, :, None, :]
        vals = G[..., None] * out
        new_x = jnp.zeros_like(x).at[jnp.arange(b)[:, None, None], I].add(vals)
        return new_x

    def _L2_gnn_ref(h, edge_feat, edge_index, hk_W1, hk_b1, hk_g, hk_be, hk_W2, hk_b2, hv_W1, hv_b1, hv_g, hv_be, hv_W2, hv_b2, hq_W1, hq_b1, hq_g, hq_be, hq_W2, hq_b2, no_W1, no_b1, no_g, no_be, no_W2, no_b2):
        import jax, jax.numpy as jnp
        import numpy as np
        N_NODES = 20000
        N_EDGES = 100000
        IN = 512
        HID = 512
        OUT = 512
        EF = 128
        NH = 16
        HEAD = OUT // NH

        def _ln(x):
            mu = jnp.mean(x, axis=-1, keepdims=True)
            var = jnp.var(x, axis=-1, keepdims=True)
            return (x - mu) / jnp.sqrt(var + 1e-05)

        def _mlp(x, W1, b1, g, be, W2, b2):
            hdn = x @ W1 + b1
            hdn = _ln(hdn) * g + be
            hdn = jax.nn.relu(hdn)
            return hdn @ W2 + b2
        N = h.shape[0]
        src, dst = (edge_index[0], edge_index[1])
        kv_in = jnp.concatenate([h[src], edge_feat], axis=-1)
        k = _mlp(kv_in, hk_W1, hk_b1, hk_g, hk_be, hk_W2, hk_b2).reshape(-1, NH, HEAD)
        v = _mlp(kv_in, hv_W1, hv_b1, hv_g, hv_be, hv_W2, hv_b2).reshape(-1, NH, HEAD)
        q = _mlp(h, hq_W1, hq_b1, hq_g, hq_be, hq_W2, hq_b2).reshape(-1, NH, HEAD)
        logits = jnp.sum(q[dst] * k, axis=-1) / np.float32(np.sqrt(HEAD))
        mx = jax.ops.segment_max(logits, dst, num_segments=N)
        ex = jnp.exp(logits - mx[dst])
        den = jax.ops.segment_sum(ex, dst, num_segments=N)
        alpha = ex / den[dst]
        m = alpha[..., None] * v
        out = jax.ops.segment_sum(m, dst, num_segments=N).reshape(N, OUT)
        out = _mlp(jnp.concatenate([out, h], axis=-1), no_W1, no_b1, no_g, no_be, no_W2, no_b2)
        return out + h

    def _L2_ffn_ref(x, Wg, bg, W1, b1, W2, b2, Ws1, bs1, Ws2, bs2):
        import jax, jax.numpy as jnp
        import numpy as np
        S, B, D, F, E, K = (1024, 2, 512, 32, 8, 2)
        gate_logits = jnp.einsum('sbd,de->sbe', x, Wg) + bg
        weights, selected = jax.lax.top_k(gate_logits, K)
        weights = jax.nn.softmax(weights.astype(jnp.float32), axis=-1)
        onehot = jax.nn.one_hot(selected, E, dtype=weights.dtype)
        comb = jnp.einsum('sbk,sbke->sbe', weights, onehot)
        h = jax.nn.relu(jnp.einsum('sbd,edf->sbef', x, W1) + b1)
        y = jnp.einsum('sbef,efd->sbed', h, W2) + b2
        out = jnp.einsum('sbe,sbed->sbd', comb, y)
        hs = jax.nn.relu(jnp.einsum('sbd,df->sbf', x, Ws1) + bs1)
        shared = jnp.einsum('sbf,fd->sbd', hs, Ws2) + bs2
        out = out + 1.0 / K * shared
        return out

    def _L3_gnn_ref(x, edge_index, num_local_nodes, W, b):
        import jax, jax.numpy as jnp
        import numpy as np
        N_NODES = 10000
        N_EDGES = 2500
        D_FEAT = 512
        OUT_CH = 512
        src = edge_index[:, 0]
        tgt = edge_index[:, 1]
        x_i = x[src]
        x_j = x[tgt]
        x_ij = jnp.concatenate([x_i, x_j], axis=1)
        m_ij = jax.nn.relu(x_ij @ W.T + b)
        out = jax.ops.segment_sum(m_ij, src, num_segments=num_local_nodes)
        return out

    def _L3_ffn_ref(x, ln_g, ln_b, w_r, b_r, W1, b1, W2, b2):
        import jax, jax.numpy as jnp
        import numpy as np
        D = 512
        E = 8
        K = 2
        EXP = 4
        LN_EPS = 1e-05
        B, T, d = x.shape
        mu = jnp.mean(x, axis=-1, keepdims=True)
        var = jnp.mean(jnp.square(x - mu), axis=-1, keepdims=True)
        h = (x - mu) * jax.lax.rsqrt(var + LN_EPS) * ln_g + ln_b
        logits = jnp.einsum('btd,ed->bte', h, w_r) + b_r
        topk_vals, topk_idx = jax.lax.top_k(logits, K)
        gates = jax.nn.softmax(topk_vals, axis=-1)
        hf = h.reshape(B * T, d)
        hid = jax.nn.gelu(jnp.einsum('nd,edf->nef', hf, W1) + b1, approximate=False)
        expert_stack = jnp.einsum('nef,efd->ned', hid, W2) + b2
        idx_flat = topk_idx.reshape(B * T, K)
        gates_flat = gates.reshape(B * T, K)
        gathered = jnp.take_along_axis(expert_stack, idx_flat[:, :, None], axis=1)
        mixed = jnp.sum(gathered * gates_flat[:, :, None], axis=1).reshape(B, T, d)
        return x + mixed
    edge_index = jnp.stack([src, dst])
    edge_index_t = jnp.stack([src, dst], axis=1)
    batch0 = jnp.zeros((256,), jnp.int32)
    x = x + _L0_gnn_ref(_layernorm(x, axis=-1), batch0, edge_index, edge_attr_16, L0_gnn_Wq, L0_gnn_bq, L0_gnn_Wk, L0_gnn_bk, L0_gnn_Wv, L0_gnn_bv, L0_gnn_Wo, L0_gnn_bo, L0_gnn_We, L0_gnn_be, 32)
    x = x + _L0_ffn_ref(_layernorm(x, axis=-1)[None], L0_ffn_ln1_g, L0_ffn_ln1_b, L0_ffn_Wr, L0_ffn_codebook, L0_ffn_W1, L0_ffn_b1, L0_ffn_W2, L0_ffn_b2, L0_ffn_Ws1, L0_ffn_bs1, L0_ffn_Ws2, L0_ffn_bs2, L0_ffn_ffln_g, L0_ffn_ffln_b, L0_ffn_Wf1, L0_ffn_bf1, L0_ffn_Wf2, L0_ffn_bf2)[0]
    x = x + _L1_gnn_ref(_layernorm(x, axis=-1), edge_attr_4, edge_attr_8, edge_index, L1_gnn_W_up0, L1_gnn_W_up1, L1_gnn_W_mlp1, L1_gnn_W_mlp2, L1_gnn_W_mlp3, L1_gnn_W_mlp4, L1_gnn_W_out0, L1_gnn_W_out1)
    x = x + _L1_ffn_ref(_layernorm(x, axis=-1)[None], L1_ffn_Wg, L1_ffn_W1, L1_ffn_b1, L1_ffn_W2, L1_ffn_b2)[0]
    x = x + _L2_gnn_ref(_layernorm(x, axis=-1), edge_attr_128, edge_index, L2_gnn_hk_W1, L2_gnn_hk_b1, L2_gnn_hk_g, L2_gnn_hk_be, L2_gnn_hk_W2, L2_gnn_hk_b2, L2_gnn_hv_W1, L2_gnn_hv_b1, L2_gnn_hv_g, L2_gnn_hv_be, L2_gnn_hv_W2, L2_gnn_hv_b2, L2_gnn_hq_W1, L2_gnn_hq_b1, L2_gnn_hq_g, L2_gnn_hq_be, L2_gnn_hq_W2, L2_gnn_hq_b2, L2_gnn_no_W1, L2_gnn_no_b1, L2_gnn_no_g, L2_gnn_no_be, L2_gnn_no_W2, L2_gnn_no_b2)
    x = x + _L2_ffn_ref(_layernorm(x, axis=-1)[None], L2_ffn_Wg, L2_ffn_bg, L2_ffn_W1, L2_ffn_b1, L2_ffn_W2, L2_ffn_b2, L2_ffn_Ws1, L2_ffn_bs1, L2_ffn_Ws2, L2_ffn_bs2)[0]
    x = x + _L3_gnn_ref(_layernorm(x, axis=-1), edge_index_t, 256, L3_gnn_W, L3_gnn_b)
    x = x + _L3_ffn_ref(_layernorm(x, axis=-1)[None], L3_ffn_ln_g, L3_ffn_ln_b, L3_ffn_w_r, L3_ffn_b_r, L3_ffn_W1, L3_ffn_b1, L3_ffn_W2, L3_ffn_b2)[0]
    return x

_drawn_inputs = setup_inputs


def setup_inputs(seed=0):
    import zlib

    import numpy as np

    out = dict(_drawn_inputs(seed))
    spreads = {'L0_gnn_bq': (0.0, 0.281),
     'L0_gnn_bk': (0.0, 0.8),
     'L0_gnn_bv': (0.0, 0.1),
     'L0_gnn_bo': (0.0, 0.1),
     'L0_gnn_be': (0.0, 0.1),
     'L0_ffn_ln1_g': (1.0, 0.6),
     'L0_ffn_ln1_b': (0.0, 0.636),
     'L0_ffn_b1': (0.0, 0.8),
     'L0_ffn_b2': (0.0, 0.1),
     'L0_ffn_bs1': (0.0, 0.8),
     'L0_ffn_bs2': (0.0, 0.406),
     'L0_ffn_ffln_g': (1.0, 0.6),
     'L0_ffn_ffln_b': (0.0, 0.8),
     'L0_ffn_bf1': (0.0, 0.8),
     'L0_ffn_bf2': (0.0, 0.1),
     'L1_ffn_b1': (0.0, 0.443),
     'L1_ffn_b2': (0.0, 0.396),
     'L2_gnn_hk_b1': (0.0, 0.8),
     'L2_gnn_hk_g': (1.0, 0.6),
     'L2_gnn_hk_be': (0.0, 0.8),
     'L2_gnn_hk_b2': (0.0, 0.8),
     'L2_gnn_hv_b1': (0.0, 0.671),
     'L2_gnn_hv_g': (1.0, 0.6),
     'L2_gnn_hv_be': (0.0, 0.571),
     'L2_gnn_hv_b2': (0.0, 0.353),
     'L2_gnn_hq_b1': (0.0, 0.8),
     'L2_gnn_hq_g': (1.0, 0.6),
     'L2_gnn_hq_be': (0.0, 0.8),
     'L2_gnn_hq_b2': (0.0, 0.8),
     'L2_gnn_no_b1': (0.0, 0.1),
     'L2_gnn_no_g': (1.0, 0.2),
     'L2_gnn_no_be': (0.0, 0.342),
     'L2_gnn_no_b2': (0.0, 0.1),
     'L2_ffn_bg': (0.0, 0.1),
     'L2_ffn_b1': (0.0, 0.609),
     'L2_ffn_b2': (0.0, 0.425),
     'L2_ffn_bs1': (0.0, 0.8),
     'L2_ffn_bs2': (0.0, 0.493),
     'L3_ffn_ln_g': (1.0, 0.6),
     'L3_ffn_ln_b': (0.0, 0.8),
     'L3_ffn_b_r': (0.0, 0.8),
     'L3_ffn_b1': (0.0, 0.8),
     'L3_ffn_b2': (0.0, 0.8)}
    factors = {'edge_attr_128': 3.638,
     'L0_ffn_W1': 4.68,
     'L0_ffn_W2': 3.342,
     'L0_ffn_Ws1': 2.807,
     'L0_ffn_Ws2': 3.099,
     'L0_ffn_Wf1': 4.05,
     'L0_ffn_Wf2': 3.171,
     'L2_gnn_hk_W1': 4.353,
     'L2_gnn_hk_W2': 4.53,
     'L2_gnn_hq_W1': 7.245,
     'L2_gnn_hq_W2': 4.671,
     'L3_gnn_b': 5.639,
     'L3_ffn_w_r': 2.946,
     'L3_ffn_W1': 2.962,
     'L3_ffn_W2': 2.71}
    for name, (base, spread) in spreads.items():
        noise = np.random.default_rng([zlib.crc32(name.encode()), seed]).standard_normal(out[name].shape)
        drawn = base * np.exp(spread * noise) if base else spread * noise
        out[name] = jnp.asarray(drawn.astype(out[name].dtype))
    for name, factor in factors.items():
        out[name] = (out[name] * factor).astype(out[name].dtype)
    return out
```

```python
from contextlib import ExitStack

import numpy as np

import concourse.bass as bass
from concourse import mybir

F32 = mybir.dt.float32
F32R = mybir.dt.float32r
I32 = mybir.dt.int32
U32 = mybir.dt.uint32
ALU = mybir.AluOpType
ACT = mybir.ActivationFunctionType
AX_X = mybir.AxisListType.X

P = 128
N = 256
HALVES = N // P
D = 512
C = D // P
E = 8192
TILES = E // P
EPS = 1e-5
FAR = -1.0e30
FIRST_SEM = 200
LAST = 8


SMALL_SHAPES = {
    "ffn0": {
        "ffn0_ln": (P, 16), "Wr": (P, 4, 64), "codebookT": (64, 64), "ffn0_b1": (P, 24), "ffn0_bs2": (P, D),
        "ffn0_b2": (64, D), "Wf1": (P, 4, 32), "bf1": (32, 1), "Wf2": (32, D), "bf2": (P, D),
    },
    "gnn1": {
        "up0": (P, P), "up1": (P, P), "mlp1": (8, P), "mlp2": (64, P), "mlp3": (64, P), "mlp4": (P, D),
        "out0": (P, 2, P), "out1": (P, 2, P), "attr4": (P, TILES, 4),
    },
    "ffn1": {"ffn1_Wg": (P, 4, 8), "ffn1_b1": (P, 8, 8), "ffn1_b2": (8, D)},
    "ffn2": {
        "ffn2_Wg": (P, 4, 8), "ffn2_bg": (P, 8), "ffn2_W1": (P, 4, 288), "ffn2_b1": (P, 3), "ffn2_W2": (P, 3, D),
        "ffn2_bs2": (P, D), "ffn2_b2": (8, D), "expand2": (8, N),
    },
    "gnn3": {"gnn3_b": (P, D), "gnn3_zero": (P, D)},
    "ffn3": {"ffn3_ln": (P, 8), "ffn3_wr": (P, 4, 8), "ffn3_br": (P, 8), "ffn3_b1": (P, 8, 16), "ffn3_b2": (8, D)},
    "gnn2": {"gnn2_rows": (P, 8, D), "gnn2_cols": (P, 8, 4), "place": (P, TILES), "place1": (P, TILES)},
}


def flat(ap):
    return ap.rearrange("p a b -> p (a b)")


class Stage:

    def __init__(self, nc, name):
        self.nc, self.name = nc, name

    def __enter__(self):
        self.stack = ExitStack()
        self.blocks = ExitStack()
        self.sems = []
        return self

    def sem(self, name):
        s = self.stack.enter_context(self.nc.semaphore(f"{self.name}_{name}", num=FIRST_SEM + len(self.sems)))
        self.sems.append(s)
        return s

    def sb(self, name, shape, dt=F32):
        return self.stack.enter_context(self.nc.sbuf_tensor(f"{self.name}_{name}", shape, dt))

    def block(self):
        return self.blocks.enter_context(self.nc.Block())

    def __exit__(self, *a):
        if a[0] is not None:
            return False
        self.blocks.close()
        numbers = sorted(s.num for s in self.sems)
        if not numbers:
            self.stack.close()
            return False
        assert numbers == list(range(numbers[0], numbers[-1] + 1))
        self.nc.all_engine_barrier(sems_to_clear=range(numbers[0], numbers[-1] + 1))
        self.stack.close()
        return False


class Chain:

    def __init__(self, eng, sem, base=0):
        self.eng, self.sem, self.base, self.n = eng, sem, base, 0

    def link(self, ins):
        self.n += 1
        ins.then_inc(self.sem, 1)
        self.eng.wait_ge(self.sem, self.base + self.n)


def build(nc, t, out):
    with ExitStack() as ctx:
        def sb(name, shape, dt=F32):
            return ctx.enter_context(nc.sbuf_tensor(name, shape, dt))

        def sem(name):
            return ctx.enter_context(nc.semaphore(name))

        r0_at = (nc.sbuf_base + 31) // 32 * 32
        R0 = sb("R0", [P, 16384])
        PS = ctx.enter_context(nc.psum_tensor("PS", [P, 8, 512], F32))
        X = sb("X", [P, HALVES, D])
        XN = sb("XN", [P, HALVES, D])
        HT = sb("HT", [P, C, N])
        ident = sb("ident", [P, P])
        iota = sb("iota", [P, N])
        ones = sb("ones", [P, P])
        src_col = sb("src_col", [P, TILES])
        dst_col = sb("dst_col", [P, TILES])
        pos_i = sb("pos_i", [P, TILES], I32)
        bounds = sb("bounds", [P, HALVES, 2])
        loaded = sem("loaded")
        R1 = sb("R1", [P, 76 * 256])

        def r0(a, shape):
            n = int(np.prod(shape))
            v = R0[:, a:a + n]
            return v.rearrange("p (a b) -> p a b", a=shape[0]) if len(shape) == 2 else v

        def r1(a, shape):
            n = int(np.prod(shape))
            v = R1[:, a:a + n]
            return v.rearrange("p (a b) -> p a b", a=shape[0]) if len(shape) == 2 else v

        Wq, Wk, Wv, Wo = (r0(2048 * k, (C, D)) for k in range(4))
        small = {}

        def layer(name):
            stack = ExitStack()
            with Stage(nc, name + "_small") as st:
                small_in = st.sem("in")
                block = st.block()

                @block.sync
                def _(sp):
                    for key, shape in SMALL_SHAPES[name].items():
                        w = stack.enter_context(nc.sbuf_tensor("s_" + key, list(shape), F32))
                        small[key] = w[tuple(slice(None) for _ in shape)]
                        sp.dma_start(small[key], t[key]).then_inc(small_in, 16)
                    sp.wait_ge(small_in, 16 * len(SMALL_SHAPES[name]))

            return stack

        def col(name, a, b):
            return small[name][:, a:b]

        w_gnn0 = sem("w_gnn0")
        w_ffn0 = sem("w_ffn0")
        w_gnn2 = sem("w_gnn2")
        w_gnn3 = sem("w_gnn3")
        moved = sem("moved")
        ring_in = [sem(f"ring_in{k}") for k in range(4)]
        unit_in = [sem(f"unit_in{k}") for k in range(8)]

        with Stage(nc, "load") as st:
            converted = st.sem("converted")
            src_i, dst_i = st.sb("src_i", [P, TILES], I32), st.sb("dst_i", [P, TILES], I32)
            block = st.block()

            @block.sync
            def _(sp):
                for a, b in ((X[:, :, :], t["x"].rearrange("(h p) d -> p h d", p=P)), (ident[:, :], t["ident"]),
                             (iota[:, :], t["iota"]), (src_i[:, :], t["src"]), (dst_i[:, :], t["dst"])):
                    sp.dma_start(a, b).then_inc(loaded, 16)
                for w, name in ((Wq, "L0_gnn_Wq"), (Wk, "L0_gnn_Wk"), (Wv, "L0_gnn_Wv"), (Wo, "L0_gnn_Wo")):
                    sp.dma_start(w, t[name].rearrange("(c p) n -> p c n", p=P)).then_inc(w_gnn0, 16)

                for a, name in ((r1(0, (C, 2048)), "ffn0_W1"), (r1(8192, (16, D)), "L0_ffn_W2")):
                    sp.dma_start(a, t[name].rearrange("(c p) n -> p c n", p=P)).then_inc(w_ffn0, 16)
                sp.dma_start(R1[0:64, 16384:16384 + 2048], t["expand0"]).then_inc(w_ffn0, 16)

            @block.vector
            def _(dve):
                dve.memset(ones[:, :], 1.0)
                dve.wait_ge(loaded, 5 * 16)
                dve.tensor_copy(src_col[:, :], src_i[:, :])
                dve.tensor_copy(dst_col[:, :], dst_i[:, :]).then_inc(converted, 1)

        def norm_and_turn(name, passes=1, affine=None, turned=True, source=X, columns=None, into=XN,
                          func=ACT.Identity):
            with Stage(nc, name) as st:
                stats = st.sb("stats", [P, HALVES, 6])
                moments = st.sb("moments", [P, HALVES, 2])
                spread = st.sb("spread", [P, HALVES])
                Y = st.sb("Y", [P, HALVES, D]) if passes == 2 else None
                varied, rooted, scaled = st.sem("varied"), st.sem("rooted"), st.sem("scaled")
                dve_chain, turned_half, shifted = st.sem("dve_chain"), st.sem("turned_half"), st.sem("shifted")
                final = into if passes == 1 else Y
                block = st.block()

                @block.vector
                def _(dve):
                    chain = Chain(dve, dve_chain)
                    for k in range(passes):
                        a, b = (source, into) if k == 0 else (into, Y)
                        for h in range(HALVES):
                            chain.link(dve.bn_stats(stats[:, h, :], a[:, h, :]))
                            chain.link(dve.bn_aggr(moments[:, h, :], stats[:, h, :]))
                        dve.tensor_scalar(spread[:, :], moments[:, :, 1], EPS, None, ALU.add).then_inc(varied, 1)
                        dve.wait_ge(rooted, k + 1)
                        chain.link(dve.reciprocal(spread[:, :], spread[:, :]))
                        for h in range(HALVES):
                            ins = dve.tensor_scalar(b[:, h, :], a[:, h, :], moments[:, h, 0:1], spread[:, h:h + 1],
                                                    ALU.subtract, ALU.mult)
                            if k == passes - 1:
                                ins.then_inc(scaled, 1)
                            else:
                                chain.link(ins)

                @block.scalar
                def _(act):
                    for k in range(passes):
                        act.wait_ge(varied, k + 1)
                        act.activation(spread[:, :], spread[:, :], ACT.Sqrt).then_inc(rooted, 1)
                    if turned:
                        for h in range(HALVES):
                            act.wait_ge(turned_half, h + 1)
                            src = PS[:, h, :].rearrange("p (c n) -> p c n", c=C)
                            if affine is None:
                                act.activation(HT[:, :, h * P:(h + 1) * P], src, ACT.Copy)
                            else:
                                for c in range(C):
                                    act.activation(HT[:, c, h * P:(h + 1) * P], src[:, c, :], func,
                                                   bias=affine[1][:, c:c + 1], scale=affine[0][:, c:c + 1])

                @block.tensor
                def _(pe):
                    if turned:
                        for h in range(HALVES):
                            pe.wait_ge(scaled, h + 1)
                            for c in range(C):
                                last = pe.transpose(PS[:, h, c * P:(c + 1) * P],
                                                    columns(final[:, h, :], c) if columns else final[:, h, c * P:(c + 1) * P],
                                                    ident[:, :])
                            last.then_inc(turned_half, 1)

        G, NH0, HD0 = 8, 8, D // 8
        norm_and_turn("gnn0_norm")
        with ExitStack() as keep:
            bias0 = keep.enter_context(nc.sbuf_tensor("bias0", [P, HALVES, G * NH0], F32))
            with Stage(nc, "gnn0_bias") as st:
                attr = R0[0:17, 8192:8192 + E]
                We = st.sb("We", [17, NH0])
                dmod_i = st.sb("dmod_i", [P, TILES], I32)
                dmod = st.sb("dmod", [P, TILES])
                EB = st.sb("EB", [P, TILES, NH0])
                to_slot = st.sb("to_slot", [P, TILES, G])
                spread_bias = st.sb("spread_bias", [P, TILES, G * NH0], F32)
                from_src = st.sb("from_src", [P, 2, N])
                attrs_in, eb_done, eb_out = st.sem("attrs_in"), st.sem("eb_done"), st.sem("eb_out")
                picks, summed, chain_s, bias_sum = st.sem("picks"), st.sem("summed"), st.sem("chain_s"), st.sem("bias_sum")
                block = st.block()

                @block.sync
                def _(sp):
                    sp.dma_start(attr[:, :], t["attr16"]).then_inc(attrs_in, 16)
                    sp.dma_start(We[:, :], t["We17"]).then_inc(attrs_in, 16)
                    sp.dma_start(dmod_i[:, :], t["dst"]).then_inc(attrs_in, 16)

                @block.tensor
                def _(pe):
                    pe.wait_ge(attrs_in, 48)
                    for k in range(TILES):
                        last = pe.matmul(PS[:, 0, k * NH0:(k + 1) * NH0], attr[:, k * P:(k + 1) * P], We[:, :],
                                         start=True, stop=True, skip_group_check=True)
                    last.then_inc(eb_done, 1)
                    pe.wait_ge(eb_out, 1)

                    def tile(k, j, first, end):
                        for h in range(HALVES):
                            last = pe.matmul(PS[:, 1 + h, 0:G * NH0], from_src[:, j, h * P:(h + 1) * P],
                                             spread_bias[:, bass.ds(k, 1), :].rearrange("p a b -> p (a b)"),
                                             start=first, stop=end, skip_group_check=True)
                        last.then_inc(summed, 1)

                    pe.wait_ge(picks, 1)
                    tile(0, 0, True, False)
                    pe.wait_ge(picks, 2)
                    tile(1, 1, False, False)
                    with pe.Fori(1, TILES // 2) as i:
                        for j in range(2):
                            pe.wait_ge(picks, 2 * i + j + 1)
                            tile(2 * i + j, j, False, False)

                @block.vector
                def _(dve):
                    chain = Chain(dve, chain_s)
                    dve.wait_ge(attrs_in, 48)
                    chain.link(dve.tensor_scalar(dmod_i[:, :], dmod_i[:, :], G - 1, None, ALU.bitwise_and))
                    chain.link(dve.tensor_copy(dmod[:, :], dmod_i[:, :]))
                    chain.link(dve.tensor_tensor(to_slot[:, :, :], dmod[:, :].unsqueeze(2).broadcast_to([P, TILES, G]),
                                      iota[:, 0:G].unsqueeze(1).broadcast_to([P, TILES, G]), ALU.is_equal))
                    dve.wait_ge(eb_done, 1)
                    chain.link(dve.tensor_copy(EB[:, :, :], PS[:, 0, :].rearrange("p (a b) -> p a b", b=NH0)))
                    q = TILES // 4
                    for k in range(0, TILES, q):
                        ins = dve.tensor_tensor(
                            spread_bias[:, k:k + q, :].rearrange("p t (m h) -> p t m h", m=G),
                            to_slot[:, k:k + q, :].unsqueeze(3).broadcast_to([P, q, G, NH0]),
                            EB[:, k:k + q, :].unsqueeze(2).broadcast_to([P, q, G, NH0]), ALU.mult)
                        if k == TILES - q:
                            ins.then_inc(eb_out, 1)
                    for k in range(2):
                        dve.tensor_scalar(from_src[:, k, :], iota[:, :], src_col[:, k:k + 1], None,
                                          ALU.is_equal).then_inc(picks, 1)
                    with dve.Fori(1, TILES // 2) as i:
                        for j in range(2):
                            dve.wait_ge(summed, 2 * i + j - 1)
                            dve.tensor_scalar(from_src[:, j, :], iota[:, :], src_col[:, bass.ds(2 * i + j, 1)], None,
                                              ALU.is_equal).then_inc(picks, 1)
                    dve.wait_ge(summed, TILES)
                    for h in range(HALVES):
                        dve.tensor_copy(bias0[:, h, :], PS[:, 1 + h, 0:G * NH0])

            with Stage(nc, "gnn0_attention") as st:
                pair = st.sb("pair", [P, P])
                b4 = st.sb("b4", [P, 4, D])
                b4c = st.sb("b4c", [P, 2, C])
                qT = st.sb("qT", [P, C, N])
                kT = st.sb("kT", [P, C, N])
                V = st.sb("V", [P, HALVES, D])
                S = st.sb("S", [P, NH0, P])
                pT = st.sb("pT", [P, NH0, P])
                top = st.sb("top", [P, NH0])
                total = st.sb("total", [P, NH0])
                A = st.sb("A", [P, D])
                AT = st.sb("AT", [P, C, P])
                names = ("ins", "qk", "qk_out", "vdone", "vout", "scores", "scored", "shifted", "exped", "pturned",
                         "pout", "mixed", "mixed_out", "aturned", "aout", "projected", "chain_v", "chain_a", "added")
                s = {n: st.sem("g0_" + n) for n in names}
                block = st.block()
                bq, bk, bv, bo = (b4[:, k, :] for k in range(4))

                @block.sync
                def _(sp):
                    sp.dma_start(pair[:, :], t["pair"]).then_inc(s["ins"], 16)
                    sp.dma_start(b4c[:, :, :], t["qk_bias"]).then_inc(s["ins"], 16)
                    for k, name in enumerate(("L0_gnn_bv", "L0_gnn_bo")):
                        sp.dma_start(b4[:, 2 + k, :], t[name].unsqueeze(0).broadcast_to([P, D])).then_inc(s["ins"], 16)

                @block.tensor
                def _(pe):
                    pe.wait_ge(w_gnn0, 64)
                    for k, W in enumerate((Wq, Wk)):
                        for m in range(C):
                            for c in range(C):
                                last = pe.matmul(PS[:, 2 * k + m // 2, (m % 2) * N:(m % 2 + 1) * N],
                                                 W[:, c, m * P:(m + 1) * P], HT[:, c, :], start=(c == 0), stop=(c == C - 1),
                                                 skip_group_check=True)
                            last.then_inc(s["qk"], 1)
                    for h in range(HALVES):
                        for c in range(C):
                            last = pe.matmul(PS[:, 4 + h, :], HT[:, c, h * P:(h + 1) * P], Wv[:, c, :],
                                             start=(c == 0), stop=(c == C - 1))
                        last.then_inc(s["vdone"], 1)
                    for h in range(HALVES):
                        pe.wait_ge(s["qk_out"], 2 * C)
                        if h:
                            pe.wait_ge(s["scored"], 2 * h)
                        for a in range(NH0):
                            o = (a % 2) * HD0
                            last = pe.matmul(PS[:, a % 2, (a // 2) * P:(a // 2 + 1) * P],
                                             qT[o:o + HD0, a // 2, h * P:(h + 1) * P],
                                             kT[o:o + HD0, a // 2, h * P:(h + 1) * P], start=True, stop=True,
                                             skip_group_check=True)
                        last.then_inc(s["scores"], 1)
                        pe.wait_ge(s["exped"], h + 1)
                        if h:
                            pe.wait_ge(s["pout"], 2 * h)
                        for a in range(NH0):
                            last = pe.transpose(PS[:, 2 + a // 4, (a % 4) * P:(a % 4 + 1) * P], S[:, a, :], ident[:, :])
                        last.then_inc(s["pturned"], 1)
                        pe.wait_ge(s["pout"], 2 * h + 2)
                        pe.wait_ge(s["vout"], h + 1)
                        for a in range(NH0):
                            last = pe.matmul(PS[:, 6, a * HD0:(a + 1) * HD0], pT[:, a, :],
                                             V[:, h, a * HD0:(a + 1) * HD0], start=True, stop=True,
                                             skip_group_check=True)
                        last.then_inc(s["mixed"], 1)
                        pe.wait_ge(s["mixed_out"], h + 1)
                        for c in range(C):
                            last = pe.transpose(PS[:, 7, c * P:(c + 1) * P], A[:, c * P:(c + 1) * P], ident[:, :])
                        last.then_inc(s["aturned"], 1)
                        pe.wait_ge(s["aout"], h + 1)
                        for c in range(C):
                            last = pe.matmul(PS[:, 4 + h, :], AT[:, c, :], Wo[:, c, :], start=(c == 0), stop=(c == C - 1))
                        last.then_inc(s["projected"], 1)

                @block.scalar
                def _(act):
                    act.wait_ge(s["ins"], 64)
                    for k, dest in enumerate((qT, kT)):
                        for m in range(C):
                            act.wait_ge(s["qk"], (k * C + m // 2 * 2 + 2))
                            act.activation(dest[:, m, :], PS[:, 2 * k + m // 2, (m % 2) * N:(m % 2 + 1) * N],
                                           ACT.Identity, bias=b4c[:, k, m:m + 1]).then_inc(s["qk_out"], 1)
                    for h in range(HALVES):
                        act.wait_ge(s["shifted"], h + 1)
                        act.activation(S[:, :, :], S[:, :, :], ACT.Exp).then_inc(s["exped"], 1)
                        act.wait_ge(s["pturned"], h + 1)
                        for b in range(2):
                            act.activation(pT[:, 4 * b:4 * b + 4, :], PS[:, 2 + b, :].rearrange("p (a b) -> p a b", a=4),
                                           ACT.Copy).then_inc(s["pout"], 1)
                        act.wait_ge(s["aturned"], h + 1)
                        act.activation(AT[:, :, :], PS[:, 7, :].rearrange("p (a b) -> p a b", a=C),
                                       ACT.Copy).then_inc(s["aout"], 1)

                @block.vector
                def _(dve):
                    chain = Chain(dve, s["chain_v"])
                    dve.wait_ge(s["ins"], 64)
                    for h in range(HALVES):
                        dve.wait_ge(s["vdone"], h + 1)
                        dve.tensor_tensor(V[:, h, :], PS[:, 4 + h, :], bv, ALU.add).then_inc(s["vout"], 1)
                    for h in range(HALVES):
                        dve.wait_ge(s["scores"], h + 1)
                        if h:
                            dve.wait_ge(s["pturned"], h)
                        for b in range(2):
                            ins = dve.scalar_tensor_tensor(
                                S[:, b::2, :], PS[:, b, :].rearrange("p (a b) -> p a b", a=4), HD0 ** -0.5,
                                pair[:, :].unsqueeze(1).broadcast_to([P, 4, P]), ALU.mult, ALU.add)
                            ins.then_inc(s["scored"], 1)
                        dve.wait_ge(s["scored"], 2 * h + 2)
                        for a in range(NH0):
                            ins = dve.tensor_tensor(
                                S[:, a, :].rearrange("p (g m) -> p g m", m=G), S[:, a, :].rearrange("p (g m) -> p g m", m=G),
                                bias0[:, h, :].rearrange("p (m h) -> p m h", h=NH0)[:, :, a].unsqueeze(1)
                                .broadcast_to([P, P // G, G]), ALU.add)
                        chain.link(ins)
                        chain.link(dve.tensor_reduce(top[:, :], S[:, :, :], AX_X, ALU.max))
                        dve.tensor_tensor(S[:, :, :], S[:, :, :], top[:, :].unsqueeze(2).broadcast_to([P, NH0, P]),
                                          ALU.subtract).then_inc(s["shifted"], 1)
                        dve.wait_ge(s["exped"], h + 1)
                        chain.link(dve.tensor_reduce(total[:, :], S[:, :, :], AX_X, ALU.add))
                        chain.link(dve.reciprocal(total[:, :], total[:, :]))
                        dve.wait_ge(s["mixed"], h + 1)
                        if h:
                            dve.wait_ge(s["aturned"], h)
                        dve.tensor_tensor(A[:, :].rearrange("p (h d) -> p h d", h=NH0),
                                          PS[:, 6, :].rearrange("p (h d) -> p h d", h=NH0),
                                          total[:, :].unsqueeze(2).broadcast_to([P, NH0, HD0]),
                                          ALU.mult).then_inc(s["mixed_out"], 1)
                        dve.wait_ge(s["projected"], h + 1)
                        chain.link(dve.tensor_tensor(X[:, h, :], X[:, h, :], bo, ALU.add))
                        chain.link(dve.tensor_tensor(X[:, h, :], X[:, h, :], PS[:, 4 + h, :], ALU.add))
        gates = sb("gates", [P, HALVES, 64])
        gatesT = sb("gatesT", [64, N])

        def route(name, n_exp, w, bias=None, codebook=None, scale=1.0):
            with Stage(nc, name) as st:
                rT = st.sb("rT", [64, N])
                logits = st.sb("logits", [P, HALVES, n_exp])
                best = st.sb("best", [P, HALVES, 8])
                at = st.sb("at", [P, HALVES, 8], U32)
                atf = st.sb("atf", [P, HALVES, 8])
                e2 = st.sb("e2", [P, HALVES, 2])
                total = st.sb("total", [P, HALVES])
                r_done, r_out, l_done = st.sem("r_done"), st.sem("r_out"), st.sem("l_done")
                shifted, exped, chosen, turned, v = (st.sem(n) for n in ("shifted", "exped", "chosen", "turned", "v"))
                tout = st.sem("tout")
                block = st.block()

                @block.tensor
                def _(pe):
                    if codebook is not None:
                        for c in range(C):
                            last = pe.matmul(PS[0:64, 0, 0:N], w[:, c, :], HT[:, c, :], start=(c == 0), stop=(c == C - 1))
                        last.then_inc(r_done, 1)
                        pe.wait_ge(r_out, 1)
                    for h in range(HALVES):
                        if codebook is not None:
                            last = pe.matmul(PS[:, 1 + h, 0:n_exp], rT[:, h * P:(h + 1) * P], codebook[:, :],
                                             start=True, stop=True)
                        else:
                            for c in range(C):
                                last = pe.matmul(PS[:, 1 + h, 0:n_exp], HT[:, c, h * P:(h + 1) * P], w[:, c, :],
                                                 start=(c == 0), stop=(c == C - 1))
                        last.then_inc(l_done, 1)
                    pe.wait_ge(chosen, HALVES)
                    for h in range(HALVES):
                        pe.transpose(PS[0:n_exp, 3, h * P:(h + 1) * P], gates[:, h, 0:n_exp],
                                     ident[:, :]).then_inc(turned, 1)

                @block.scalar
                def _(act):
                    if codebook is not None:
                        act.wait_ge(r_done, 1)
                        act.activation(rT[:, :], PS[0:64, 0, 0:N], ACT.Copy).then_inc(r_out, 1)
                    act.wait_ge(shifted, 1)
                    act.activation(e2[:, :, :], e2[:, :, :], ACT.Exp).then_inc(exped, 1)
                    act.wait_ge(turned, HALVES)
                    act.activation(gatesT[0:n_exp, :], PS[0:n_exp, 3, 0:N], ACT.Copy)

                @block.vector
                def _(dve):
                    chain = Chain(dve, v)
                    for h in range(HALVES):
                        dve.wait_ge(l_done, h + 1)
                        if bias is None:
                            chain.link(dve.tensor_scalar(logits[:, h, :], PS[:, 1 + h, 0:n_exp], scale, None, ALU.mult))
                        else:
                            chain.link(dve.tensor_tensor(logits[:, h, :], PS[:, 1 + h, 0:n_exp], bias, ALU.add))
                        chain.link(dve.max(best[:, h, :], logits[:, h, :]))
                        chain.link(dve.max_index(at[:, h, :], best[:, h, :], logits[:, h, :]))
                    chain.link(dve.tensor_copy(atf[:, :, :], at[:, :, :]))
                    dve.tensor_tensor(e2[:, :, :], best[:, :, 0:2], best[:, :, 0:1].broadcast_to([P, HALVES, 2]),
                                      ALU.subtract).then_inc(shifted, 1)
                    dve.wait_ge(exped, 1)
                    chain.link(dve.tensor_reduce(total[:, :], e2[:, :, :], AX_X, ALU.add))
                    chain.link(dve.reciprocal(total[:, :], total[:, :]))
                    chain.link(dve.tensor_tensor(e2[:, :, :], e2[:, :, :], total[:, :].unsqueeze(2).broadcast_to([P, HALVES, 2]),
                                                 ALU.mult))
                    for h in range(HALVES):
                        chain.link(dve.tensor_scalar(gates[:, h, 0:n_exp], iota[:, 0:n_exp], atf[:, h, 0:1], e2[:, h, 0:1],
                                                     ALU.is_equal, ALU.mult))
                        chain.link(dve.tensor_scalar(logits[:, h, :], iota[:, 0:n_exp], atf[:, h, 1:2], e2[:, h, 1:2],
                                                     ALU.is_equal, ALU.mult))
                        dve.tensor_tensor(gates[:, h, 0:n_exp], gates[:, h, 0:n_exp], logits[:, h, :],
                                          ALU.add).then_inc(chosen, 1)

        def mix(name, chunks, hidden, func, w1, b1, w2, out_bias, bias_scale, n_exp=0, b2=None, into_xn=False,
                weights=None):
            with Stage(nc, name) as st:
                h_done, h_out, g_done, ready, y_done, v = (st.sem(n) for n in ("h_done", "h_out", "g_done", "ready", "y_done", "v"))
                block = st.block()
                n = len(chunks)

                @block.tensor
                def _(pe):
                    if weights is not None:
                        pe.wait_ge(*weights)
                    for k, (units, expand, _) in enumerate(chunks):
                        if k >= 2:
                            pe.wait_ge(h_out, k - 1)
                        for c in range(C):
                            last = pe.matmul(PS[0:units, k % 2, 0:N], w1(c, k, units), HT[:, c, :],
                                             start=(c == 0), stop=(c == C - 1))
                        last.then_inc(h_done, 1)
                        if k >= 2:
                            pe.wait_ge(ready, k - 1)
                        if expand is not None:
                            pe.matmul(PS[0:units, 2 + k % 2, 0:N], expand, gatesT[0:n_exp, :],
                                      start=True, stop=True).then_inc(g_done, 1)
                    pe.wait_ge(ready, n)
                    for h in range(HALVES):
                        for k, (units, _, _) in enumerate(chunks):
                            last = pe.matmul(PS[:, 4 + h, :], hidden[0:units, k, h * P:(h + 1) * P], w2(k, units),
                                             start=(k == 0), stop=(k == n - 1 and b2 is None))
                        if b2 is not None:
                            last = pe.matmul(PS[:, 4 + h, :], gatesT[0:n_exp, h * P:(h + 1) * P], b2,
                                             start=False, stop=True)
                        last.then_inc(y_done, 1)

                @block.scalar
                def _(act):
                    for k, (units, _, _) in enumerate(chunks):
                        act.wait_ge(h_done, k + 1)
                        act.activation(hidden[0:units, k, :], PS[0:units, k % 2, 0:N], func,
                                       bias=b1[0:units, k:k + 1]).then_inc(h_out, 1)

                @block.vector
                def _(dve):
                    chain = Chain(dve, v)
                    if into_xn:
                        for h in range(HALVES):
                            chain.link(dve.tensor_tensor(X[:, h, :], X[:, h, :], XN[:, h, :], ALU.add))
                    gated = 0
                    for k, (units, expand, factor) in enumerate(chunks):
                        dve.wait_ge(h_out, k + 1)
                        a = hidden[0:units, k, :]
                        if expand is not None:
                            gated += 1
                            dve.wait_ge(g_done, gated)
                            dve.tensor_tensor(a, a, PS[0:units, 2 + k % 2, 0:N], ALU.mult).then_inc(ready, 1)
                        else:
                            dve.tensor_scalar(a, a, factor, None, ALU.mult).then_inc(ready, 1)
                    for h in range(HALVES):
                        dve.wait_ge(y_done, h + 1)
                        y = XN[:, h, :]
                        chain.link(dve.scalar_tensor_tensor(y, out_bias, bias_scale, PS[:, 4 + h, :], ALU.mult, ALU.add))
                        chain.link(dve.tensor_tensor(X[:, h, :], X[:, h, :], y, ALU.add))

        DFF, DSH, E0 = 32, 1024, 64
        W1_0, W2_0 = r1(0, (C, E0 * DFF)), r1(8192, (E0 * DFF // P, D))
        expand0 = R1[0:64, 16384:16384 + E0 * DFF]
        Ws1_0, Ws2_0 = r0(0, (C, DSH)), r0(4096, (DSH // P, D))
        hidden0 = r0(8192, (24, N))
        if LAST >= 2:
            weights = layer("ffn0")
            with Stage(nc, "ffn0_load") as st:
                block = st.block()

                @block.sync
                def _(sp):
                    sp.dma_start(Ws1_0, t["L0_ffn_Ws1"].rearrange("(c p) n -> p c n", p=P)).then_inc(w_ffn0, 16)
                    sp.dma_start(Ws2_0, t["L0_ffn_Ws2"].rearrange("(c p) n -> p c n", p=P)).then_inc(w_ffn0, 16)
            norm_and_turn("ffn0_norm", passes=2, affine=(col("ffn0_ln", 0, C), col("ffn0_ln", C, 2 * C)))
            route("ffn0_route", E0, small["Wr"], codebook=small["codebookT"], scale=1.0 / 0.7)
            nE = E0 * DFF // P
            mix("ffn0_mix", [(P, expand0[:, k * P:(k + 1) * P], None) for k in range(nE)] + [(P, None, 0.25)] * (DSH // P),
                hidden0, ACT.Silu,
                lambda c, k, u: W1_0[:, c, k * P:(k + 1) * P] if k < nE else Ws1_0[:, c, (k - nE) * P:(k - nE + 1) * P],
                small["ffn0_b1"], lambda k, u: W2_0[:, k, :] if k < nE else Ws2_0[:, k - nE, :],
                small["ffn0_bs2"], 0.25, n_exp=E0, b2=small["ffn0_b2"], into_xn=True, weights=(w_ffn0, 5 * 16))
            norm_and_turn("ffn0_norm2", affine=(col("ffn0_ln", 2 * C, 3 * C), col("ffn0_ln", 3 * C, 4 * C)), source=XN)
            mix("ffn0_last", [(DFF, None, 1.0)], hidden0, ACT.Silu, lambda c, k, u: small["Wf1"][:, c, :],
                small["bf1"], lambda k, u: small["Wf2"][:, :], small["bf2"], 1.0)
            weights.close()

        def guard(eng, semaphore, k, back):
            if not isinstance(k, int) or k >= back:
                eng.wait_ge(semaphore, k - back + 1)

        def over_tiles(eng, body, head=2):
            for k in range(head):
                body(k, k % 2)
            with eng.Fori(head // 2, TILES // 2 - 1) as i:
                for j in range(2):
                    body(2 * i + j, j)
            for k in (TILES - 2, TILES - 1):
                body(k, k % 2)

        B_, HID1 = 8, 64
        MOM = 1.679177
        ring = [r0(4096 * k, (4096,)) for k in range(4)]
        W1_1, W2_1 = t.get("L1_ffn_W1"), t.get("L1_ffn_W2")
        if LAST >= 3:
            weights = layer("gnn1")
            attr8 = R1[0:B_, 0:E]
            h3 = R1[0:HID1, 8192:8192 + E]
            norm_and_turn("gnn1_norm", columns=lambda a, c: a[:, 0:P] if c == 0 else a[:, P + c - 1:D:3])
            keep1 = ExitStack()
            table_hi = keep1.enter_context(nc.sbuf_tensor("table_hi", [P, HALVES, D], F32R))
            table_lo = keep1.enter_context(nc.sbuf_tensor("table_lo", [P, HALVES, D], F32R))
            W4_hi = keep1.enter_context(nc.sbuf_tensor("W4_hi", [P, D], F32R))
            W4_lo = keep1.enter_context(nc.sbuf_tensor("W4_lo", [HID1, D], F32R))
            with Stage(nc, "gnn1_nodes") as st:
                a1 = st.sb("a1", [HID1, 2, D])
                a2 = st.sb("a2", [HID1, 2, D])
                fed, t_done, l1, l2, l3, s1, s2, s3, v = (st.sem(n) for n in
                                                         ("fed", "t_done", "l1", "l2", "l3", "s1", "s2", "s3", "v"))
                block = st.block()
                W1, W2, W3 = small["mlp1"], small["mlp2"], small["mlp3"]
                CH = E // D

                @block.sync
                def _(sp):
                    sp.dma_start(attr8, t["attr8"]).then_inc(fed, 16)
                    for k, w in enumerate((W1_1, W2_1) * 2):
                        sp.dma_start(ring[k], w[k // 2].rearrange("(c p) n -> p c n", p=P)).then_inc(ring_in[k], 16)

                @block.tensor
                def _(pe):
                    for h in range(HALVES):
                        for c in range(C):
                            last = pe.matmul(PS[:, 6 + h, c * P:(c + 1) * P], HT[:, c, h * P:(h + 1) * P],
                                             small["up0"] if c == 0 else small["up1"], start=True, stop=True,
                                             skip_group_check=True)
                        last.then_inc(t_done, 1)
                    pe.wait_ge(fed, 16)

                    def pair(i, peeled):
                        for j in range(2):
                            if not peeled:
                                pe.wait_ge(s1, 2 * i + j - 1)
                            pe.matmul(PS[:, j, :], W1, attr8[:, bass.ds((2 * i + j) * D, D)], start=True,
                                      stop=True).then_inc(l1, 1)
                        for j in range(2):
                            pe.wait_ge(s1, 2 * i + j + 1)
                            if not peeled:
                                pe.wait_ge(s2, 2 * i + j - 1)
                            pe.matmul(PS[:, 2 + j, :], W2, a1[:, j, :], start=True, stop=True).then_inc(l2, 1)
                        for j in range(2):
                            pe.wait_ge(s2, 2 * i + j + 1)
                            if not peeled:
                                pe.wait_ge(s3, 2 * i + j - 1)
                            pe.matmul(PS[:, 4 + j, :], W3, a2[:, j, :], start=True, stop=True).then_inc(l3, 1)

                    pair(0, True)
                    with pe.Fori(1, CH // 2) as i:
                        pair(i, False)

                @block.scalar
                def _(act):
                    def pair(i, peeled):
                        for j in range(2):
                            act.wait_ge(l1, 2 * i + j + 1)
                            if not peeled:
                                act.wait_ge(l2, 2 * i + j - 1)
                            act.activation(a1[:, j, :], PS[0:HID1, j, :], ACT.Silu, scale=B_ ** -0.5).then_inc(s1, 1)
                        for j in range(2):
                            act.wait_ge(l2, 2 * i + j + 1)
                            if not peeled:
                                act.wait_ge(l3, 2 * i + j - 1)
                            act.activation(a2[:, j, :], PS[0:HID1, 2 + j, :], ACT.Silu, scale=MOM / 8).then_inc(s2, 1)
                        for j in range(2):
                            act.wait_ge(l3, 2 * i + j + 1)
                            act.activation(h3[:, bass.ds((2 * i + j) * D, D)], PS[0:HID1, 4 + j, :], ACT.Silu,
                                           scale=MOM / 8).then_inc(s3, 1)

                    pair(0, True)
                    with act.Fori(1, CH // 2) as i:
                        pair(i, False)

                @block.vector
                def _(dve):
                    chain = Chain(dve, v)
                    for h in range(HALVES):
                        dve.wait_ge(t_done, h + 1)
                        chain.link(dve.tensor_copy(table_hi[:, h, :], PS[:, 6 + h, :]))
                        dve.tensor_tensor(table_lo[:, h, :], PS[:, 6 + h, :], table_hi[:, h, :].bitcast(F32), ALU.subtract)
                    chain.link(dve.tensor_copy(W4_hi[:, :], small["mlp4"]))
                    chain.link(dve.tensor_tensor(W4_lo[:, :], small["mlp4"][0:HID1, :], W4_hi[0:HID1, :].bitcast(F32),
                                                 ALU.subtract))

            with Stage(nc, "gnn1_edges") as st:
                from_src = st.sb("from_src", [P, 2, N])
                to_dst = st.sb("to_dst", [P, 2, N])
                pick = st.sb("pick", [P, 2, HALVES, P], F32R)
                h3_2 = st.sb("h3_2", [P, 2, P], F32R)
                w = R1[:, 16384:17408].rearrange("p (j k e) -> p j k e", j=2, k=4)
                prod = R1[:, 17408:18688].rearrange("p (j k e) -> p j k e", j=2, k=5)
                dots = R1[:, 18688:19456].rearrange("p (j k e) -> p j k e", j=2, k=3)
                sum4 = st.sb("sum4", [P, P])
                msg = st.sb("msg", [P, 2, 8, P])
                y = small["attr4"]
                names = ("src_hot", "dst_hot", "hi", "lo", "turned", "turned_out", "w_done", "w_out", "picked", "prods",
                         "msg_a", "msg_v", "summed", "v", "total_out")
                s = {n: st.sem(n) for n in names}
                block = st.block()

                @block.tensor
                def _(pe):
                    def front(k, j):
                        pe.wait_ge(s["src_hot"], k + 1)
                        guard(pe, s["turned_out"], k, 1)
                        for h in range(HALVES):
                            last = pe.transpose(PS[:, 4, h * P:(h + 1) * P], from_src[:, j, h * P:(h + 1) * P], ident[:, :])
                        last.then_inc(s["turned"], 1)
                        pe.wait_ge(s["lo"], k + 1)
                        guard(pe, s["w_out"], k, 1)
                        pe.matmul(PS[:, 5, :], h3_2[:, j, :], W4_hi[:, :], start=True, stop=False)
                        pe.matmul(PS[:, 5, :], h3_2[0:HID1, j, :], W4_lo[:, :], start=False, stop=True).then_inc(s["w_done"], 1)
                        pe.wait_ge(s["turned_out"], k + 1)
                        guard(pe, s["prods"], k, 1)
                        for h in range(HALVES):
                            pe.matmul(PS[:, 6, :], pick[:, j, h, :], table_hi[:, h, :], start=(h == 0), stop=False)
                            last = pe.matmul(PS[:, 6, :], pick[:, j, h, :], table_lo[:, h, :], start=False, stop=(h == 1))
                        last.then_inc(s["picked"], 1)

                    def back(k, j):
                        pe.wait_ge(s["dst_hot"], k + 1)
                        pe.wait_ge(s["msg_a"], k + 1)
                        pe.wait_ge(s["msg_v"], k + 1)
                        for h in range(HALVES):
                            for q in range(2):
                                last = pe.matmul(PS[:, 2 * h + q, :], to_dst[:, j, h * P:(h + 1) * P],
                                                 flat(msg[:, j, 4 * q:4 * q + 4, :]),
                                                 start=(isinstance(k, int) and k == 0),
                                                 stop=(isinstance(k, int) and k == TILES - 1), skip_group_check=True)
                        last.then_inc(s["summed"], 1)

                    def body(k, j):
                        if not (isinstance(k, int) and k == TILES - 1):
                            front(k + 1, 1 - j)
                        back(k, j)

                    front(0, 0)
                    over_tiles(pe, body)

                @block.scalar
                def _(act):
                    def hidden(k, j):
                        guard(act, s["w_done"], k, 2)
                        act.activation(h3_2[0:HID1, j, :], h3[:, bass.ds(k * P, P)], ACT.Copy).then_inc(s["hi"], 1)

                    def leave(k, j):
                        act.wait_ge(s["turned"], k + 1)
                        guard(act, s["picked"], k, 2)
                        act.activation(pick[:, j, :, :], PS[:, 4, 0:N].rearrange("p (a b) -> p a b", a=2),
                                       ACT.Copy).then_inc(s["turned_out"], 1)
                        act.wait_ge(s["w_done"], k + 1)
                        guard(act, s["prods"], k, 2)
                        act.activation(flat(w[:, j, :, :]), PS[:, 5, :], ACT.Copy).then_inc(s["w_out"], 1)

                    def messages(k, j):
                        act.wait_ge(s["prods"], k + 1)
                        guard(act, s["summed"], k, 2)
                        act.activation(msg[:, j, 0:4, :], prod[:, j, 0:4, :], ACT.Copy, scale=y[:, bass.ds(k, 1), 0])
                        for m in range(3):
                            last = act.activation(msg[:, j, 5 + m, :], prod[:, j, 4, :], ACT.Copy,
                                                  scale=y[:, bass.ds(k, 1), 1 + m])
                        last.then_inc(s["msg_a"], 1)

                    def body(k, j):
                        end = isinstance(k, int) and k == TILES - 1
                        if not end:
                            hidden(k + 1, 1 - j)
                        messages(k, j)
                        if not end:
                            leave(k + 1, 1 - j)

                    hidden(0, 0)
                    leave(0, 0)
                    over_tiles(act, body)

                @block.vector
                def _(dve):
                    def hot(k, j):
                        guard(dve, s["turned"], k, 2)
                        dve.tensor_scalar(from_src[:, j, :], iota[:, :], src_col[:, bass.ds(k, 1)], None,
                                          ALU.is_equal).then_inc(s["src_hot"], 1)
                        dve.wait_ge(s["hi"], k + 1)
                        dve.tensor_tensor(h3_2[HID1:P, j, :], h3[:, bass.ds(k * P, P)], h3_2[0:HID1, j, :].bitcast(F32),
                                          ALU.subtract).then_inc(s["lo"], 1)

                    def products(k, j):
                        dve.wait_ge(s["picked"], k + 1)
                        dve.wait_ge(s["w_out"], k + 1)
                        guard(dve, s["msg_a"], k, 2)
                        x = PS[:, 6, :].rearrange("p (a b) -> p a b", a=4)
                        three = lambda a: a.unsqueeze(1).broadcast_to([P, 3, P])
                        dve.tensor_tensor(prod[:, j, 0::4, :], w[:, j, 0:2, :],
                                          x[:, 0, :].unsqueeze(1).broadcast_to([P, 2, P]), ALU.mult)
                        dve.tensor_tensor(prod[:, j, 1:4, :], x[:, 1:4, :], three(w[:, j, 2, :]), ALU.mult)
                        dve.tensor_tensor(dots[:, j, :, :], x[:, 1:4, :], three(w[:, j, 3, :]),
                                          ALU.mult).then_inc(s["prods"], 1)
                        dve.wait_ge(s["prods"], k + 1)
                        dve.tensor_scalar(sum4[:, :], dots[:, j, 0, :], y[:, bass.ds(k, 1), 1], None,
                                          ALU.mult).then_inc(s["v"], 1)
                        dve.wait_ge(s["v"], 2 * k + 1)
                        dve.scalar_tensor_tensor(sum4[:, :], dots[:, j, 1, :], y[:, bass.ds(k, 1), 2], sum4[:, :],
                                                 ALU.mult, ALU.add).then_inc(s["v"], 1)
                        dve.wait_ge(s["v"], 2 * k + 2)
                        guard(dve, s["summed"], k, 2)
                        dve.scalar_tensor_tensor(msg[:, j, 4, :], dots[:, j, 2, :], y[:, bass.ds(k, 1), 3], sum4[:, :],
                                                 ALU.mult, ALU.add).then_inc(s["msg_v"], 1)
                        dve.tensor_scalar(to_dst[:, j, :], iota[:, :], dst_col[:, bass.ds(k, 1)], None,
                                          ALU.is_equal).then_inc(s["dst_hot"], 1)
                        dve.wait_ge(s["msg_v"], k + 1)

                    def body(k, j):
                        if not (isinstance(k, int) and k == TILES - 1):
                            hot(k + 1, 1 - j)
                        products(k, j)

                    hot(0, 0)
                    over_tiles(dve, body)

            with Stage(nc, "gnn1_out") as st:
                sums = st.sb("sums", [P, HALVES, 8, P])
                sumsT = st.sb("sumsT", [P, 8, N])
                out_, turned, tout, done, v = (st.sem(n) for n in ("out", "turned", "tout", "done", "v"))
                block = st.block()
                order = [(0, 4), (5, 1), (6, 2), (7, 3)]

                @block.vector
                def _(dve):
                    chain = Chain(dve, v)
                    for h in range(HALVES):
                        for q in range(2):
                            dve.tensor_copy(flat(sums[:, h, 4 * q:4 * q + 4, :]), PS[:, 2 * h + q, :]).then_inc(out_, 1)
                    scale = MOM / 8 * P ** -0.5 / 16 / 10
                    for h in range(HALVES):
                        dve.wait_ge(done, h + 1)
                        o = PS[:, 6 + h, :].rearrange("p (c n) -> p c n", c=C)
                        chain.link(dve.scalar_tensor_tensor(X[:, h, 0:P], o[:, 0, :], scale, X[:, h, 0:P], ALU.mult, ALU.add))
                        x1 = X[:, h, P:D].rearrange("p (u m) -> p m u", m=3)
                        chain.link(dve.scalar_tensor_tensor(x1, o[:, 1:4, :], scale, x1, ALU.mult, ALU.add))

                @block.tensor
                def _(pe):
                    pe.wait_ge(out_, 4)
                    for k in range(8):
                        if k >= 4:
                            pe.wait_ge(tout, k - 3)
                        for h in range(HALVES):
                            last = pe.transpose(PS[:, k % 4, h * P:(h + 1) * P], sums[:, h, k, :], ident[:, :])
                        last.then_inc(turned, 1)
                    pe.wait_ge(tout, 8)
                    for h in range(HALVES):
                        for c in range(C):
                            W = small["out0"] if c == 0 else small["out1"]
                            for b in range(2):
                                last = pe.matmul(PS[:, 6 + h, c * P:(c + 1) * P], sumsT[:, order[c][b], h * P:(h + 1) * P],
                                                 W[:, b, :], start=(b == 0), stop=(b == 1), skip_group_check=True)
                        last.then_inc(done, 1)

                @block.scalar
                def _(act):
                    for k in range(8):
                        act.wait_ge(turned, k + 1)
                        act.activation(sumsT[:, k, :], PS[:, k % 4, 0:N], ACT.Copy,
                                       scale=3 ** -0.5 if k == 4 else 1.0).then_inc(tout, 1)
            keep1.close()
            weights.close()
        NE1, CAP, F1 = 8, 64, 1024
        FC1 = F1 // P
        if LAST >= 4:
            weights = layer("ffn1")
            norm_and_turn("ffn1_norm")
            keep1 = ExitStack()
            chosenT = keep1.enter_context(nc.sbuf_tensor("chosenT", [P, 4, N], F32))
            exT = keep1.enter_context(nc.sbuf_tensor("exT", [P, C, NE1 * CAP], F32))
            Yp = R1[:, 0:4 * D].rearrange("p (g d) -> p g d", g=4)
            with Stage(nc, "ffn1_choose") as st:
                before = R1[:, 2048:2048 + 512].rearrange("p (h n) -> p h n", h=2)
                S8 = st.sb("S8", [P, HALVES, NE1])
                S8T = st.sb("S8T", [NE1, N])
                sel = st.sb("sel", [NE1, NE1, P])
                best = st.sb("best", [P, HALVES])
                above = st.sb("above", [P, HALVES, NE1])
                level = st.sb("level", [P, HALVES, NE1])
                junk = R1[:, 2560:2560 + 256]
                place = R1[:, 3072:3072 + 1024].rearrange("p (h s) -> p h s", h=2)
                placeG = R1[:, 4096:4096 + 1024].rearrange("p (h s) -> p h s", h=2)
                names = ("ins", "logits", "shifted", "exped", "probs", "turned", "turned_out", "spread_", "ranked",
                         "placed", "gathered", "gturned", "g8", "v")
                s = {n: st.sem(n) for n in names}
                block = st.block()

                @block.sync
                def _(sp):
                    sp.dma_start(before, t["before"]).then_inc(s["ins"], 16)
                    sp.dma_start(sel[:, :, :], t["select8"]).then_inc(s["ins"], 16)

                @block.tensor
                def _(pe):
                    pe.wait_ge(s["ins"], 32)
                    for h in range(HALVES):
                        for c in range(C):
                            last = pe.matmul(PS[:, 4 + h, 0:NE1], HT[:, c, h * P:(h + 1) * P], small["ffn1_Wg"][:, c, :],
                                             start=(c == 0), stop=(c == C - 1))
                        last.then_inc(s["logits"], 1)
                    pe.wait_ge(s["probs"], HALVES)
                    for h in range(HALVES):
                        last = pe.transpose(PS[0:NE1, 6, h * P:(h + 1) * P], S8[:, h, :], ident[:, :])
                    last.then_inc(s["turned"], 1)
                    pe.wait_ge(s["turned_out"], 1)
                    for e in range(NE1):
                        last = pe.matmul(PS[:, e // 2, (e % 2) * N:(e % 2 + 1) * N], sel[:, e, :], S8T[:, :], start=True,
                                         stop=True, skip_group_check=True)
                    last.then_inc(s["spread_"], 1)
                    pe.wait_ge(s["placed"], 1)
                    for c in range(C):
                        for h in range(HALVES):
                            last = pe.matmul(PS[:, c, :], XN[:, h, c * P:(c + 1) * P], place[:, h, :], start=(h == 0),
                                             stop=(h == 1))
                        last.then_inc(s["gathered"], 1)
                    for h in range(HALVES):
                        for g in range(4):
                            last = pe.transpose(PS[:, 4 + h, g * P:(g + 1) * P], placeG[:, h, g * P:(g + 1) * P], ident[:, :])
                        last.then_inc(s["gturned"], 1)
                    for h in range(HALVES):
                        last = pe.transpose(PS[0:NE1, 6, h * P:(h + 1) * P], gates[:, h, 0:NE1], ident[:, :])
                    last.then_inc(s["g8"], 1)

                @block.scalar
                def _(act):
                    act.wait_ge(s["shifted"], 1)
                    act.activation(S8[:, :, :], S8[:, :, :], ACT.Exp).then_inc(s["exped"], 1)
                    act.wait_ge(s["turned"], 1)
                    act.activation(S8T[:, :], PS[0:NE1, 6, 0:N], ACT.Copy).then_inc(s["turned_out"], 1)
                    for c in range(C):
                        act.wait_ge(s["gathered"], c + 1)
                        act.activation(exT[:, c, :], PS[:, c, :], ACT.Copy)
                    for h in range(HALVES):
                        act.wait_ge(s["gturned"], h + 1)
                        act.activation(chosenT[:, :, h * P:(h + 1) * P],
                                       PS[:, 4 + h, :].rearrange("p (g n) -> p g n", g=4), ACT.Copy)
                    act.wait_ge(s["g8"], 1)
                    act.activation(gatesT[0:NE1, :], PS[0:NE1, 6, 0:N], ACT.Copy)

                @block.vector
                def _(dve):
                    chain = Chain(dve, s["v"])
                    wide = lambda a: a.unsqueeze(2).broadcast_to([P, HALVES, NE1])
                    for h in range(HALVES):
                        dve.wait_ge(s["logits"], h + 1)
                        chain.link(dve.tensor_copy(S8[:, h, :], PS[:, 4 + h, 0:NE1]))
                    chain.link(dve.tensor_reduce(best[:, :], S8[:, :, :], AX_X, ALU.max))
                    dve.tensor_tensor(S8[:, :, :], S8[:, :, :], wide(best[:, :]), ALU.subtract).then_inc(s["shifted"], 1)
                    dve.wait_ge(s["exped"], 1)
                    chain.link(dve.tensor_reduce(best[:, :], S8[:, :, :], AX_X, ALU.add))
                    chain.link(dve.reciprocal(best[:, :], best[:, :]))
                    dve.tensor_tensor(S8[:, :, :], S8[:, :, :], wide(best[:, :]), ALU.mult).then_inc(s["probs"], HALVES)
                    dve.wait_ge(s["ins"], 32)
                    dve.wait_ge(s["spread_"], 1)
                    dve.wait_ge(s["probs"], HALVES)
                    for h in range(HALVES):
                        for e in range(NE1):
                            row = PS[:, e // 2, (e % 2) * N:(e % 2 + 1) * N]
                            chain.link(dve.tensor_scalar(junk, row, S8[:, h, e:e + 1], 0.0, ALU.is_gt, ALU.add,
                                                         accum_out=above[:, h, e:e + 1]))
                            chain.link(dve.scalar_tensor_tensor(junk, row, S8[:, h, e:e + 1], before[:, h, :],
                                                                ALU.is_equal, ALU.mult,
                                                                accum_out=level[:, h, e:e + 1]))
                    chain.link(dve.tensor_tensor(above[:, :, :], above[:, :, :], level[:, :, :], ALU.add))
                    chain.link(dve.scalar_tensor_tensor(gates[:, :, 0:NE1], above[:, :, :], float(CAP), S8[:, :, :],
                                                        ALU.is_lt, ALU.mult))
                    for h in range(HALVES):
                        for e in range(NE1):
                            a = slice(e * CAP, (e + 1) * CAP)
                            dve.tensor_scalar(place[:, h, a], iota[:, 0:CAP], above[:, h, e:e + 1], None, ALU.is_equal)
                            last = dve.tensor_scalar(placeG[:, h, a], iota[:, 0:CAP], above[:, h, e:e + 1],
                                                     S8[:, h, e:e + 1], ALU.is_equal, ALU.mult)
                    last.then_inc(s["placed"], 1)

            with Stage(nc, "ffn1_experts") as st:
                hid = st.sb("hid", [P, 2, FC1, CAP])
                names = ("h_done", "h_out", "y_done", "y_out")
                s = {n: st.sem(n) for n in names}
                b1c = small["ffn1_b1"]
                block = st.block()

                @block.sync
                def _(sp):
                    for g in range(1, 4):
                        for k, w in enumerate((W1_1, W2_1) * 2):
                            sp.wait_ge(s["h_done"] if k % 2 == 0 else s["y_done"], 2 * g - 1 + k // 2)
                            sp.dma_start(ring[k], w[2 * g + k // 2].rearrange("(c p) n -> p c n", p=P)).then_inc(ring_in[k], 16)

                @block.tensor
                def _(pe):
                    def expert(g, j, first):
                        W1 = ring[2 * j].rearrange("p (c n) -> p c n", c=C)
                        W2 = ring[2 * j + 1].rearrange("p (c n) -> p c n", c=FC1)
                        pe.wait_ge(ring_in[2 * j], 16 * g + 16)
                        if not first:
                            pe.wait_ge(s["h_out"], 2 * g + j - 1)
                        for f in range(FC1):
                            for c in range(C):
                                last = pe.matmul(PS[:, j, f * CAP:(f + 1) * CAP], W1[:, c, f * P:(f + 1) * P],
                                                 exT[:, c, bass.ds((2 * g + j) * CAP, CAP)], start=(c == 0),
                                                 stop=(c == C - 1), skip_group_check=True)
                        last.then_inc(s["h_done"], 1)

                    def result(g, j, first):
                        W2 = ring[2 * j + 1].rearrange("p (c n) -> p c n", c=FC1)
                        pe.wait_ge(ring_in[2 * j + 1], 16 * g + 16)
                        pe.wait_ge(s["h_out"], 2 * g + j + 1)
                        if not first:
                            pe.wait_ge(s["y_out"], 2 * g + j - 1)
                        for f in range(FC1):
                            last = pe.matmul(PS[j * CAP:(j + 1) * CAP, 2 + j, :], hid[:, j, f, :], W2[:, f, :],
                                             start=(f == 0), stop=(f == FC1 - 1))
                        last.then_inc(s["y_done"], 1)

                    for j in range(2):
                        expert(0, j, True)
                    for j in range(2):
                        result(0, j, True)
                    with pe.Fori(1, 4) as g:
                        for j in range(2):
                            expert(g, j, False)
                        for j in range(2):
                            result(g, j, False)

                @block.scalar
                def _(act):
                    def expert(g, j, first):
                        act.wait_ge(s["h_done"], 2 * g + j + 1)
                        if not first:
                            act.wait_ge(s["y_done"], 2 * g + j - 1)
                        for f in range(FC1):
                            last = act.activation(hid[:, j, f, :], PS[:, j, f * CAP:(f + 1) * CAP], ACT.Gelu,
                                                  bias=b1c[:, bass.ds(2 * g + j, 1), f])
                        last.then_inc(s["h_out"], 1)

                    for j in range(2):
                        expert(0, j, True)
                    with act.Fori(1, 4) as g:
                        for j in range(2):
                            expert(g, j, False)

                @block.vector
                def _(dve):
                    with dve.Fori(0, 4) as g:
                        for j in range(2):
                            dve.wait_ge(s["y_done"], 2 * g + j + 1)
                            dve.tensor_copy(Yp[j * CAP:(j + 1) * CAP, bass.ds(g, 1), :].rearrange("p a b -> p (a b)"),
                                            PS[j * CAP:(j + 1) * CAP, 2 + j, :]).then_inc(s["y_out"], 1)

            with Stage(nc, "ffn1_out") as st:
                done, v = st.sem("done"), st.sem("v")
                block = st.block()

                @block.tensor
                def _(pe):
                    for h in range(HALVES):
                        for g in range(4):
                            pe.matmul(PS[:, h, :], chosenT[:, g, h * P:(h + 1) * P], Yp[:, g, :], start=(g == 0), stop=False)
                        pe.matmul(PS[:, h, :], gatesT[0:NE1, h * P:(h + 1) * P], small["ffn1_b2"][:, :], start=False,
                                  stop=True).then_inc(done, 1)

                @block.vector
                def _(dve):
                    chain = Chain(dve, v)
                    for h in range(HALVES):
                        dve.wait_ge(done, h + 1)
                        chain.link(dve.tensor_tensor(X[:, h, :], X[:, h, :], PS[:, h, :], ALU.add))
            keep1.close()
            weights.close()
        EF, NH2, HD2 = 128, 16, 32
        ROW = EF + 2

        def project(name, parts, bias, sink, waits=()):
            with Stage(nc, name) as st:
                done = st.sem("done")
                block = st.block()

                @block.tensor
                def _(pe):
                    for w in waits:
                        pe.wait_ge(*w)
                    for h in range(HALVES):
                        every = [(a, W, c) for a, W, m in parts for c in range(m)]
                        for q, (a, W, c) in enumerate(every):
                            last = pe.matmul(PS[:, h, :], a[:, c, h * P:(h + 1) * P], W[:, c, :], start=(q == 0),
                                             stop=(q == len(every) - 1))
                        last.then_inc(done, 1)

                @block.vector
                def _(dve):
                    for h in range(HALVES):
                        dve.wait_ge(done, h + 1)
                        dve.tensor_tensor(sink[:, h, :], PS[:, h, :], bias, ALU.add)

        def split(name, pairs, start=None):
            with Stage(nc, name) as st:
                v = st.sem("v")
                block = st.block()

                @block.vector
                def _(dve):
                    chain = Chain(dve, v)
                    for a, hi, lo in pairs:
                        chain.link(dve.tensor_copy(hi, a))
                        chain.link(dve.tensor_tensor(lo, a, hi.bitcast(F32), ALU.subtract))

        if LAST >= 5:
            weights = layer("gnn2")
            scratch = nc.dram_tensor("sorted_edges", (E, ROW), F32, kind="Internal").ap()
            pens = nc.dram_tensor("pens", (2, E), F32, kind="Internal").ap()
            at, W2 = 0, {}
            for name, n in (("hk_W1a", 4), ("hk_W1b", 1), ("hv_W1a", 4), ("hv_W1b", 1), ("hq_W1", 4), ("hk_W2", 4),
                            ("hv_W2", 4), ("hq_W2", 4), ("no_W1", 8), ("no_W2", 4)):
                W2[name] = r1(at, (n, D))
                at += n * D
            edges = R0[:, 0:TILES * ROW].rearrange("p (t r) -> p t r", r=ROW)
            with Stage(nc, "gnn2_rank") as st:
                BF = mybir.dt.bfloat16
                pos = st.sb("pos", [P, TILES])
                masks = st.sb("masks", [P, 2, P])
                strict = st.sb("strict", [P, 2, P], BF)
                onesb = st.sb("onesb", [P, P], BF)
                below = st.sb("below", [P, 2, N], BF)
                hot = st.sb("hot", [P, 2, N], BF)
                junk = st.sb("junk", [P, N])
                total = st.sb("total", [P, 2, N])
                names = ("ins", "consts", "under", "counted", "first_out", "hots", "ranked", "read", "closed", "last_out",
                         "turned", "v", "pos_done")
                s = {n: st.sem(n) for n in names}
                block = st.block()

                @block.sync
                def _(sp):
                    sp.dma_start(masks[:, :, :], t["masks"]).then_inc(s["ins"], 16)
                    sp.dma_start(edges[:, :, 0:EF], t["attr128"]).then_inc(s["ins"], 16)
                    for name, w in W2.items():
                        sp.dma_start(w, t["g2_" + name].rearrange("(c p) n -> p c n", p=P)).then_inc(w_gnn2, 16)

                @block.tensor
                def _(pe):
                    def count(k, j, first):
                        pe.wait_ge(s["under"], k + 1)
                        pe.matmul(PS[:, 0, 0:N], onesb[:, :], below[:, j, :], start=first, stop=False,
                                  skip_group_check=True).then_inc(s["counted"], 1)

                    pe.wait_ge(s["consts"], 1)
                    count(0, 0, True)
                    count(1, 1, False)
                    with pe.Fori(1, TILES // 2) as i:
                        for j in range(2):
                            count(2 * i + j, j, False)
                    pe.wait_ge(s["first_out"], 1)
                    with pe.Fori(0, TILES // 2) as i:
                        for j in range(2):
                            pe.wait_ge(s["hots"], 2 * i + j + 1)
                            pe.matmul(PS[:, 0, 0:N], strict[:, 0, :], hot[:, j, :], start=False, stop=False,
                                      skip_group_check=True).then_inc(s["ranked"], 1)
                            pe.wait_ge(s["read"], 2 * i + j + 1)
                            pe.matmul(PS[:, 0, 0:N], strict[:, 1, :], hot[:, j, :], start=False, stop=False,
                                      skip_group_check=True).then_inc(s["closed"], 1)
                    pe.wait_ge(s["last_out"], 1)
                    for q in range(2):
                        for h in range(HALVES):
                            last = pe.transpose(PS[:, 2 + q, h * P:(h + 1) * P], total[:, q, h * P:(h + 1) * P], ident[:, :])
                    last.then_inc(s["turned"], 1)

                @block.vector
                def _(dve):
                    chain = Chain(dve, s["v"])
                    dve.wait_ge(s["ins"], 32)
                    dve.memset(onesb[:, :], 1.0)
                    dve.tensor_copy(edges[:, :, EF], src_col[:, :])
                    dve.tensor_copy(edges[:, :, EF + 1], dst_col[:, :])
                    dve.tensor_copy(strict[:, :, :], masks[:, :, :]).then_inc(s["consts"], 1)

                    def under(k, j, first):
                        if not first:
                            dve.wait_ge(s["counted"], k - 1)
                        dve.tensor_scalar(below[:, j, :], iota[:, :], dst_col[:, bass.ds(k, 1)], None,
                                          ALU.is_gt).then_inc(s["under"], 1)

                    under(0, 0, True)
                    under(1, 1, True)
                    with dve.Fori(1, TILES // 2) as i:
                        for j in range(2):
                            under(2 * i + j, j, False)
                    dve.wait_ge(s["counted"], TILES)
                    dve.tensor_copy(total[:, 0, :], PS[:, 0, 0:N]).then_inc(s["first_out"], 1)

                    def hots(k, j, first):
                        if not first:
                            dve.wait_ge(s["closed"], k - 1)
                        dve.tensor_scalar(hot[:, j, :], iota[:, :], dst_col[:, bass.ds(k, 1)], None,
                                          ALU.is_equal).then_inc(s["hots"], 1)

                    def ranked(k, j):
                        dve.wait_ge(s["ranked"], k + 1)
                        dve.scalar_tensor_tensor(junk[:, :], PS[:, 0, 0:N], 1.0, hot[:, j, :], ALU.mult, ALU.mult,
                                                 accum_out=pos[:, bass.ds(k, 1)]).then_inc(s["read"], 1)
                        dve.wait_ge(s["read"], k + 1)

                    hots(0, 0, True)
                    hots(1, 1, True)
                    with dve.Fori(0, TILES // 2 - 1) as i:
                        for j in range(2):
                            ranked(2 * i + j, j)
                            hots(2 * i + j + 2, j, False)
                    for k in (TILES - 2, TILES - 1):
                        ranked(k, k % 2)
                    chain.link(dve.tensor_copy(pos_i[:, :], pos[:, :]))
                    dve.wait_ge(s["closed"], TILES)
                    dve.tensor_copy(total[:, 1, :], PS[:, 0, 0:N]).then_inc(s["last_out"], 1)
                    dve.wait_ge(s["turned"], 1)
                    for q in range(2):
                        dve.tensor_copy(bounds[:, :, q], PS[:, 2 + q, 0:N:P])

            q2 = ExitStack()
            sr = lambda name, shape: q2.enter_context(nc.sbuf_tensor(name, shape, F32R))
            A_hi, A_lo = sr("A_hi", [P, HALVES, D]), sr("A_lo", [P, HALVES, D])
            Q_hi, Q_lo = sr("Q_hi", [P, HALVES, D]), sr("Q_lo", [P, HALVES, D])
            NX = NH2 + 2
            X_hi, X_lo = sr("X_hi", [P, HALVES, NX]), sr("X_lo", [P, HALVES, NX])
            with Stage(nc, "gnn2_sort") as st:
                block = st.block()

                @block.gpsimd
                def _(pool):
                    for k in range(TILES):
                        pool.indirect_dma_start(scratch, bass.IndirectOffsetOnAxis(ap=pos_i[:, k:k + 1], axis=0),
                                                edges[:, k, :], None, bounds_check=E - 1).then_inc(moved, 16)
                    pool.wait_ge(moved, 16 * TILES)

            u = 8192
            def up(shape):
                upper_at[0] += int(np.prod(shape))
                v = R0[:, upper_at[0] - int(np.prod(shape)):upper_at[0]]
                return v.rearrange("p (a b) -> p a b", a=shape[0]) if len(shape) == 2 else v
            upper_at = [u]
            L = up((TILES, NH2))
            node_k, node_v, hid_no = up((HALVES, D)), up((HALVES, D)), up((HALVES, D))
            extra = q2.enter_context(nc.sbuf_tensor("extra", [P, HALVES, NX], F32))
            norm_and_turn("gnn2_norm")
            wait2 = [(w_gnn2, 16 * len(W2))]
            rows2 = {n: small["gnn2_rows"][:, k, :] for k, n in enumerate(("hk_b1", "hv_b1", "hq_b1", "hk_b2", "hv_b2",
                                                                          "hq_b2", "no_b1", "no_b2"))}
            cols2 = {n: (small["gnn2_cols"][:, 2 * k, :], small["gnn2_cols"][:, 2 * k + 1, :])
                     for k, n in enumerate(("hk", "hv", "hq", "no"))}
            qh = R0[:, 0:1024].rearrange("p (h d) -> p h d", h=2)
            project("gnn2_nk", [(HT, W2["hk_W1a"], C)], rows2["hk_b1"], node_k, wait2)
            project("gnn2_nv", [(HT, W2["hv_W1a"], C)], rows2["hv_b1"], node_v)
            project("gnn2_nh", [(HT, W2["no_W1"][:, 4:8, :], C)], rows2["no_b1"], hid_no)
            project("gnn2_nq", [(HT, W2["hq_W1"], C)], rows2["hq_b1"], qh)
            norm_and_turn("gnn2_qnorm", affine=cols2["hq"], source=qh, into=qh, func=ACT.Relu)
            project("gnn2_q", [(HT, W2["hq_W2"], C)], rows2["hq_b2"], qh)
            with Stage(nc, "gnn2_tables") as st:
                v = st.sem("v")
                qb = R0[:, 1024:2048].rearrange("p (h d) -> p h d", h=2)
                block = st.block()

                @block.vector
                def _(dve):
                    chain = Chain(dve, v)
                    chain.link(dve.tensor_scalar(flat(qh), flat(qh), HD2 ** -0.5, None, ALU.mult))
                    for h in range(HALVES):
                        chain.link(dve.tensor_tensor(qb[:, h, :], qh[:, h, :], rows2["hk_b2"], ALU.mult))
                        chain.link(dve.tensor_reduce(extra[:, h, 0:NH2], qb[:, h, :].rearrange("p (a b) -> p a b", a=NH2),
                                                     AX_X, ALU.add))
                    chain.link(dve.tensor_copy(extra[:, :, NH2:NX], bounds[:, :, :]))
                    for a, hi, lo in ((qh, Q_hi, Q_lo), (extra, X_hi, X_lo)):
                        chain.link(dve.tensor_copy(hi[:, :, :], a[:, :, :]))
                        chain.link(dve.tensor_tensor(lo[:, :, :], a[:, :, :], hi[:, :, :].bitcast(F32), ALU.subtract))

            mid = upper_at[0]
            penF, penL = [q2.enter_context(nc.sbuf_tensor(f"pen{k}", [P, TILES], F32)) for k in range(2)]
            sdst = q2.enter_context(nc.sbuf_tensor("sdst", [P, TILES, 2], F32))

            def edge_pass(name, keys, W1b, W2e, gain, offset, table):
                with Stage(nc, name) as st:
                    upper_at[0] = mid
                    overlay = lambda label, at, shape: nc.alloc_sbuf_tensor_at(f"{name}_{label}", shape, F32R,
                                                                              offset=r0_at + at)
                    W_hi, W_lo = overlay("W_hi", 0, [P, C, D]), overlay("W_lo", 8192, [P, C, D])
                    B_hi, B_lo = overlay("B_hi", 16384, [P, D]), overlay("B_lo", 18432, [P, D])
                    ef_hi, ef_lo = overlay("ef_hi", 20480, [P, 2, P]), overlay("ef_lo", 21504, [P, 2, P])
                    r_hi, r_lo = overlay("r_hi", 24576, [P, 2, D]), overlay("r_lo", 28672, [P, 2, D])
                    prod = R0[:, 5632:6144]
                    hn = up((2, D))
                    rT = up((2, D))
                    n_hot = 4 if keys else 2
                    WIDE = D + NH2
                    if keys:
                        qs = up((2, D))
                        hots = up((4, N))
                    else:
                        hots = up((2, N))
                        to_dst = st.sb("to_dst", [P, 2, N], F32R)
                        full = up((2, WIDE))
                        m_hi, m_lo = st.sb("m_hi", [P, 2, WIDE], F32R), st.sb("m_lo", [P, 2, WIDE], F32R)
                    rowt = st.sb("rowt", [P, 2, ROW])
                    pick = st.sb("pick", [P, 2, n_hot * P], F32R)
                    stats, mv = st.sb("stats", [P, 2, 6]), st.sb("mv", [P, 2, 2])
                    rstd, shift = st.sb("rstd", [P, 2]), st.sb("shift", [P, 2])
                    names = ("rows0", "rows1", "hot", "saved", "f1", "ef_hi", "ef_out", "ef_lo", "hidden", "varied", "rooted",
                             "scaled", "normed", "hn_turned", "relued", "r_hi", "r_lo", "f4", "q_out", "used", "m_hi", "m_lo",
                             "scattered", "q_done", "v", "stat", "split")
                    s = {n: st.sem(n) for n in names}
                    block = st.block()

                    @block.sync
                    def _(sp):
                        def body(k, j):
                            guard(sp, s["f1"], k, 2)
                            guard(sp, s["saved"], k, 2)
                            sp.dma_start(rowt[:, j, :], scratch[bass.ds(k * P, P), :]).then_inc(s[f"rows{j}"], 16)

                        over_tiles(sp, body)

                    @block.tensor
                    def _(pe):
                        def turn_hot(k, j):
                            pe.wait_ge(s["hot"], k + 1)
                            guard(pe, s["ef_out"], k, 1)
                            guard(pe, s["ef_lo"], k, 1)
                            pe.wait_ge(s[f"rows{j}"], 8 * (k - j) + 16)
                            pe.transpose(PS[:, 5, 0:P], rowt[:, j, 0:EF], ident[:, :])
                            for q in range(n_hot):
                                last = pe.transpose(PS[:, 4, q * P:(q + 1) * P],
                                                    hots[:, 2 * (q // 2) + j, (q % 2) * P:(q % 2 + 1) * P], ident[:, :])
                            last.then_inc(s["f1"], 1)

                        def hidden(k, j):
                            pe.wait_ge(s["ef_out"], k + 1)
                            guard(pe, s["normed"], k, 1)
                            for h in range(HALVES):
                                pe.matmul(PS[:, 0, :], pick[:, j, h * P:(h + 1) * P], A_hi[:, h, :], start=(h == 0), stop=False)
                                pe.matmul(PS[:, 0, :], pick[:, j, h * P:(h + 1) * P], A_lo[:, h, :], start=False, stop=False)
                            pe.matmul(PS[:, 0, :], ef_hi[:, j, :], B_hi[:, :], start=False, stop=False)
                            pe.matmul(PS[:, 0, :], ef_hi[:, j, :], B_lo[:, :], start=False, stop=False)
                            pe.wait_ge(s["ef_lo"], k + 1)
                            pe.matmul(PS[:, 0, :], ef_lo[:, j, :], B_hi[:, :], start=False, stop=True).then_inc(s["hidden"], 1)
                            if keys:
                                guard(pe, s["q_out"], k, 1)
                                for h in range(HALVES):
                                    a = pick[:, j, (2 + h) * P:(3 + h) * P]
                                    pe.matmul(PS[:, 1, :], a, Q_hi[:, h, :], start=(h == 0), stop=False)
                                    pe.matmul(PS[:, 1, :], a, Q_lo[:, h, :], start=False, stop=(h == 1))
                                guard(pe, s["used"], k, 2)
                                for h in range(HALVES):
                                    a = pick[:, j, (2 + h) * P:(3 + h) * P]
                                    pe.matmul(PS[:, 6 + j, 0:NX], a, X_hi[:, h, :], start=(h == 0), stop=False)
                                    last = pe.matmul(PS[:, 6 + j, 0:NX], a, X_lo[:, h, :], start=False, stop=(h == 1))
                                last.then_inc(s["q_done"], 1)

                        def outer(k, j):
                            pe.wait_ge(s["r_hi"], k + 1)
                            guard(pe, s["used"], k, 1)
                            for c in range(C):
                                a = r_hi[:, j, c * P:(c + 1) * P]
                                pe.matmul(PS[:, 3, :], a, W_hi[:, c, :], start=(c == 0), stop=False)
                                pe.matmul(PS[:, 3, :], a, W_lo[:, c, :], start=False, stop=False)
                            pe.wait_ge(s["r_lo"], k + 1)
                            for c in range(C):
                                last = pe.matmul(PS[:, 3, :], r_lo[:, j, c * P:(c + 1) * P], W_hi[:, c, :], start=False,
                                                 stop=(c == C - 1))
                            last.then_inc(s["f4"], 1)

                        def turn_normed(k, j):
                            pe.wait_ge(s["normed"], k + 1)
                            guard(pe, s["relued"], k, 1)
                            for c in range(C):
                                last = pe.transpose(PS[:, 2, c * P:(c + 1) * P], hn[:, j, c * P:(c + 1) * P], ident[:, :])
                            last.then_inc(s["hn_turned"], 1)

                        def scatter(k, j):
                            pe.wait_ge(s["m_lo"], k + 1)
                            first, end = isinstance(k, int) and k == 0, isinstance(k, int) and k == TILES - 1
                            for h in range(HALVES):
                                a = to_dst[:, j, h * P:(h + 1) * P]
                                for part in (m_hi, m_lo):
                                    one, two = first and part is m_hi, end and part is m_lo
                                    if h == 0:
                                        pe.matmul(PS[0:NH2, 1, 0:N], part[:, j, D:WIDE], to_dst[:, j, :], start=one,
                                                  stop=two, skip_group_check=True)
                                    last = pe.matmul(PS[:, 6 + h, :], a, part[:, j, 0:D], start=one, stop=two,
                                                     skip_group_check=True)
                            last.then_inc(s["scattered"], 1)

                        pe.wait_ge(s["split"], 1)
                        turn_hot(0, 0)

                        def body(k, j):
                            fixed = isinstance(k, int)
                            hidden(k, j)
                            if not (fixed and k == TILES - 1):
                                turn_hot(k + 1, 1 - j)
                            if not (fixed and k == 0):
                                outer(k - 1, 1 - j)
                            if not keys and not (fixed and k < 2):
                                scatter(k - 2, j)
                            turn_normed(k, j)

                        over_tiles(pe, body, head=4)
                        outer(TILES - 1, 1)
                        if not keys:
                            scatter(TILES - 2, 0)
                            scatter(TILES - 1, 1)

                    @block.scalar
                    def _(act):
                        def leave(k, j):
                            act.wait_ge(s["f1"], k + 1)
                            guard(act, s["hidden"], k, 2)
                            act.activation(ef_hi[:, j, :], PS[:, 5, 0:P], ACT.Copy).then_inc(s["ef_hi"], 1)
                            if keys:
                                guard(act, s["q_done"], k, 2)
                            act.activation(pick[:, j, :], PS[:, 4, 0:n_hot * P], ACT.Copy).then_inc(s["ef_out"], 1)

                        def weigh(k, j):
                            act.wait_ge(s["used"], k + 1)
                            guard(act, s["scattered"], k, 2)
                            act.activation(m_hi[:, j, :], full[:, j, :], ACT.Copy).then_inc(s["m_hi"], 1)

                        leave(0, 0)

                        def body(k, j):
                            fixed = isinstance(k, int)
                            act.wait_ge(s["varied"], k + 1)
                            act.activation(rstd[:, j:j + 1], rstd[:, j:j + 1], ACT.Sqrt).then_inc(s["rooted"], 1)
                            if not (fixed and k == TILES - 1):
                                leave(k + 1, 1 - j)
                            act.wait_ge(s["scaled"], k + 1)
                            guard(act, s["hn_turned"], k, 2)
                            act.activation(hn[:, j, :], PS[:, 0, :], ACT.Identity, bias=shift[:, j:j + 1],
                                           scale=rstd[:, j:j + 1]).then_inc(s["normed"], 1)
                            if keys:
                                act.wait_ge(s["q_done"], k + 1)
                                guard(act, s["used"], k, 2)
                                act.activation(qs[:, j, :], PS[:, 1, :], ACT.Copy).then_inc(s["q_out"], 1)
                            act.wait_ge(s["hn_turned"], k + 1)
                            guard(act, s["r_lo"], k, 2)
                            for c in range(C):
                                last = act.activation(rT[:, j, c * P:(c + 1) * P], PS[:, 2, c * P:(c + 1) * P], ACT.Relu,
                                                      bias=offset[:, c:c + 1], scale=gain[:, c:c + 1])
                            last.then_inc(s["relued"], 1)
                            act.wait_ge(s["relued"], k + 1)
                            guard(act, s["f4"], k, 2)
                            act.activation(r_hi[:, j, :], rT[:, j, :], ACT.Copy).then_inc(s["r_hi"], 1)
                            if not keys and not (fixed and k == 0):
                                weigh(k - 1, 1 - j)

                        over_tiles(act, body, head=4)
                        if not keys:
                            weigh(TILES - 1, 1)

                    @block.vector
                    def _(dve):
                        chain = Chain(dve, s["v"])
                        for a, hi, lo in ((flat(W2e), flat(W_hi[:, :, :]), flat(W_lo[:, :, :])), (W1b, B_hi[:, :], B_lo[:, :]),
                                          (flat(table), flat(A_hi[:, :, :]), flat(A_lo[:, :, :]))):
                            chain.link(dve.tensor_copy(hi, a))
                            last = dve.tensor_tensor(lo, a, hi.bitcast(F32), ALU.subtract)
                        last.then_inc(s["split"], 1)
                        steps = chain.n

                        def hot(k, j):
                            dve.wait_ge(s[f"rows{j}"], 8 * (k - j) + 16)
                            guard(dve, s["f1"], k, 2)
                            if keys:
                                dve.tensor_scalar(hots[:, 2 + j, :], iota[:, :], rowt[:, j, EF + 1:ROW], None, ALU.is_equal)
                            dve.tensor_scalar(hots[:, j, :], iota[:, :], rowt[:, j, EF:EF + 1], None,
                                              ALU.is_equal).then_inc(s["hot"], 1)

                        def save(k, j):
                            dve.tensor_copy(sdst[:, bass.ds(k, 1), :].rearrange("p a b -> p (a b)"),
                                            rowt[:, j, EF:ROW]).then_inc(s["saved"], 1)

                        def low_ef(k, j):
                            dve.wait_ge(s["ef_hi"], k + 1)
                            guard(dve, s["hidden"], k, 2)
                            dve.tensor_tensor(ef_lo[:, j, :], PS[:, 5, 0:P], ef_hi[:, j, :].bitcast(F32),
                                              ALU.subtract).then_inc(s["ef_lo"], 1)

                        def low_r(k, j):
                            dve.wait_ge(s["r_hi"], k + 1)
                            guard(dve, s["f4"], k, 2)
                            dve.tensor_tensor(r_lo[:, j, :], rT[:, j, :], r_hi[:, j, :].bitcast(F32),
                                              ALU.subtract).then_inc(s["r_lo"], 1)

                        def low_m(k, j):
                            dve.wait_ge(s["m_hi"], k + 1)
                            guard(dve, s["scattered"], k, 2)
                            dve.tensor_tensor(m_lo[:, j, :], full[:, j, :], m_hi[:, j, :].bitcast(F32),
                                              ALU.subtract).then_inc(s["m_lo"], 1)

                        def use(k, j):
                            dve.wait_ge(s["f4"], k + 1)
                            Lk = L[:, bass.ds(k, 1), :].rearrange("p a b -> p (a b)")
                            if keys:
                                dve.wait_ge(s["q_out"], k + 1)
                                dve.tensor_tensor(prod, PS[:, 3, :], qs[:, j, :], ALU.mult).then_inc(s["v"], 1)
                                dve.wait_ge(s["v"], 2 * k + steps + 1)
                                dve.tensor_reduce(Lk, prod.rearrange("p (a b) -> p a b", a=NH2), AX_X,
                                                  ALU.add).then_inc(s["v"], 1)
                                dve.tensor_scalar(penF[:, bass.ds(k, 1)], PS[:, 6 + j, NH2:NH2 + 1],
                                                  small["place"][:, bass.ds(k, 1)], FAR, ALU.is_equal, ALU.mult)
                                dve.tensor_scalar(penL[:, bass.ds(k, 1)], PS[:, 6 + j, NH2 + 1:NX],
                                                  small["place1"][:, bass.ds(k, 1)], FAR, ALU.is_equal, ALU.mult)
                                dve.wait_ge(s["v"], 2 * k + steps + 2)
                                dve.tensor_tensor(Lk, Lk, PS[:, 6 + j, 0:NH2], ALU.add).then_inc(s["used"], 1)
                            else:
                                guard(dve, s["scattered"], k, 2)
                                dve.wait_ge(s["saved"], k + 1)
                                dve.tensor_scalar(to_dst[:, j, :], iota[:, :], sdst[:, bass.ds(k, 1), 1], None, ALU.is_equal)
                                guard(dve, s["m_lo"], k, 2)
                                dve.tensor_copy(full[:, j, D:WIDE], Lk)
                                dve.tensor_tensor(full[:, j, 0:D].rearrange("p (a b) -> p a b", a=NH2),
                                                  PS[:, 3, :].rearrange("p (a b) -> p a b", a=NH2),
                                                  Lk.unsqueeze(2).broadcast_to([P, NH2, HD2]), ALU.mult).then_inc(s["used"], 1)

                        hot(0, 0)
                        hot(1, 1)
                        save(0, 0)
                        low_ef(0, 0)
                        stat = s["stat"]

                        def body(k, j):
                            fixed = isinstance(k, int)
                            dve.wait_ge(s["hidden"], k + 1)
                            guard(dve, s["normed"], k, 2)
                            dve.bn_stats(stats[:, j, :], PS[:, 0, :]).then_inc(stat, 1)
                            dve.wait_ge(stat, 3 * k + 1)
                            if not (fixed and k == TILES - 1):
                                save(k + 1, 1 - j)
                            dve.bn_aggr(mv[:, j, :], stats[:, j, :]).then_inc(stat, 1)
                            dve.wait_ge(stat, 3 * k + 2)
                            dve.tensor_scalar(rstd[:, j:j + 1], mv[:, j, 1:2], EPS, None, ALU.add).then_inc(s["varied"], 1)
                            if not (fixed and k == 0):
                                low_r(k - 1, 1 - j)
                            dve.wait_ge(s["rooted"], k + 1)
                            dve.reciprocal(rstd[:, j:j + 1], rstd[:, j:j + 1]).then_inc(stat, 1)
                            dve.wait_ge(stat, 3 * k + 3)
                            dve.tensor_scalar(shift[:, j:j + 1], mv[:, j, 0:1], rstd[:, j:j + 1], -1.0, ALU.mult,
                                              ALU.mult).then_inc(s["scaled"], 1)
                            if not (fixed and k == TILES - 1):
                                low_ef(k + 1, 1 - j)
                            if keys and not (fixed and k >= TILES - 2):
                                hot(k + 2, j)
                            if not keys and not (fixed and k < 2):
                                low_m(k - 2, j)
                            if not (fixed and k == 0):
                                use(k - 1, 1 - j)
                            if not keys and not (fixed and k >= TILES - 2):
                                hot(k + 2, j)

                        over_tiles(dve, body, head=4)
                        low_r(TILES - 1, 1)
                        if not keys:
                            low_m(TILES - 2, 0)
                        use(TILES - 1, 1)
                        if not keys:
                            low_m(TILES - 1, 1)

            edge_pass("gnn2_keys", True, W2["hk_W1b"][:, 0, :], W2["hk_W2"], *cols2["hk"], node_k)

            with Stage(nc, "gnn2_pens") as st:
                penT = st.sb("penT", [TILES, 2, P])
                turned, out_, stored = st.sem("turned"), st.sem("out"), st.sem("stored")
                block = st.block()

                @block.tensor
                def _(pe):
                    pe.transpose(PS[0:TILES, 0, 0:P], penF[:, :], ident[:, :])
                    pe.transpose(PS[0:TILES, 0, P:2 * P], penL[:, :], ident[:, :]).then_inc(turned, 1)

                @block.vector
                def _(dve):
                    dve.wait_ge(turned, 1)
                    dve.tensor_copy(flat(penT[:, :, :]), PS[0:TILES, 0, 0:2 * P]).then_inc(out_, 1)

                @block.sync
                def _(sp):
                    sp.wait_ge(out_, 1)
                    sp.dma_start(pens.rearrange("a (t p) -> t a p", p=P), penT[:, :, :]).then_inc(stored, 16)
                    sp.wait_ge(stored, 16)

            with Stage(nc, "gnn2_max") as st:
                CK = 4 * P
                STEPS = E // CK
                F = R0[0:NH2, 0:E]
                pf = st.sb("pf", [NH2, 4, CK])
                back = st.sb("back", [NH2, 2, CK])
                names = ("pen_in0", "pen_in1", "pen_in2", "pen_in3", "turned", "scanned", "scanned_back", "returned", "shifted", "exped")
                s = {n: st.sem(n) for n in names}
                block = st.block()
                order = list(range(STEPS)) + list(reversed(range(STEPS)))

                @block.sync
                def _(sp):
                    for q, chunk in enumerate(order):
                        if q >= 4:
                            if q - 4 < STEPS:
                                sp.wait_ge(s["scanned"], q - 3)
                            else:
                                sp.wait_ge(s["scanned_back"], q - 3 - STEPS)
                        sp.dma_start(pf[:, q % 4, :], pens[int(q >= STEPS):int(q >= STEPS) + 1, chunk * CK:(chunk + 1) * CK]
                                     .broadcast_to([NH2, CK])).then_inc(s[f"pen_in{q % 4}"], 16)

                @block.tensor
                def _(pe):
                    for q in range(STEPS):
                        if q >= 2:
                            pe.wait_ge(s["scanned"], q - 1)
                        for m in range(4):
                            last = pe.transpose(PS[0:NH2, q % 2, m * P:(m + 1) * P], L[:, 4 * q + m, :], ident[:, :])
                        last.then_inc(s["turned"], 1)
                    for q in range(STEPS):
                        pe.wait_ge(s["scanned_back"], q + 1)
                        if q >= 2:
                            pe.wait_ge(s["shifted"], q - 1)
                        for m in range(4):
                            last = pe.transpose(PS[:, 2 + q % 2, m * NH2:(m + 1) * NH2], back[:, q % 2, m * P:(m + 1) * P],
                                                ident[0:NH2, 0:NH2])
                        last.then_inc(s["returned"], 1)

                @block.vector
                def _(dve):
                    for q in range(STEPS):
                        dve.wait_ge(s["turned"], q + 1)
                        dve.wait_ge(s[f"pen_in{q % 4}"], 16 * (q // 4) + 16)
                        if q:
                            dve.wait_ge(s["scanned"], q)
                        dve.tensor_tensor_scan(F[:, q * CK:(q + 1) * CK], pf[:, q % 4, :], PS[0:NH2, q % 2, :],
                                               0.0 if q == 0 else F[:, q * CK - 1:q * CK], ALU.add,
                                               ALU.max).then_inc(s["scanned"], 1)
                    dve.wait_ge(s["scanned"], STEPS)

                    def shift(q):
                        chunk = STEPS - 1 - q
                        dve.wait_ge(s["returned"], q + 1)
                        a = flat(L[:, 4 * chunk:4 * chunk + 4, :])
                        dve.tensor_tensor(a, a, PS[:, 2 + q % 2, 0:4 * NH2], ALU.subtract).then_inc(s["shifted"], 1)

                    for q in range(STEPS):
                        chunk = STEPS - 1 - q
                        dve.wait_ge(s[f"pen_in{(STEPS + q) % 4}"], 16 * ((STEPS + q) // 4) + 16)
                        if q >= 2:
                            dve.wait_ge(s["returned"], q - 1)
                        if q:
                            dve.wait_ge(s["scanned_back"], q)
                        dve.tensor_tensor_scan(back[:, q % 2, ::-1], pf[:, (STEPS + q) % 4, ::-1],
                                               F[:, chunk * CK:(chunk + 1) * CK][:, ::-1],
                                               0.0 if q == 0 else back[:, 1 - q % 2, 0:1], ALU.add,
                                               ALU.max).then_inc(s["scanned_back"], 1)
                        if q:
                            shift(q - 1)
                    shift(STEPS - 1)

                @block.scalar
                def _(act):
                    act.wait_ge(s["shifted"], STEPS)
                    act.activation(flat(L[:, :, :]), flat(L[:, :, :]), ACT.Exp)

            edge_pass("gnn2_values", False, W2["hv_W1b"][:, 0, :], W2["hv_W2"], *cols2["hv"], node_v)
            mixed = R0[:, 0:1024].rearrange("p (h d) -> p h d", h=2)
            mixedT = R0[:, 1024:2048].rearrange("p (c n) -> p c n", c=C)
            with Stage(nc, "gnn2_mean") as st:
                den, inv = st.sb("den", [P, HALVES, NH2]), st.sb("inv", [P, HALVES, NH2])
                denT = st.sb("denT", [NH2, N])
                v, ready, turned, den_out, den_turned = (st.sem(n) for n in ("v", "ready", "turned", "den_out", "den_turned"))
                block = st.block()
                spare = R0[:, 2048:3072].rearrange("p (h d) -> p h d", h=2)
                heads = lambda a: a.rearrange("p (a b) -> p a b", a=NH2)
                wide = lambda a: a.unsqueeze(2).broadcast_to([P, NH2, HD2])

                @block.vector
                def _(dve):
                    chain = Chain(dve, v)
                    dve.tensor_copy(denT[:, :], PS[0:NH2, 1, 0:N]).then_inc(den_out, 1)
                    dve.wait_ge(den_turned, 1)
                    chain.link(dve.tensor_copy(flat(den[:, :, :]), PS[:, 0, 0:2 * NH2]))
                    chain.link(dve.tensor_scalar(flat(inv[:, :, :]), flat(den[:, :, :]), 1e-30, None, ALU.max))
                    chain.link(dve.reciprocal(flat(inv[:, :, :]), flat(inv[:, :, :])))
                    chain.link(dve.tensor_tensor(flat(den[:, :, :]), flat(den[:, :, :]), flat(inv[:, :, :]), ALU.mult))
                    for h in range(HALVES):
                        chain.link(dve.tensor_tensor(heads(mixed[:, h, :]), heads(PS[:, 6 + h, :]), wide(inv[:, h, :]), ALU.mult))
                        chain.link(dve.tensor_tensor(heads(spare[:, h, :]), heads(rows2["hv_b2"]), wide(den[:, h, :]), ALU.mult))
                        dve.tensor_tensor(mixed[:, h, :], mixed[:, h, :], spare[:, h, :], ALU.add).then_inc(ready, 1)

                @block.tensor
                def _(pe):
                    pe.wait_ge(den_out, 1)
                    for h in range(HALVES):
                        last = pe.transpose(PS[:, 0, h * NH2:(h + 1) * NH2], denT[:, h * P:(h + 1) * P],
                                            ident[0:NH2, 0:NH2])
                    last.then_inc(den_turned, 1)
                    for h in range(HALVES):
                        pe.wait_ge(ready, h + 1)
                        for c in range(C):
                            last = pe.transpose(PS[:, 2 + h, c * P:(c + 1) * P], mixed[:, h, c * P:(c + 1) * P], ident[:, :])
                        last.then_inc(turned, 1)

                @block.scalar
                def _(act):
                    for h in range(HALVES):
                        act.wait_ge(turned, h + 1)
                        act.activation(mixedT[:, :, h * P:(h + 1) * P], PS[:, 2 + h, :].rearrange("p (c n) -> p c n", c=C),
                                       ACT.Copy)

            with Stage(nc, "gnn2_no") as st:
                done, v = st.sem("done"), st.sem("v")
                block = st.block()

                @block.tensor
                def _(pe):
                    for h in range(HALVES):
                        for c in range(C):
                            last = pe.matmul(PS[:, h, :], mixedT[:, c, h * P:(h + 1) * P], W2["no_W1"][:, c, :],
                                             start=(c == 0), stop=(c == C - 1))
                        last.then_inc(done, 1)

                @block.vector
                def _(dve):
                    chain = Chain(dve, v)
                    for h in range(HALVES):
                        chain.link(dve.tensor_tensor(X[:, h, :], X[:, h, :], XN[:, h, :], ALU.add))
                        dve.wait_ge(done, h + 1)
                        chain.link(dve.tensor_tensor(hid_no[:, h, :], hid_no[:, h, :], PS[:, h, :], ALU.add))

            norm_and_turn("gnn2_nonorm", affine=cols2["no"], source=hid_no, into=hid_no, func=ACT.Relu)
            project("gnn2_last", [(HT, W2["no_W2"], C)], rows2["no_b2"], mixed)
            with Stage(nc, "gnn2_add") as st:
                block = st.block()

                @block.vector
                def _(dve):
                    dve.tensor_tensor(flat(X[:, :, :]), flat(X[:, :, :]), flat(mixed), ALU.add)
            q2.close()
            weights.close()
        NE2, F2 = 8, 32
        if LAST >= 6:
            weights = layer("ffn2")
            norm_and_turn("ffn2_norm")
            route("ffn2_route", NE2, small["ffn2_Wg"], bias=small["ffn2_bg"])
            nC = NE2 * F2 // P
            mix("ffn2_mix", [(P, small["expand2"][:, k * P:(k + 1) * P], None) for k in range(nC)] + [(F2, None, 0.5)],
                r0(0, (3, N)), ACT.Relu, lambda c, k, u: small["ffn2_W1"][:, c, k * P:k * P + u], small["ffn2_b1"],
                lambda k, u: small["ffn2_W2"][0:u, k, :], small["ffn2_bs2"], 0.5, n_exp=NE2, b2=small["ffn2_b2"])
            weights.close()

        NE3, F3, UN = 8, 2048, 512
        Q3 = F3 // UN
        unit = [(r0(4096 * q, (C, UN)), r0(4096 * q + 2048, (UN // P, D))) for q in range(Q3)]

        def load_unit(sp, e, q):
            W1d, W2d = t["L3_ffn_W1"], t["L3_ffn_W2"]
            return ((unit[q][0], W1d[bass.ds(e, 1), :, q * UN:(q + 1) * UN].rearrange("e (c p) n -> p (e c) n", p=P)),
                    (unit[q][1], W2d[bass.ds(e, 1), q * UN:(q + 1) * UN, :].rearrange("e (c p) n -> p (e c) n", p=P)))

        if LAST >= 7:
            weights = layer("gnn3")
            Wi, Wj = r1(0, (C, D)), r1(2048, (C, D))
            with Stage(nc, "gnn3_load") as st:
                block = st.block()

                @block.sync
                def _(sp):
                    for w, name in ((Wi, "gnn3_Wi"), (Wj, "gnn3_Wj")):
                        sp.dma_start(w, t[name].rearrange("(c p) n -> p c n", p=P)).then_inc(w_gnn3, 16)
                    for q in range(Q3):
                        for b, (w, a) in enumerate(load_unit(sp, 0, q)):
                            sp.dma_start(w, a).then_inc(unit_in[2 * q + b], 16)

            norm_and_turn("gnn3_norm")
            nodes = R1[:, 4096:6144].rearrange("p (a h d) -> p a h d", a=2, h=2)
            project("gnn3_i", [(HT, Wi, C)], small["gnn3_b"], nodes[:, 0], [(w_gnn3, 32)])
            project("gnn3_j", [(HT, Wj, C)], small["gnn3_zero"], nodes[:, 1])
            q3 = ExitStack()
            T_hi, T_lo = (q3.enter_context(nc.sbuf_tensor(n, [P, 4, D], F32R)) for n in ("T_hi", "T_lo"))
            split("gnn3_split", [(R1[:, 4096:6144], T_hi[:, :, :].rearrange("p a b -> p (a b)"),
                                  T_lo[:, :, :].rearrange("p a b -> p (a b)"))])
            with Stage(nc, "gnn3_edges") as st:
                hots = R1[:, 6144:7168].rearrange("p (a n) -> p a n", a=4)
                pick = st.sb("pick", [P, 2, 4 * P], F32R)
                m = R1[:, 8192:9216].rearrange("p (a n) -> p a n", a=2)
                names = ("hot", "f1", "f1_out", "picked", "relued", "summed", "v")
                s = {n: st.sem(n) for n in names}
                block = st.block()

                @block.tensor
                def _(pe):
                    def front(k, j):
                        pe.wait_ge(s["hot"], k + 1)
                        guard(pe, s["f1_out"], k, 1)
                        for q in range(4):
                            last = pe.transpose(PS[:, 4, q * P:(q + 1) * P],
                                                hots[:, 2 * (q // 2) + j, (q % 2) * P:(q % 2 + 1) * P], ident[:, :])
                        last.then_inc(s["f1"], 1)

                    def gather(k, j):
                        pe.wait_ge(s["f1_out"], k + 1)
                        guard(pe, s["relued"], k, 2)
                        for q in range(4):
                            pe.matmul(PS[:, 2 + j, :], pick[:, j, q * P:(q + 1) * P], T_hi[:, q, :], start=(q == 0), stop=False)
                            last = pe.matmul(PS[:, 2 + j, :], pick[:, j, q * P:(q + 1) * P], T_lo[:, q, :], start=False,
                                             stop=(q == 3))
                        last.then_inc(s["picked"], 1)

                    def back(k, j):
                        pe.wait_ge(s["relued"], k + 1)
                        for h in range(HALVES):
                            last = pe.matmul(PS[:, 6 + h, :], hots[:, j, h * P:(h + 1) * P], m[:, j, :],
                                             start=isinstance(k, int) and k == 0,
                                             stop=isinstance(k, int) and k == TILES - 1, skip_group_check=True)
                        last.then_inc(s["summed"], 1)

                    def body(k, j):
                        if not (isinstance(k, int) and k == TILES - 1):
                            front(k + 1, 1 - j)
                        back(k, j)
                        if not (isinstance(k, int) and k == TILES - 1):
                            gather(k + 1, 1 - j)

                    front(0, 0)
                    gather(0, 0)
                    over_tiles(pe, body)

                @block.scalar
                def _(act):
                    def leave(k, j):
                        act.wait_ge(s["f1"], k + 1)
                        guard(act, s["picked"], k, 2)
                        act.activation(pick[:, j, :], PS[:, 4, :], ACT.Copy).then_inc(s["f1_out"], 1)

                    def body(k, j):
                        if not (isinstance(k, int) and k == TILES - 1):
                            leave(k + 1, 1 - j)
                        act.wait_ge(s["picked"], k + 1)
                        guard(act, s["summed"], k, 2)
                        act.activation(m[:, j, :], PS[:, 2 + j, :], ACT.Relu).then_inc(s["relued"], 1)

                    leave(0, 0)
                    over_tiles(act, body)

                @block.vector
                def _(dve):
                    def hot(k, j):
                        guard(dve, s["summed"], k, 2)
                        dve.tensor_scalar(hots[:, j, :], iota[:, :], src_col[:, bass.ds(k, 1)], None, ALU.is_equal)
                        dve.tensor_scalar(hots[:, 2 + j, :], iota[:, :], dst_col[:, bass.ds(k, 1)], None,
                                          ALU.is_equal).then_inc(s["hot"], 1)

                    over_tiles(dve, hot)
                    chain = Chain(dve, s["v"])
                    dve.wait_ge(s["summed"], TILES)
                    for h in range(HALVES):
                        chain.link(dve.tensor_tensor(X[:, h, :], X[:, h, :], PS[:, 6 + h, :], ALU.add))
            q3.close()
            weights.close()

        if LAST >= 8:
            weights = layer("ffn3")
            norm_and_turn("ffn3_norm", passes=2, affine=(small["ffn3_ln"][:, 0:C], small["ffn3_ln"][:, C:2 * C]))
            route("ffn3_route", NE3, small["ffn3_wr"], bias=small["ffn3_br"])
            with Stage(nc, "ffn3_experts") as st:
                sel = R1[0:NE3, 0:NE3 * P].rearrange("p (e n) -> p e n", e=NE3)
                spread_gates = R1[:, 1024:3072].rearrange("p (e n) -> p e n", e=NE3)
                FU = UN // P
                hid = R1[:, 3072:3072 + 2 * FU * N].rearrange("p (j f n) -> p j f n", j=2, f=FU)
                names = ("ins", "spread_", "spread_out", "h_done", "h_out", "gated", "y_done", "all_done", "v")
                s = {n: st.sem(n) for n in names}
                b1c = small["ffn3_b1"]
                block = st.block()

                @block.sync
                def _(sp):
                    sp.dma_start(sel, t["select8"]).then_inc(s["ins"], 16)
                    with sp.Fori(1, NE3) as e:
                        for q in range(Q3):
                            for b, (w, a) in enumerate(load_unit(sp, e, q)):
                                sp.wait_ge(s["y_done"] if b else s["h_done"], 4 * e + (q - 3))
                                sp.dma_start(w, a).then_inc(unit_in[2 * q + b], 16)

                @block.tensor
                def _(pe):
                    pe.wait_ge(s["ins"], 16)
                    for e in range(NE3):
                        last = pe.matmul(PS[:, e // 2, (e % 2) * N:(e % 2 + 1) * N], sel[:, e, :], gatesT[0:NE3, :],
                                         start=True, stop=True, skip_group_check=True)
                    last.then_inc(s["spread_"], 1)
                    pe.wait_ge(s["spread_out"], 1)

                    def hidden(e, q):
                        pe.wait_ge(unit_in[2 * q], 16 * e + 16)
                        if not (isinstance(e, int) and e == 0 and q < 2):
                            pe.wait_ge(s["h_out"], Q3 * e + (q - 1))
                        for f in range(FU):
                            for c in range(C):
                                last = pe.matmul(PS[:, 2 * (q % 2) + f // 2, (f % 2) * N:(f % 2 + 1) * N],
                                                 unit[q][0][:, c, f * P:(f + 1) * P], HT[:, c, :], start=(c == 0),
                                                 stop=(c == C - 1), skip_group_check=True)
                        last.then_inc(s["h_done"], 1)

                    def outer(e, q):
                        pe.wait_ge(unit_in[2 * q + 1], 16 * e + 16)
                        pe.wait_ge(s["gated"], Q3 * e + (q + 1))
                        first = isinstance(e, int) and e == 0 and q == 0
                        for h in range(HALVES):
                            for f in range(FU):
                                last = pe.matmul(PS[:, 6 + h, :], hid[:, q % 2, f, h * P:(h + 1) * P], unit[q][1][:, f, :],
                                                 start=first and f == 0, stop=False, skip_group_check=True)
                        last.then_inc(s["y_done"], 1)

                    def expert(e):
                        for q in range(Q3):
                            if q < Q3 - 1:
                                hidden(e, q + 1)
                            elif not (isinstance(e, int) and e == NE3 - 1):
                                hidden(e + 1, 0)
                            outer(e, q)

                    hidden(0, 0)
                    expert(0)
                    with pe.Fori(1, NE3 - 1) as e:
                        expert(e)
                    expert(NE3 - 1)
                    for h in range(HALVES):
                        last = pe.matmul(PS[:, 6 + h, :], gatesT[0:NE3, h * P:(h + 1) * P], small["ffn3_b2"][:, :],
                                         start=False, stop=True, skip_group_check=True)
                    last.then_inc(s["all_done"], 1)

                @block.scalar
                def _(act):
                    def expert(e):
                        for q in range(Q3):
                            act.wait_ge(s["h_done"], Q3 * e + (q + 1))
                            if not (isinstance(e, int) and e == 0 and q < 2):
                                act.wait_ge(s["y_done"], Q3 * e + (q - 1))
                            for f in range(FU):
                                last = act.activation(hid[:, q % 2, f, :],
                                                      PS[:, 2 * (q % 2) + f // 2, (f % 2) * N:(f % 2 + 1) * N], ACT.Gelu,
                                                      bias=b1c[:, bass.ds(e, 1), q * FU + f])
                            last.then_inc(s["h_out"], 1)

                    expert(0)
                    with act.Fori(1, NE3) as e:
                        expert(e)

                @block.vector
                def _(dve):
                    chain = Chain(dve, s["v"])
                    for h in range(HALVES):
                        chain.link(dve.tensor_tensor(X[:, h, :], X[:, h, :], XN[:, h, :], ALU.add))
                    dve.wait_ge(s["spread_"], 1)
                    for b in range(4):
                        last = dve.tensor_copy(flat(spread_gates[:, 2 * b:2 * b + 2, :]), PS[:, b, :])
                    last.then_inc(s["spread_out"], 1)
                    dve.wait_ge(s["spread_out"], 1)
                    with dve.Fori(0, NE3) as e:
                        for q in range(Q3):
                            dve.wait_ge(s["h_out"], Q3 * e + (q + 1))
                            a = hid[:, q % 2, :, :]
                            dve.tensor_tensor(a, a, spread_gates[:, bass.ds(e, 1), :].broadcast_to([P, FU, N]),
                                              ALU.mult).then_inc(s["gated"], 1)
                    dve.wait_ge(s["all_done"], 1)
                    for h in range(HALVES):
                        chain.link(dve.tensor_tensor(X[:, h, :], X[:, h, :], PS[:, 6 + h, :], ALU.add))
            weights.close()
        with Stage(nc, "result") as st:
            stored = st.sem("stored")
            block = st.block()

            @block.sync
            def _(sp):
                sp.dma_start(out.rearrange("(h p) d -> p h d", p=P), X[:, :, :]).then_inc(stored, 16)
                sp.wait_ge(stored, 16)


def _columns(a):
    return np.ascontiguousarray(np.moveaxis(a.reshape(-1, P, *a.shape[1:]), 0, 1))


def _constants():
    n = np.arange(P)
    return {
        "ident": np.eye(P, dtype=np.float32),
        "iota": np.broadcast_to(np.arange(N, dtype=np.float32), (P, N)).copy(),
        "pair": np.where(n[:, None] // 8 == n[None, :] // 8, 0.0, FAR).astype(np.float32),
    }


def _laid_out(i):
    f = lambda a: np.ascontiguousarray(np.asarray(a))
    o = {k: f(v) for k, v in i.items()}
    arrays = dict(_constants())
    arrays["x"] = o["x"]
    arrays["src"], arrays["dst"] = _columns(o["src"]), _columns(o["dst"])
    arrays["attr16"] = f(np.concatenate([o["edge_attr_16"].T, np.ones((1, E), np.float32)]))
    arrays["We17"] = f(np.concatenate([o["L0_gnn_We"], o["L0_gnn_be"][None]]))
    arrays["qk_bias"] = f(np.stack([_columns(o["L0_gnn_bq"]), _columns(o["L0_gnn_bk"])], 1))
    for k in ("L0_gnn_Wq", "L0_gnn_Wk", "L0_gnn_Wv", "L0_gnn_Wo", "L0_gnn_bv", "L0_gnn_bo"):
        arrays[k] = o[k]
    twice = lambda a, axis: f(np.concatenate([a, a], axis))
    rows = lambda a: f(np.broadcast_to(a, (P, a.shape[-1])))
    chunks = lambda a: f(np.moveaxis(a.reshape(-1, P, a.shape[-1]), 0, 1))
    n = np.arange(2048)
    arrays |= {
        "ffn0_W1": f(np.moveaxis(o["L0_ffn_W1"], 0, 1).reshape(D, -1)), "L0_ffn_W2": f(o["L0_ffn_W2"].reshape(-1, D)),
        "expand0": (n[None] // 32 == np.arange(64)[:, None]).astype(np.float32),
        "L0_ffn_Ws1": o["L0_ffn_Ws1"], "L0_ffn_Ws2": o["L0_ffn_Ws2"],
        "ffn0_ln": f(np.concatenate([_columns(o["L0_ffn_" + k]) for k in ("ln1_g", "ln1_b", "ffln_g", "ffln_b")], 1)),
        "Wr": chunks(o["L0_ffn_Wr"]), "codebookT": f(o["L0_ffn_codebook"].T),
        "ffn0_b1": f(np.concatenate([_columns(o["L0_ffn_b1"].reshape(-1)), _columns(o["L0_ffn_bs1"])], 1)),
        "ffn0_bs2": rows(o["L0_ffn_bs2"]), "ffn0_b2": o["L0_ffn_b2"], "Wf1": chunks(o["L0_ffn_Wf1"]),
        "bf1": o["L0_ffn_bf1"][:, None], "Wf2": o["L0_ffn_Wf2"], "bf2": rows(o["L0_ffn_bf2"]),
    }
    arrays |= {
        "up0": o["L1_gnn_W_up0"], "up1": o["L1_gnn_W_up1"], "mlp1": twice(o["L1_gnn_W_mlp1"], 1), "mlp2": twice(o["L1_gnn_W_mlp2"], 1),
        "mlp3": twice(o["L1_gnn_W_mlp3"], 1), "mlp4": twice(o["L1_gnn_W_mlp4"], 0), "out0": chunks(o["L1_gnn_W_out0"]),
        "out1": chunks(o["L1_gnn_W_out1"]), "attr4": _columns(o["edge_attr_4"]), "attr8": f(o["edge_attr_8"].T),
        "L1_ffn_W1": o["L1_ffn_W1"], "L1_ffn_W2": o["L1_ffn_W2"],
    }
    node = _columns(np.arange(N))
    arrays |= {
        "ffn1_Wg": chunks(o["L1_ffn_Wg"]), "ffn1_b1": f(o["L1_ffn_b1"].reshape(8, 8, P).transpose(2, 0, 1)),
        "ffn1_b2": o["L1_ffn_b2"], "before": (np.arange(N) < node[..., None]).astype(np.float32),
        "select8": np.repeat(np.eye(8, dtype=np.float32)[:, :, None], P, 2),
    }
    g2 = lambda k: o["L2_gnn_" + k]
    place = (np.arange(TILES)[None] * P + np.arange(P)[:, None]).astype(np.float32)
    later = (n[:P, None] < n[None, :P]).astype(np.float32)
    arrays |= {
        "attr128": _columns(o["edge_attr_128"]), "place": place, "place1": place + 1,
        "masks": f(np.stack([later, 1 - later], 1)),
        "gnn2_rows": f(np.broadcast_to(np.stack([g2(k) for k in ("hk_b1", "hv_b1", "hq_b1", "hk_b2", "hv_b2", "hq_b2",
                                                                "no_b1", "no_b2")]), (P, 8, D))),
        "gnn2_cols": f(np.stack([_columns(g2(f"{m}_{k}")) for m in ("hk", "hv", "hq", "no") for k in ("g", "be")], 1)),
        "g2_hk_W1a": f(g2("hk_W1")[:D]), "g2_hk_W1b": f(g2("hk_W1")[D:]), "g2_hv_W1a": f(g2("hv_W1")[:D]),
        "g2_hv_W1b": f(g2("hv_W1")[D:]),
    } | {"g2_" + k: g2(k) for k in ("hq_W1", "hk_W2", "hv_W2", "hq_W2", "no_W1", "no_W2")}
    pad = lambda a: np.concatenate([a, np.zeros((P - a.shape[0], *a.shape[1:]), np.float32)])
    side = lambda a: np.moveaxis(a, 0, 1).reshape(D, -1)
    arrays |= {
        "ffn2_Wg": chunks(o["L2_ffn_Wg"]), "ffn2_bg": rows(o["L2_ffn_bg"]),
        "ffn2_W1": chunks(np.concatenate([side(o["L2_ffn_W1"]), o["L2_ffn_Ws1"]], 1)),
        "ffn2_b1": _columns(np.concatenate([o["L2_ffn_b1"].reshape(-1), pad(o["L2_ffn_bs1"])])),
        "ffn2_W2": chunks(np.concatenate([o["L2_ffn_W2"].reshape(-1, D), pad(o["L2_ffn_Ws2"])])),
        "ffn2_bs2": rows(o["L2_ffn_bs2"]), "ffn2_b2": o["L2_ffn_b2"],
        "expand2": (n[None, :N] // 32 == np.arange(8)[:, None]).astype(np.float32),
        "gnn3_Wi": f(o["L3_gnn_W"][:, :D].T), "gnn3_Wj": f(o["L3_gnn_W"][:, D:].T), "gnn3_b": rows(o["L3_gnn_b"]),
        "gnn3_zero": np.zeros((P, D), np.float32),
        "ffn3_ln": f(np.concatenate([_columns(o["L3_ffn_ln_g"]), _columns(o["L3_ffn_ln_b"])], 1)),
        "ffn3_wr": chunks(o["L3_ffn_w_r"].T), "ffn3_br": rows(o["L3_ffn_b_r"]),
        "ffn3_b1": f(o["L3_ffn_b1"].reshape(8, 16, P).transpose(2, 0, 1)), "ffn3_b2": o["L3_ffn_b2"],
        "L3_ffn_W1": o["L3_ffn_W1"], "L3_ffn_W2": o["L3_ffn_W2"],
    }
    return arrays


def kernel(**inputs):
    import concourse.bacc as _bacc
    from concourse.bass_utils import run_bass_kernel_spmd as _run

    nc = _bacc.Bacc("TRN2", target_bir_lowering=False, num_devices=1)
    arrays = _laid_out(inputs)
    t = {k: nc.dram_tensor(f"in_{k}", a.shape, mybir.dt.from_np(a.dtype), kind="ExternalInput").ap()
         for k, a in arrays.items()}
    out = nc.dram_tensor("out_0", (N, D), F32, kind="ExternalOutput").ap()
    build(nc, t, out)
    r = _run(nc, [{f"in_{k}": a for k, a in arrays.items()}], core_ids=[0])
    return r.results[0]["out_0"]
```

```python
from contextlib import ExitStack

import numpy as np

import concourse.bass as bass
from concourse import mybir

F32 = mybir.dt.float32
F32R = mybir.dt.float32r
I32 = mybir.dt.int32
U32 = mybir.dt.uint32
ALU = mybir.AluOpType
ACT = mybir.ActivationFunctionType
AX_X = mybir.AxisListType.X

P = 128
N = 256
HALVES = N // P
D = 512
C = D // P
E = 8192
TILES = E // P
EPS = 1e-5
FAR = -1.0e30
FIRST_SEM = 200


SMALL_SHAPES = {
    "ffn0": {
        "ffn0_ln": (P, 16), "Wr": (P, 4, 64), "codebookT": (64, 64), "ffn0_b1": (P, 24), "ffn0_bs2": (P, D),
        "ffn0_b2": (64, D), "Wf1": (P, 4, 32), "bf1": (32, 1), "Wf2": (32, D), "bf2": (P, D),
    },
    "gnn1": {
        "up0": (P, P), "up1": (P, P), "mlp1": (16, P), "mlp2": (P, P), "mlp3": (P, P), "mlp4": (P, D),
        "out0": (P, 2, P), "out1": (P, 2, P), "attr4": (P, TILES, 4),
    },
    "ffn1": {"ffn1_Wg": (P, 4, 8), "ffn1_b1": (P, 8, 8), "ffn1_b2": (8, D)},
    "ffn2": {
        "ffn2_Wg": (P, 4, 8), "ffn2_bg": (P, 8), "ffn2_W1": (P, 4, 288), "ffn2_b1": (P, 3), "ffn2_W2": (P, 3, D),
        "ffn2_bs2": (P, D), "ffn2_b2": (8, D), "expand2": (8, N),
    },
    "gnn3": {"gnn3_b": (P, D), "gnn3_zero": (P, D)},
    "ffn3": {"ffn3_ln": (P, 8), "ffn3_wr": (P, 4, 8), "ffn3_br": (P, 8), "ffn3_b1": (P, 8, 16), "ffn3_b2": (8, D)},
    "gnn2": {"gnn2_rows": (P, 8, D), "gnn2_cols": (P, 8, 4), "place": (P, TILES), "place1": (P, TILES)},
}


def flat(ap):
    return ap.rearrange("p a b -> p (a b)")


class Stage:

    def __init__(self, nc, name):
        self.nc, self.name = nc, name

    def __enter__(self):
        self.stack = ExitStack()
        self.blocks = ExitStack()
        self.sems = []
        return self

    def sem(self, name):
        s = self.stack.enter_context(self.nc.semaphore(f"{self.name}_{name}", num=FIRST_SEM + len(self.sems)))
        self.sems.append(s)
        return s

    def sb(self, name, shape, dt=F32):
        return self.stack.enter_context(self.nc.sbuf_tensor(f"{self.name}_{name}", shape, dt))

    def block(self):
        return self.blocks.enter_context(self.nc.Block())

    def __exit__(self, *a):
        if a[0] is not None:
            return False
        self.blocks.close()
        numbers = sorted(s.num for s in self.sems)
        if not numbers:
            self.stack.close()
            return False
        assert numbers == list(range(numbers[0], numbers[-1] + 1))
        self.nc.all_engine_barrier(sems_to_clear=range(numbers[0], numbers[-1] + 1))
        self.stack.close()
        return False


class Chain:

    def __init__(self, eng, sem, base=0):
        self.eng, self.sem, self.base, self.n = eng, sem, base, 0

    def link(self, ins):
        self.n += 1
        ins.then_inc(self.sem, 1)
        self.eng.wait_ge(self.sem, self.base + self.n)


def build(nc, t, out):
    with ExitStack() as ctx:
        def sb(name, shape, dt=F32):
            return ctx.enter_context(nc.sbuf_tensor(name, shape, dt))

        def sem(name):
            return ctx.enter_context(nc.semaphore(name))

        r0_at = (nc.sbuf_base + 31) // 32 * 32
        R0 = sb("R0", [P, 16384])
        PS = ctx.enter_context(nc.psum_tensor("PS", [P, 8, 512], F32))
        X = sb("X", [P, HALVES, D])
        XN = sb("XN", [P, HALVES, D])
        HT = sb("HT", [P, C, N])
        ident = sb("ident", [P, P])
        iota = sb("iota", [P, N])
        ones = sb("ones", [P, P])
        src_col = sb("src_col", [P, TILES])
        dst_col = sb("dst_col", [P, TILES])
        pos_i = sb("pos_i", [P, TILES], I32)
        bounds = sb("bounds", [P, HALVES, 2])
        loaded = sem("loaded")
        r1_at = (nc.sbuf_base + 31) // 32 * 32
        R1 = sb("R1", [P, 76 * 256])

        def r0(a, shape):
            n = int(np.prod(shape))
            v = R0[:, a:a + n]
            return v.rearrange("p (a b) -> p a b", a=shape[0]) if len(shape) == 2 else v

        def r1(a, shape):
            n = int(np.prod(shape))
            v = R1[:, a:a + n]
            return v.rearrange("p (a b) -> p a b", a=shape[0]) if len(shape) == 2 else v

        Wq, Wk, Wv, Wo = (r0(2048 * k, (C, D)) for k in range(4))
        small = {}

        def layer(name):
            stack = ExitStack()
            for key, shape in SMALL_SHAPES[name].items():
                w = stack.enter_context(nc.sbuf_tensor("s_" + key, list(shape), F32))
                small[key] = w[tuple(slice(None) for _ in shape)]
            return stack

        def load_small(sp, name, small_in):
            for key in SMALL_SHAPES[name]:
                sp.dma_start(small[key], t[key]).then_inc(small_in, 16)

        def col(name, a, b):
            return small[name][:, a:b]

        w_gnn0 = sem("w_gnn0")
        w_ffn0 = sem("w_ffn0")
        w_gnn2 = sem("w_gnn2")
        w_gnn3 = sem("w_gnn3")
        moved = sem("moved")
        ring_in = [sem(f"ring_in{k}") for k in range(8)]
        unit_in = [sem(f"unit_in{k}") for k in range(8)]

        with Stage(nc, "load") as st:
            converted = st.sem("converted")
            src_i, dst_i = st.sb("src_i", [P, TILES], I32), st.sb("dst_i", [P, TILES], I32)
            block = st.block()

            @block.sync
            def _(sp):
                for a, b in ((X[:, :, :], t["x"].rearrange("(h p) d -> p h d", p=P)), (ident[:, :], t["ident"]),
                             (iota[:, :], t["iota"]), (src_i[:, :], t["src"]), (dst_i[:, :], t["dst"])):
                    sp.dma_start(a, b).then_inc(loaded, 16)

            @block.vector
            def _(dve):
                dve.memset(ones[:, :], 1.0)
                dve.wait_ge(loaded, 5 * 16)
                dve.tensor_copy(src_col[:, :], src_i[:, :])
                dve.tensor_copy(dst_col[:, :], dst_i[:, :]).then_inc(converted, 1)

        def norm_and_turn(name, passes=1, affine=None, turned=True, source=X, columns=None, into=XN,
                          func=ACT.Identity, pool_program=None, loads=None, large=None):
            with Stage(nc, name) as st:
                stats = st.sb("stats", [P, HALVES, 6])
                moments = st.sb("moments", [P, HALVES, 2])
                spread = st.sb("spread", [P, HALVES])
                Y = st.sb("Y", [P, HALVES, D]) if passes == 2 else None
                varied, rooted, scaled = st.sem("varied"), st.sem("rooted"), st.sem("scaled")
                dve_chain, turned_half, shifted = st.sem("dve_chain"), st.sem("turned_half"), st.sem("shifted")
                small_in = st.sem("small_in")
                final = into if passes == 1 else Y
                block = st.block()

                if loads:
                    @block.sync
                    def _(sp):
                        load_small(sp, loads, small_in)
                        if large:
                            large(sp)
                        sp.wait_ge(small_in, 16 * len(SMALL_SHAPES[loads]))

                if pool_program:
                    block.gpsimd(pool_program)

                @block.vector
                def _(dve):
                    chain = Chain(dve, dve_chain)
                    for k in range(passes):
                        a, b = (source, into) if k == 0 else (into, Y)
                        for h in range(HALVES):
                            chain.link(dve.bn_stats(stats[:, h, :], a[:, h, :]))
                            chain.link(dve.bn_aggr(moments[:, h, :], stats[:, h, :]))
                        dve.tensor_scalar(spread[:, :], moments[:, :, 1], EPS, None, ALU.add).then_inc(varied, 1)
                        dve.wait_ge(rooted, k + 1)
                        chain.link(dve.reciprocal(spread[:, :], spread[:, :]))
                        for h in range(HALVES):
                            ins = dve.tensor_scalar(b[:, h, :], a[:, h, :], moments[:, h, 0:1], spread[:, h:h + 1],
                                                    ALU.subtract, ALU.mult)
                            if k == passes - 1:
                                ins.then_inc(scaled, 1)
                            else:
                                chain.link(ins)

                @block.scalar
                def _(act):
                    for k in range(passes):
                        act.wait_ge(varied, k + 1)
                        act.activation(spread[:, :], spread[:, :], ACT.Sqrt).then_inc(rooted, 1)
                    if turned:
                        if loads and affine is not None:
                            act.wait_ge(small_in, 16 * len(SMALL_SHAPES[loads]))
                        for h in range(HALVES):
                            act.wait_ge(turned_half, h + 1)
                            src = PS[:, h, :].rearrange("p (c n) -> p c n", c=C)
                            if affine is None:
                                act.activation(HT[:, :, h * P:(h + 1) * P], src, ACT.Copy)
                            else:
                                for c in range(C):
                                    act.activation(HT[:, c, h * P:(h + 1) * P], src[:, c, :], func,
                                                   bias=affine[1][:, c:c + 1], scale=affine[0][:, c:c + 1])

                @block.tensor
                def _(pe):
                    if turned:
                        for h in range(HALVES):
                            pe.wait_ge(scaled, h + 1)
                            for c in range(C):
                                last = pe.transpose(PS[:, h, c * P:(c + 1) * P],
                                                    columns(final[:, h, :], c) if columns else final[:, h, c * P:(c + 1) * P],
                                                    ident[:, :])
                            last.then_inc(turned_half, 1)

        G, NH0, HD0 = 8, 8, D // 8
        norm_and_turn("gnn0_norm")
        with ExitStack() as keep:
            bias0 = keep.enter_context(nc.sbuf_tensor("bias0", [P, HALVES, G * NH0], F32))
            with Stage(nc, "gnn0_bias") as st:
                attr = R0[0:4 * 17, 8192:8192 + E // 4]
                We = st.sb("We", [4 * 17, 4 * NH0])
                dmod_i = st.sb("dmod_i", [P, TILES], I32)
                dmod = st.sb("dmod", [P, TILES])
                EB = st.sb("EB", [P, TILES, NH0])
                to_slot = st.sb("to_slot", [P, TILES, G])
                spread_bias = nc.alloc_sbuf_tensor_at("g0_spread_bias", [P, TILES, 2, G * NH0], F32R, offset=r0_at + 4 * 8192)
                EB_part = st.sb("EB_part", [P, 2, TILES, NH0], F32R)
                BUFS = 4
                from_src = st.sb("from_src", [P, BUFS, N], F32R)
                low = st.sb("low", [P, HALVES, G * NH0])
                attrs_in, eb_done, eb_out = st.sem("attrs_in"), st.sem("eb_done"), st.sem("eb_out")
                picks, summed, chain_s = st.sem("picks"), st.sem("summed"), st.sem("chain_s")
                block = st.block()

                @block.sync
                def _(sp):
                    sp.dma_start(attr[:, :], t["attr16"]).then_inc(attrs_in, 16)
                    sp.dma_start(We[:, :], t["We17"]).then_inc(attrs_in, 16)
                    sp.dma_start(dmod_i[:, :], t["dst"]).then_inc(attrs_in, 16)
                    for w, name in ((Wq, "L0_gnn_Wq"), (Wk, "L0_gnn_Wk"), (Wv, "L0_gnn_Wv"), (Wo, "L0_gnn_Wo")):
                        sp.dma_start(w, t[name].rearrange("(c p) n -> p c n", p=P)).then_inc(w_gnn0, 16)
                    for a, name in ((r1(0, (C, 2048)), "ffn0_W1"), (r1(8192, (16, D)), "L0_ffn_W2")):
                        sp.dma_start(a, t[name].rearrange("(c p) n -> p c n", p=P)).then_inc(w_ffn0, 16)
                    sp.dma_start(R1[0:64, 16384:16384 + 2048], t["expand0"]).then_inc(w_ffn0, 16)

                @block.tensor
                def _(pe):
                    pe.wait_ge(attrs_in, 48)
                    for k in range(TILES // 4):
                        last = pe.matmul(PS[:, 0, k * 4 * NH0:(k + 1) * 4 * NH0], attr[:, k * P:(k + 1) * P], We[:, :],
                                         start=True, stop=True, skip_group_check=True)
                    last.then_inc(eb_done, 1)
                    pe.wait_ge(eb_out, 1)

                    def tile(k, j, first, end):
                        for h in range(HALVES):
                            last = pe.matmul(PS[:, 1 + h, 0:2 * G * NH0], from_src[:, j, h * P:(h + 1) * P],
                                             spread_bias[:, bass.ds(k, 1), :, :].rearrange("p a b c -> p (a b c)"),
                                             start=first, stop=end, skip_group_check=True)
                        last.then_inc(summed, 1)

                    for k in range(BUFS):
                        pe.wait_ge(picks, k + 1)
                        tile(k, k, k == 0, False)
                    with pe.Fori(1, TILES // BUFS) as i:
                        for j in range(BUFS):
                            pe.wait_ge(picks, BUFS * i + j + 1)
                            tile(BUFS * i + j, j, False, False)

                @block.vector
                def _(dve):
                    chain = Chain(dve, chain_s)
                    dve.wait_ge(attrs_in, 48)
                    chain.link(dve.tensor_scalar(dmod_i[:, :], dmod_i[:, :], G - 1, None, ALU.bitwise_and))
                    chain.link(dve.tensor_copy(dmod[:, :], dmod_i[:, :]))
                    chain.link(dve.tensor_tensor(to_slot[:, :, :], dmod[:, :].unsqueeze(2).broadcast_to([P, TILES, G]),
                                      iota[:, 0:G].unsqueeze(1).broadcast_to([P, TILES, G]), ALU.is_equal))
                    dve.wait_ge(eb_done, 1)
                    chain.link(dve.tensor_copy(EB[:, :, :], PS[:, 0, :].rearrange("p (a b) -> p a b", b=NH0)))
                    chain.link(dve.tensor_copy(EB_part[:, 0, :, :], EB[:, :, :]))
                    chain.link(dve.tensor_tensor(EB_part[:, 1, :, :], EB[:, :, :], EB_part[:, 0, :, :].bitcast(F32),
                                                 ALU.subtract))
                    q = TILES // 4
                    for k in range(0, TILES, q):
                        for part in range(2):
                            ins = dve.tensor_tensor(
                                spread_bias[:, k:k + q, part, :].rearrange("p t (m h) -> p t m h", m=G),
                                to_slot[:, k:k + q, :].unsqueeze(3).broadcast_to([P, q, G, NH0]),
                                EB_part[:, part, k:k + q, :].bitcast(F32).unsqueeze(2).broadcast_to([P, q, G, NH0]), ALU.mult)
                    ins.then_inc(eb_out, 1)
                    for k in range(BUFS):
                        dve.tensor_scalar(from_src[:, k, :], iota[:, :], src_col[:, k:k + 1], None,
                                          ALU.is_equal).then_inc(picks, 1)
                    with dve.Fori(1, TILES // BUFS) as i:
                        for j in range(BUFS):
                            dve.wait_ge(summed, BUFS * i + j + 1 - BUFS)
                            dve.tensor_scalar(from_src[:, j, :], iota[:, :], src_col[:, bass.ds(BUFS * i + j, 1)], None,
                                              ALU.is_equal).then_inc(picks, 1)
                    dve.wait_ge(summed, TILES)
                    for h in range(HALVES):
                        chain.link(dve.tensor_copy(low[:, h, :], PS[:, 1 + h, G * NH0:2 * G * NH0]))
                        dve.tensor_tensor(bias0[:, h, :], low[:, h, :], PS[:, 1 + h, 0:G * NH0], ALU.add)

            with Stage(nc, "gnn0_attention") as st:
                pair = st.sb("pair", [P, P])
                b4 = st.sb("b4", [P, 4, D])
                b4c = st.sb("b4c", [P, 2, C])
                qT = st.sb("qT", [P, C, N])
                kT = st.sb("kT", [P, C, N])
                V = st.sb("V", [P, HALVES, D])
                S = st.sb("S", [P, NH0, P])
                pT = st.sb("pT", [P, NH0, P])
                top = st.sb("top", [P, NH0])
                total = st.sb("total", [P, NH0])
                A = st.sb("A", [P, D])
                AT = st.sb("AT", [P, C, P])
                names = ("ins", "qk", "qk_out", "vdone", "vout", "scores", "scored", "shifted", "exped", "pturned",
                         "pout", "mixed", "mixed_out", "aturned", "aout", "projected", "chain_v")
                s = {n: st.sem("g0_" + n) for n in names}
                block = st.block()
                bq, bk, bv, bo = (b4[:, k, :] for k in range(4))

                @block.sync
                def _(sp):
                    sp.dma_start(pair[:, :], t["pair"]).then_inc(s["ins"], 16)
                    sp.dma_start(b4c[:, :, :], t["qk_bias"]).then_inc(s["ins"], 16)
                    for k, name in enumerate(("L0_gnn_bv", "L0_gnn_bo")):
                        sp.dma_start(b4[:, 2 + k, :], t[name].unsqueeze(0).broadcast_to([P, D])).then_inc(s["ins"], 16)

                @block.tensor
                def _(pe):
                    pe.wait_ge(w_gnn0, 64)
                    for k, W in enumerate((Wq, Wk)):
                        for m in range(C):
                            for c in range(C):
                                last = pe.matmul(PS[:, 2 * k + m // 2, (m % 2) * N:(m % 2 + 1) * N],
                                                 W[:, c, m * P:(m + 1) * P], HT[:, c, :], start=(c == 0), stop=(c == C - 1),
                                                 skip_group_check=True)
                            last.then_inc(s["qk"], 1)
                    for h in range(HALVES):
                        for c in range(C):
                            last = pe.matmul(PS[:, 4 + h, :], HT[:, c, h * P:(h + 1) * P], Wv[:, c, :],
                                             start=(c == 0), stop=(c == C - 1))
                        last.then_inc(s["vdone"], 1)
                    for h in range(HALVES):
                        pe.wait_ge(s["qk_out"], 2 * C)
                        if h:
                            pe.wait_ge(s["scored"], 2 * h)
                        for a in range(NH0):
                            o = (a % 2) * HD0
                            last = pe.matmul(PS[:, a % 2, (a // 2) * P:(a // 2 + 1) * P],
                                             qT[o:o + HD0, a // 2, h * P:(h + 1) * P],
                                             kT[o:o + HD0, a // 2, h * P:(h + 1) * P], start=True, stop=True,
                                             skip_group_check=True)
                        last.then_inc(s["scores"], 1)
                        pe.wait_ge(s["exped"], h + 1)
                        if h:
                            pe.wait_ge(s["pout"], 2 * h)
                        for a in range(NH0):
                            last = pe.transpose(PS[:, 2 + a // 4, (a % 4) * P:(a % 4 + 1) * P], S[:, a, :], ident[:, :])
                        last.then_inc(s["pturned"], 1)
                        pe.wait_ge(s["pout"], 2 * h + 2)
                        pe.wait_ge(s["vout"], h + 1)
                        for a in range(NH0):
                            last = pe.matmul(PS[:, 6, a * HD0:(a + 1) * HD0], pT[:, a, :],
                                             V[:, h, a * HD0:(a + 1) * HD0], start=True, stop=True,
                                             skip_group_check=True)
                        last.then_inc(s["mixed"], 1)
                        pe.wait_ge(s["mixed_out"], h + 1)
                        for c in range(C):
                            last = pe.transpose(PS[:, 7, c * P:(c + 1) * P], A[:, c * P:(c + 1) * P], ident[:, :])
                        last.then_inc(s["aturned"], 1)
                        pe.wait_ge(s["aout"], h + 1)
                        for c in range(C):
                            last = pe.matmul(PS[:, 4 + h, :], AT[:, c, :], Wo[:, c, :], start=(c == 0), stop=(c == C - 1))
                        last.then_inc(s["projected"], 1)

                @block.scalar
                def _(act):
                    act.wait_ge(s["ins"], 64)
                    for k, dest in enumerate((qT, kT)):
                        for m in range(C):
                            act.wait_ge(s["qk"], (k * C + m // 2 * 2 + 2))
                            act.activation(dest[:, m, :], PS[:, 2 * k + m // 2, (m % 2) * N:(m % 2 + 1) * N],
                                           ACT.Identity, bias=b4c[:, k, m:m + 1]).then_inc(s["qk_out"], 1)
                    for h in range(HALVES):
                        act.wait_ge(s["shifted"], h + 1)
                        act.activation(S[:, :, :], S[:, :, :], ACT.Exp).then_inc(s["exped"], 1)
                        act.wait_ge(s["pturned"], h + 1)
                        for b in range(2):
                            act.activation(pT[:, 4 * b:4 * b + 4, :], PS[:, 2 + b, :].rearrange("p (a b) -> p a b", a=4),
                                           ACT.Copy).then_inc(s["pout"], 1)
                        act.wait_ge(s["aturned"], h + 1)
                        act.activation(AT[:, :, :], PS[:, 7, :].rearrange("p (a b) -> p a b", a=C),
                                       ACT.Copy).then_inc(s["aout"], 1)

                @block.vector
                def _(dve):
                    chain = Chain(dve, s["chain_v"])
                    dve.wait_ge(s["ins"], 64)
                    for h in range(HALVES):
                        dve.wait_ge(s["vdone"], h + 1)
                        dve.tensor_tensor(V[:, h, :], PS[:, 4 + h, :], bv, ALU.add).then_inc(s["vout"], 1)
                    for h in range(HALVES):
                        dve.wait_ge(s["scores"], h + 1)
                        if h:
                            dve.wait_ge(s["pturned"], h)
                        for b in range(2):
                            ins = dve.scalar_tensor_tensor(
                                S[:, b::2, :], PS[:, b, :].rearrange("p (a b) -> p a b", a=4), HD0 ** -0.5,
                                pair[:, :].unsqueeze(1).broadcast_to([P, 4, P]), ALU.mult, ALU.add)
                            ins.then_inc(s["scored"], 1)
                        dve.wait_ge(s["scored"], 2 * h + 2)
                        for a in range(NH0):
                            ins = dve.tensor_tensor(
                                S[:, a, :].rearrange("p (g m) -> p g m", m=G), S[:, a, :].rearrange("p (g m) -> p g m", m=G),
                                bias0[:, h, :].rearrange("p (m h) -> p m h", h=NH0)[:, :, a].unsqueeze(1)
                                .broadcast_to([P, P // G, G]), ALU.add)
                        chain.link(ins)
                        chain.link(dve.tensor_reduce(top[:, :], S[:, :, :], AX_X, ALU.max))
                        dve.tensor_tensor(S[:, :, :], S[:, :, :], top[:, :].unsqueeze(2).broadcast_to([P, NH0, P]),
                                          ALU.subtract).then_inc(s["shifted"], 1)
                        dve.wait_ge(s["exped"], h + 1)
                        chain.link(dve.tensor_reduce(total[:, :], S[:, :, :], AX_X, ALU.add))
                        chain.link(dve.reciprocal(total[:, :], total[:, :]))
                        dve.wait_ge(s["mixed"], h + 1)
                        if h:
                            dve.wait_ge(s["aturned"], h)
                        dve.tensor_tensor(A[:, :].rearrange("p (h d) -> p h d", h=NH0),
                                          PS[:, 6, :].rearrange("p (h d) -> p h d", h=NH0),
                                          total[:, :].unsqueeze(2).broadcast_to([P, NH0, HD0]),
                                          ALU.mult).then_inc(s["mixed_out"], 1)
                        dve.wait_ge(s["projected"], h + 1)
                        chain.link(dve.tensor_tensor(X[:, h, :], X[:, h, :], bo, ALU.add))
                        chain.link(dve.tensor_tensor(X[:, h, :], X[:, h, :], PS[:, 4 + h, :], ALU.add))
        gates = sb("gates", [P, HALVES, 64])
        gatesT = sb("gatesT", [64, N])

        def route(name, n_exp, w, bias=None, codebook=None, scale=1.0):
            with Stage(nc, name) as st:
                rT = st.sb("rT", [64, N])
                logits = st.sb("logits", [P, HALVES, n_exp])
                best = st.sb("best", [P, HALVES, 8])
                at = st.sb("at", [P, HALVES, 8], U32)
                atf = st.sb("atf", [P, HALVES, 8])
                e2 = st.sb("e2", [P, HALVES, 2])
                total = st.sb("total", [P, HALVES])
                r_done, r_out, l_done = st.sem("r_done"), st.sem("r_out"), st.sem("l_done")
                shifted, exped, chosen, turned, v = (st.sem(n) for n in ("shifted", "exped", "chosen", "turned", "v"))
                tout = st.sem("tout")
                block = st.block()

                @block.tensor
                def _(pe):
                    if codebook is not None:
                        for c in range(C):
                            last = pe.matmul(PS[0:64, 0, 0:N], w[:, c, :], HT[:, c, :], start=(c == 0), stop=(c == C - 1))
                        last.then_inc(r_done, 1)
                        pe.wait_ge(r_out, 1)
                    for h in range(HALVES):
                        if codebook is not None:
                            last = pe.matmul(PS[:, 1 + h, 0:n_exp], rT[:, h * P:(h + 1) * P], codebook[:, :],
                                             start=True, stop=True)
                        else:
                            for c in range(C):
                                last = pe.matmul(PS[:, 1 + h, 0:n_exp], HT[:, c, h * P:(h + 1) * P], w[:, c, :],
                                                 start=(c == 0), stop=(c == C - 1))
                        last.then_inc(l_done, 1)
                    pe.wait_ge(chosen, HALVES)
                    for h in range(HALVES):
                        pe.transpose(PS[0:n_exp, 3, h * P:(h + 1) * P], gates[:, h, 0:n_exp],
                                     ident[:, :]).then_inc(turned, 1)

                @block.scalar
                def _(act):
                    if codebook is not None:
                        act.wait_ge(r_done, 1)
                        act.activation(rT[:, :], PS[0:64, 0, 0:N], ACT.Copy).then_inc(r_out, 1)
                    act.wait_ge(shifted, 1)
                    act.activation(e2[:, :, :], e2[:, :, :], ACT.Exp).then_inc(exped, 1)
                    act.wait_ge(turned, HALVES)
                    act.activation(gatesT[0:n_exp, :], PS[0:n_exp, 3, 0:N], ACT.Copy)

                @block.vector
                def _(dve):
                    chain = Chain(dve, v)
                    for h in range(HALVES):
                        dve.wait_ge(l_done, h + 1)
                        if bias is None:
                            chain.link(dve.tensor_scalar(logits[:, h, :], PS[:, 1 + h, 0:n_exp], scale, None, ALU.mult))
                        else:
                            chain.link(dve.tensor_tensor(logits[:, h, :], PS[:, 1 + h, 0:n_exp], bias, ALU.add))
                        chain.link(dve.max(best[:, h, :], logits[:, h, :]))
                        chain.link(dve.max_index(at[:, h, :], best[:, h, :], logits[:, h, :]))
                    chain.link(dve.tensor_copy(atf[:, :, :], at[:, :, :]))
                    dve.tensor_tensor(e2[:, :, :], best[:, :, 0:2], best[:, :, 0:1].broadcast_to([P, HALVES, 2]),
                                      ALU.subtract).then_inc(shifted, 1)
                    dve.wait_ge(exped, 1)
                    chain.link(dve.tensor_reduce(total[:, :], e2[:, :, :], AX_X, ALU.add))
                    chain.link(dve.reciprocal(total[:, :], total[:, :]))
                    chain.link(dve.tensor_tensor(e2[:, :, :], e2[:, :, :], total[:, :].unsqueeze(2).broadcast_to([P, HALVES, 2]),
                                                 ALU.mult))
                    for h in range(HALVES):
                        chain.link(dve.tensor_scalar(gates[:, h, 0:n_exp], iota[:, 0:n_exp], atf[:, h, 0:1], e2[:, h, 0:1],
                                                     ALU.is_equal, ALU.mult))
                        chain.link(dve.tensor_scalar(logits[:, h, :], iota[:, 0:n_exp], atf[:, h, 1:2], e2[:, h, 1:2],
                                                     ALU.is_equal, ALU.mult))
                        dve.tensor_tensor(gates[:, h, 0:n_exp], gates[:, h, 0:n_exp], logits[:, h, :],
                                          ALU.add).then_inc(chosen, 1)

        def mix(name, chunks, hidden, func, w1, b1, w2, out_bias, bias_scale, n_exp=0, b2=None, into_xn=False,
                weights=None):
            with Stage(nc, name) as st:
                h_done, h_out, g_done, ready, y_done, v = (st.sem(n) for n in ("h_done", "h_out", "g_done", "ready", "y_done", "v"))
                block = st.block()
                n = len(chunks)

                @block.tensor
                def _(pe):
                    if weights is not None:
                        pe.wait_ge(*weights)
                    for k, (units, expand, _) in enumerate(chunks):
                        if k >= 2:
                            pe.wait_ge(h_out, k - 1)
                        for c in range(C):
                            last = pe.matmul(PS[0:units, k % 2, 0:N], w1(c, k, units), HT[:, c, :],
                                             start=(c == 0), stop=(c == C - 1))
                        last.then_inc(h_done, 1)
                        if k >= 2:
                            pe.wait_ge(ready, k - 1)
                        if expand is not None:
                            pe.matmul(PS[0:units, 2 + k % 2, 0:N], expand, gatesT[0:n_exp, :],
                                      start=True, stop=True).then_inc(g_done, 1)
                    pe.wait_ge(ready, n)
                    for h in range(HALVES):
                        for k, (units, _, _) in enumerate(chunks):
                            last = pe.matmul(PS[:, 4 + h, :], hidden[0:units, k, h * P:(h + 1) * P], w2(k, units),
                                             start=(k == 0), stop=(k == n - 1 and b2 is None))
                        if b2 is not None:
                            last = pe.matmul(PS[:, 4 + h, :], gatesT[0:n_exp, h * P:(h + 1) * P], b2,
                                             start=False, stop=True)
                        last.then_inc(y_done, 1)

                @block.scalar
                def _(act):
                    for k, (units, _, _) in enumerate(chunks):
                        act.wait_ge(h_done, k + 1)
                        act.activation(hidden[0:units, k, :], PS[0:units, k % 2, 0:N], func,
                                       bias=b1[0:units, k:k + 1]).then_inc(h_out, 1)

                @block.vector
                def _(dve):
                    chain = Chain(dve, v)
                    if into_xn:
                        for h in range(HALVES):
                            chain.link(dve.tensor_tensor(X[:, h, :], X[:, h, :], XN[:, h, :], ALU.add))
                    gated = 0
                    for k, (units, expand, factor) in enumerate(chunks):
                        dve.wait_ge(h_out, k + 1)
                        a = hidden[0:units, k, :]
                        if expand is not None:
                            gated += 1
                            dve.wait_ge(g_done, gated)
                            dve.tensor_tensor(a, a, PS[0:units, 2 + k % 2, 0:N], ALU.mult).then_inc(ready, 1)
                        else:
                            dve.tensor_scalar(a, a, factor, None, ALU.mult).then_inc(ready, 1)
                    for h in range(HALVES):
                        dve.wait_ge(y_done, h + 1)
                        y = XN[:, h, :]
                        chain.link(dve.scalar_tensor_tensor(y, out_bias, bias_scale, PS[:, 4 + h, :], ALU.mult, ALU.add))
                        chain.link(dve.tensor_tensor(X[:, h, :], X[:, h, :], y, ALU.add))

        DFF, DSH, E0 = 32, 1024, 64
        W1_0, W2_0 = r1(0, (C, E0 * DFF)), r1(8192, (E0 * DFF // P, D))
        expand0 = R1[0:64, 16384:16384 + E0 * DFF]
        Ws1_0, Ws2_0 = r0(0, (C, DSH)), r0(4096, (DSH // P, D))
        hidden0 = r0(8192, (24, N))
        weights = layer("ffn0")

        def shared_expert(sp):
            sp.dma_start(Ws1_0, t["L0_ffn_Ws1"].rearrange("(c p) n -> p c n", p=P)).then_inc(w_ffn0, 16)
            sp.dma_start(Ws2_0, t["L0_ffn_Ws2"].rearrange("(c p) n -> p c n", p=P)).then_inc(w_ffn0, 16)

        norm_and_turn("ffn0_norm", passes=2, affine=(col("ffn0_ln", 0, C), col("ffn0_ln", C, 2 * C)), loads="ffn0",
                      large=shared_expert)
        route("ffn0_route", E0, small["Wr"], codebook=small["codebookT"], scale=1.0 / 0.7)
        nE = E0 * DFF // P
        mix("ffn0_mix", [(P, expand0[:, k * P:(k + 1) * P], None) for k in range(nE)] + [(P, None, 0.25)] * (DSH // P),
            hidden0, ACT.Silu,
            lambda c, k, u: W1_0[:, c, k * P:(k + 1) * P] if k < nE else Ws1_0[:, c, (k - nE) * P:(k - nE + 1) * P],
            small["ffn0_b1"], lambda k, u: W2_0[:, k, :] if k < nE else Ws2_0[:, k - nE, :],
            small["ffn0_bs2"], 0.25, n_exp=E0, b2=small["ffn0_b2"], into_xn=True, weights=(w_ffn0, 5 * 16))
        norm_and_turn("ffn0_norm2", affine=(col("ffn0_ln", 2 * C, 3 * C), col("ffn0_ln", 3 * C, 4 * C)), source=XN)
        mix("ffn0_last", [(DFF, None, 1.0)], hidden0, ACT.Silu, lambda c, k, u: small["Wf1"][:, c, :],
            small["bf1"], lambda k, u: small["Wf2"][:, :], small["bf2"], 1.0)
        weights.close()

        def guard(eng, semaphore, k, back):
            if not isinstance(k, int) or k >= back:
                eng.wait_ge(semaphore, k - back + 1)

        def over_tiles(eng, body, head=2):
            for k in range(head):
                body(k, k % 2)
            with eng.Fori(head // 2, TILES // 2 - 1) as i:
                for j in range(2):
                    body(2 * i + j, j)
            for k in (TILES - 2, TILES - 1):
                body(k, k % 2)

        B_, HID1 = 8, 64
        MOM = 1.679177
        ring = [r0(4096 * k, (4096,)) for k in range(4)] + [r1(3072 + 4096 * k, (4096,)) for k in range(4)]
        W1_1, W2_1 = t.get("L1_ffn_W1"), t.get("L1_ffn_W2")
        weights = layer("gnn1")
        attr8 = R1[0:2 * B_, 0:E // 2]
        h3 = R1[0:HID1, 8192:8192 + E]
        norm_and_turn("gnn1_norm", columns=lambda a, c: a[:, 0:P] if c == 0 else a[:, P + c - 1:D:3],
                      loads="gnn1")
        keep1 = ExitStack()
        table_hi = keep1.enter_context(nc.sbuf_tensor("table_hi", [P, HALVES, D], F32R))
        table_lo = keep1.enter_context(nc.sbuf_tensor("table_lo", [P, HALVES, D], F32R))
        W4_hi = keep1.enter_context(nc.sbuf_tensor("W4_hi", [P, D], F32R))
        W4_lo = keep1.enter_context(nc.sbuf_tensor("W4_lo", [HID1, D], F32R))
        with Stage(nc, "gnn1_nodes") as st:
            a1 = st.sb("a1", [2 * HID1, 2, D])
            a2 = st.sb("a2", [2 * HID1, 2, D])
            fed, t_done, l1, l2, l3, s1, s2, s3, v = (st.sem(n) for n in
                                                     ("fed", "t_done", "l1", "l2", "l3", "s1", "s2", "s3", "v"))
            block = st.block()
            W1, W2, W3 = small["mlp1"], small["mlp2"], small["mlp3"]
            CH = E // (2 * D)

            @block.sync
            def _(sp):
                sp.dma_start(attr8, t["attr8"]).then_inc(fed, 16)
                for k, w in enumerate((W1_1, W2_1) * 2):
                    sp.dma_start(ring[k], w[k // 2].rearrange("(c p) n -> p c n", p=P)).then_inc(ring_in[k], 16)

            @block.tensor
            def _(pe):
                for h in range(HALVES):
                    for c in range(C):
                        last = pe.matmul(PS[:, 6 + h, c * P:(c + 1) * P], HT[:, c, h * P:(h + 1) * P],
                                         small["up0"] if c == 0 else small["up1"], start=True, stop=True,
                                         skip_group_check=True)
                    last.then_inc(t_done, 1)
                pe.wait_ge(fed, 16)

                def first(i):
                    for j in range(2):
                        if not (isinstance(i, int) and i == 0):
                            pe.wait_ge(s1, 2 * i + (j - 1))
                        pe.matmul(PS[:, j, :], W1, attr8[:, bass.ds((2 * i + j) * D, D)], start=True,
                                  stop=True).then_inc(l1, 1)

                def pair(i, peeled, end=False):
                    for j in range(2):
                        pe.wait_ge(s1, 2 * i + (j + 1))
                        if not peeled:
                            pe.wait_ge(s2, 2 * i + (j - 1))
                        pe.matmul(PS[:, 2 + j, :], W2, a1[:, j, :], start=True, stop=True).then_inc(l2, 1)
                    if not end:
                        first(i + 1)
                    for j in range(2):
                        pe.wait_ge(s2, 2 * i + (j + 1))
                        if not peeled:
                            pe.wait_ge(s3, 2 * i + (j - 1))
                        pe.matmul(PS[:, 4 + j, :], W3, a2[:, j, :], start=True, stop=True).then_inc(l3, 1)

                first(0)
                pair(0, True)
                with pe.Fori(1, CH // 2 - 1) as i:
                    pair(i, False)
                pair(CH // 2 - 1, False, True)

            @block.scalar
            def _(act):
                def first(i):
                    for j in range(2):
                        act.wait_ge(l1, 2 * i + (j + 1))
                        if not (isinstance(i, int) and i == 0):
                            act.wait_ge(l2, 2 * i + (j - 1))
                        act.activation(a1[:, j, :], PS[:, j, :], ACT.Silu, scale=B_ ** -0.5).then_inc(s1, 1)

                def pair(i, peeled, end=False):
                    for j in range(2):
                        act.wait_ge(l2, 2 * i + (j + 1))
                        if not peeled:
                            act.wait_ge(l3, 2 * i + (j - 1))
                        act.activation(a2[:, j, :], PS[:, 2 + j, :], ACT.Silu, scale=MOM / 8).then_inc(s2, 1)
                    if not end:
                        first(i + 1)
                    for j in range(2):
                        act.wait_ge(l3, 2 * i + (j + 1))
                        for half in range(2):
                            last = act.activation(h3[:, bass.ds((2 * (2 * i + j) + half) * D, D)],
                                                  PS[half * HID1:(half + 1) * HID1, 4 + j, :], ACT.Silu, scale=MOM / 8)
                        last.then_inc(s3, 1)

                first(0)
                pair(0, True)
                with act.Fori(1, CH // 2 - 1) as i:
                    pair(i, False)
                pair(CH // 2 - 1, False, True)

            @block.vector
            def _(dve):
                chain = Chain(dve, v)
                for h in range(HALVES):
                    dve.wait_ge(t_done, h + 1)
                    chain.link(dve.tensor_copy(table_hi[:, h, :], PS[:, 6 + h, :]))
                    dve.tensor_tensor(table_lo[:, h, :], PS[:, 6 + h, :], table_hi[:, h, :].bitcast(F32), ALU.subtract)
                chain.link(dve.tensor_copy(W4_hi[:, :], small["mlp4"]))
                chain.link(dve.tensor_tensor(W4_lo[:, :], small["mlp4"][0:HID1, :], W4_hi[0:HID1, :].bitcast(F32),
                                             ALU.subtract))

        with Stage(nc, "gnn1_edges") as st:
            from_src = st.sb("from_src", [P, 2, N])
            to_dst = st.sb("to_dst", [P, 2, N], F32R)
            pick = st.sb("pick", [P, 2, HALVES, P], F32R)
            h3_2 = st.sb("h3_2", [P, 2, P], F32R)
            w = R1[:, 16384:17408].rearrange("p (j k e) -> p j k e", j=2, k=4)
            prod = R1[:, 17408:18688].rearrange("p (j k e) -> p j k e", j=2, k=5)
            dots = R1[:, 18688:19456].rearrange("p (j k e) -> p j k e", j=2, k=3)
            terms = st.sb("terms", [P, 2, 3, P])
            sum4 = st.sb("sum4", [P, P])
            p4 = st.sb("p4", [P, 2, P])
            msg_hi, msg_lo = st.sb("msg_hi", [P, 2, 8, P], F32R), st.sb("msg_lo", [P, 2, 8, P], F32R)
            y = small["attr4"]
            names = ("src_hot", "dst_hot", "hi", "lo", "turned", "turned_out", "w_done", "w_out", "picked", "prods",
                     "terms", "p4", "msg_hi", "msg_lo", "summed", "v")
            s = {n: st.sem(n) for n in names}
            block = st.block()

            @block.tensor
            def _(pe):
                def turn(k, j):
                    pe.wait_ge(s["src_hot"], k + 1)
                    guard(pe, s["turned_out"], k, 1)
                    for h in range(HALVES):
                        last = pe.transpose(PS[:, 4, h * P:(h + 1) * P], from_src[:, j, h * P:(h + 1) * P], ident[:, :])
                    last.then_inc(s["turned"], 1)

                def weights_of(k, j):
                    pe.wait_ge(s["lo"], k + 1)
                    guard(pe, s["w_out"], k, 1)
                    pe.matmul(PS[:, 5, :], h3_2[:, j, :], W4_hi[:, :], start=True, stop=False)
                    pe.matmul(PS[:, 5, :], h3_2[0:HID1, j, :], W4_lo[:, :], start=False, stop=True).then_inc(s["w_done"], 1)

                def gather(k, j):
                    pe.wait_ge(s["turned_out"], k + 1)
                    guard(pe, s["prods"], k, 2)
                    for h in range(HALVES):
                        pe.matmul(PS[:, 6 + j, :], pick[:, j, h, :], table_hi[:, h, :], start=(h == 0), stop=False)
                        last = pe.matmul(PS[:, 6 + j, :], pick[:, j, h, :], table_lo[:, h, :], start=False, stop=(h == 1))
                    last.then_inc(s["picked"], 1)

                def back(k, j):
                    pe.wait_ge(s["dst_hot"], k + 1)
                    pe.wait_ge(s["msg_lo"], k + 1)
                    first, end = isinstance(k, int) and k == 0, isinstance(k, int) and k == TILES - 1
                    for h in range(HALVES):
                        for q in range(2):
                            for part in (msg_hi, msg_lo):
                                last = pe.matmul(PS[:, 2 * h + q, :], to_dst[:, j, h * P:(h + 1) * P],
                                                 flat(part[:, j, 4 * q:4 * q + 4, :]), start=first and part is msg_hi,
                                                 stop=end and part is msg_lo, skip_group_check=True)
                    last.then_inc(s["summed"], 1)

                def body(k, j):
                    if not (isinstance(k, int) and k >= TILES - 2):
                        turn(k + 2, j)
                    if not (isinstance(k, int) and k == TILES - 1):
                        weights_of(k + 1, 1 - j)
                        gather(k + 1, 1 - j)
                    if not (isinstance(k, int) and k == 0):
                        back(k - 1, 1 - j)

                turn(0, 0)
                turn(1, 1)
                weights_of(0, 0)
                gather(0, 0)
                over_tiles(pe, body)
                back(TILES - 1, 1)

            @block.scalar
            def _(act):
                def hidden(k, j):
                    guard(act, s["w_done"], k, 2)
                    act.activation(h3_2[0:HID1, j, :], h3[:, bass.ds(k * P, P)], ACT.Copy).then_inc(s["hi"], 1)

                def leave(k, j):
                    act.wait_ge(s["turned"], k + 1)
                    guard(act, s["picked"], k, 2)
                    act.activation(pick[:, j, :, :], PS[:, 4, 0:N].rearrange("p (a b) -> p a b", a=2),
                                   ACT.Copy).then_inc(s["turned_out"], 1)

                def weights_out(k, j):
                    act.wait_ge(s["w_done"], k + 1)
                    guard(act, s["prods"], k, 2)
                    act.activation(flat(w[:, j, :, :]), PS[:, 5, :], ACT.Copy).then_inc(s["w_out"], 1)

                def messages(k, j):
                    act.wait_ge(s["prods"], k + 1)
                    guard(act, s["summed"], k, 2)
                    for m in range(3):
                        last = act.activation(terms[:, j, m, :], dots[:, j, m, :], ACT.Copy, scale=y[:, bass.ds(k, 1), 1 + m])
                    last.then_inc(s["terms"], 1)
                    act.activation(msg_hi[:, j, 0:4, :], prod[:, j, 0:4, :], ACT.Copy, scale=y[:, bass.ds(k, 1), 0])
                    for m in range(3):
                        act.activation(msg_hi[:, j, 5 + m, :], prod[:, j, 4, :], ACT.Copy, scale=y[:, bass.ds(k, 1), 1 + m])

                def message4(k, j):
                    act.wait_ge(s["p4"], k + 1)
                    act.activation(msg_hi[:, j, 4, :], p4[:, j, :], ACT.Copy).then_inc(s["msg_hi"], 1)

                def body(k, j):
                    if not (isinstance(k, int) and k >= TILES - 2):
                        hidden(k + 2, j)
                    if not (isinstance(k, int) and k == TILES - 1):
                        weights_out(k + 1, 1 - j)
                    messages(k, j)
                    if not (isinstance(k, int) and k >= TILES - 2):
                        leave(k + 2, j)
                    message4(k, j)

                hidden(0, 0)
                leave(0, 0)
                hidden(1, 1)
                leave(1, 1)
                weights_out(0, 0)
                over_tiles(act, body)

            @block.vector
            def _(dve):
                def hot(k, j):
                    guard(dve, s["turned"], k, 2)
                    dve.tensor_scalar(from_src[:, j, :], iota[:, :], src_col[:, bass.ds(k, 1)], None,
                                      ALU.is_equal).then_inc(s["src_hot"], 1)

                def low_hidden(k, j):
                    dve.wait_ge(s["hi"], k + 1)
                    dve.tensor_tensor(h3_2[HID1:P, j, :], h3[:, bass.ds(k * P, P)], h3_2[0:HID1, j, :].bitcast(F32),
                                      ALU.subtract).then_inc(s["lo"], 1)

                def products(k, j):
                    dve.wait_ge(s["picked"], k + 1)
                    dve.wait_ge(s["w_out"], k + 1)
                    guard(dve, s["msg_lo"], k, 2)
                    x = PS[:, 6 + j, :].rearrange("p (a b) -> p a b", a=4)
                    three = lambda a: a.unsqueeze(1).broadcast_to([P, 3, P])
                    dve.tensor_tensor(prod[:, j, 0::4, :], w[:, j, 0:2, :],
                                      x[:, 0, :].unsqueeze(1).broadcast_to([P, 2, P]), ALU.mult)
                    dve.tensor_tensor(prod[:, j, 1:4, :], x[:, 1:4, :], three(w[:, j, 2, :]), ALU.mult)
                    dve.tensor_tensor(dots[:, j, :, :], x[:, 1:4, :], three(w[:, j, 3, :]),
                                      ALU.mult).then_inc(s["prods"], 1)

                def low(k, j):
                    dve.wait_ge(s["msg_hi"], k + 1)
                    guard(dve, s["summed"], k, 2)
                    hi = msg_hi[:, j, :, :].bitcast(F32)
                    dve.scalar_tensor_tensor(msg_lo[:, j, 0:4, :], prod[:, j, 0:4, :], y[:, bass.ds(k, 1), 0], hi[:, 0:4, :],
                                             ALU.mult, ALU.subtract)
                    for m in range(3):
                        dve.scalar_tensor_tensor(msg_lo[:, j, 5 + m, :], prod[:, j, 4, :], y[:, bass.ds(k, 1), 1 + m],
                                                 hi[:, 5 + m, :], ALU.mult, ALU.subtract)
                    dve.tensor_scalar(to_dst[:, j, :], iota[:, :], dst_col[:, bass.ds(k, 1)], None,
                                      ALU.is_equal).then_inc(s["dst_hot"], 1)
                    dve.tensor_tensor(msg_lo[:, j, 4, :], p4[:, j, :], hi[:, 4, :], ALU.subtract).then_inc(s["msg_lo"], 1)

                def body(k, j):
                    if not (isinstance(k, int) and k >= TILES - 2):
                        hot(k + 2, j)
                    products(k, j)
                    if not (isinstance(k, int) and k == 0):
                        low(k - 1, 1 - j)
                    if not (isinstance(k, int) and k >= TILES - 2):
                        low_hidden(k + 2, j)

                for k in range(2):
                    hot(k, k)
                    low_hidden(k, k)
                over_tiles(dve, body, head=4)
                low(TILES - 1, 1)

            @block.gpsimd
            def _(pool):
                def body(k, j):
                    pool.wait_ge(s["terms"], k + 1)
                    pool.tensor_tensor(sum4[:, :], terms[:, j, 0, :], terms[:, j, 1, :], ALU.add).then_inc(s["v"], 1)
                    pool.wait_ge(s["v"], k + 1)
                    guard(pool, s["msg_lo"], k, 2)
                    pool.tensor_tensor(p4[:, j, :], sum4[:, :], terms[:, j, 2, :], ALU.add).then_inc(s["p4"], 1)
                    pool.wait_ge(s["p4"], k + 1)

                over_tiles(pool, body)

        with Stage(nc, "gnn1_out") as st:
            sums = st.sb("sums", [P, HALVES, 8, P])
            sumsT = st.sb("sumsT", [P, 8, N])
            out_, turned, tout, done, v = (st.sem(n) for n in ("out", "turned", "tout", "done", "v"))
            block = st.block()
            order = [(0, 4), (5, 1), (6, 2), (7, 3)]

            @block.vector
            def _(dve):
                chain = Chain(dve, v)
                for h in range(HALVES):
                    for q in range(2):
                        dve.tensor_copy(flat(sums[:, h, 4 * q:4 * q + 4, :]), PS[:, 2 * h + q, :]).then_inc(out_, 1)
                scale = MOM / 8 * P ** -0.5 / 16 / 10
                for h in range(HALVES):
                    dve.wait_ge(done, h + 1)
                    o = PS[:, 6 + h, :].rearrange("p (c n) -> p c n", c=C)
                    chain.link(dve.scalar_tensor_tensor(X[:, h, 0:P], o[:, 0, :], scale, X[:, h, 0:P], ALU.mult, ALU.add))
                    x1 = X[:, h, P:D].rearrange("p (u m) -> p m u", m=3)
                    chain.link(dve.scalar_tensor_tensor(x1, o[:, 1:4, :], scale, x1, ALU.mult, ALU.add))

            @block.tensor
            def _(pe):
                pe.wait_ge(out_, 4)
                for k in range(8):
                    if k >= 4:
                        pe.wait_ge(tout, k - 3)
                    for h in range(HALVES):
                        last = pe.transpose(PS[:, k % 4, h * P:(h + 1) * P], sums[:, h, k, :], ident[:, :])
                    last.then_inc(turned, 1)
                pe.wait_ge(tout, 8)
                for h in range(HALVES):
                    for c in range(C):
                        W = small["out0"] if c == 0 else small["out1"]
                        for b in range(2):
                            last = pe.matmul(PS[:, 6 + h, c * P:(c + 1) * P], sumsT[:, order[c][b], h * P:(h + 1) * P],
                                             W[:, b, :], start=(b == 0), stop=(b == 1), skip_group_check=True)
                    last.then_inc(done, 1)

            @block.scalar
            def _(act):
                for k in range(8):
                    act.wait_ge(turned, k + 1)
                    act.activation(sumsT[:, k, :], PS[:, k % 4, 0:N], ACT.Copy,
                                   scale=3 ** -0.5 if k == 4 else 1.0).then_inc(tout, 1)
        keep1.close()
        weights.close()
        NE1, CAP, F1 = 8, 64, 1024
        FC1 = F1 // P
        weights = layer("ffn1")
        norm_and_turn("ffn1_norm", loads="ffn1")
        keep1 = ExitStack()
        chosenT = keep1.enter_context(nc.sbuf_tensor("chosenT", [P, 4, N], F32))
        exT = keep1.enter_context(nc.sbuf_tensor("exT", [P, C, NE1 * CAP], F32))
        Yp = R1[:, 0:4 * D].rearrange("p (g d) -> p g d", g=4)
        with Stage(nc, "ffn1_choose") as st:
            before = R1[:, 2048:2048 + 512].rearrange("p (h n) -> p h n", h=2)
            S8 = st.sb("S8", [P, HALVES, NE1])
            S8T = st.sb("S8T", [NE1, N])
            sel = st.sb("sel", [NE1, NE1, P])
            best = st.sb("best", [P, HALVES])
            above = st.sb("above", [P, HALVES, NE1])
            level = st.sb("level", [P, HALVES, NE1])
            junk = R1[:, 2560:2560 + 256]
            place, placeG = st.sb("place", [P, HALVES, NE1 * CAP]), st.sb("placeG", [P, HALVES, NE1 * CAP])
            names = ("ins", "logits", "shifted", "exped", "probs", "turned", "turned_out", "spread_", "ranked",
                     "placed", "gathered", "gturned", "g8", "v")
            s = {n: st.sem(n) for n in names}
            block = st.block()

            @block.sync
            def _(sp):
                sp.dma_start(before, t["before"]).then_inc(s["ins"], 16)
                sp.dma_start(sel[:, :, :], t["select8"]).then_inc(s["ins"], 16)
                for k in range(4, 8):
                    sp.dma_start(ring[k], (W1_1, W2_1)[k % 2][k // 2].rearrange("(c p) n -> p c n", p=P)).then_inc(
                        ring_in[k], 16)

            @block.tensor
            def _(pe):
                pe.wait_ge(s["ins"], 32)
                for h in range(HALVES):
                    for c in range(C):
                        last = pe.matmul(PS[:, 4 + h, 0:NE1], HT[:, c, h * P:(h + 1) * P], small["ffn1_Wg"][:, c, :],
                                         start=(c == 0), stop=(c == C - 1))
                    last.then_inc(s["logits"], 1)
                pe.wait_ge(s["probs"], HALVES)
                for h in range(HALVES):
                    last = pe.transpose(PS[0:NE1, 6, h * P:(h + 1) * P], S8[:, h, :], ident[:, :])
                last.then_inc(s["turned"], 1)
                pe.wait_ge(s["turned_out"], 1)
                for e in range(NE1):
                    last = pe.matmul(PS[:, e // 2, (e % 2) * N:(e % 2 + 1) * N], sel[:, e, :], S8T[:, :], start=True,
                                     stop=True, skip_group_check=True)
                last.then_inc(s["spread_"], 1)
                pe.wait_ge(s["placed"], 1)
                for c in range(C):
                    for h in range(HALVES):
                        last = pe.matmul(PS[:, c, :], XN[:, h, c * P:(c + 1) * P], place[:, h, :], start=(h == 0),
                                         stop=(h == 1))
                    last.then_inc(s["gathered"], 1)
                for h in range(HALVES):
                    for g in range(4):
                        last = pe.transpose(PS[:, 4 + h, g * P:(g + 1) * P], placeG[:, h, g * P:(g + 1) * P], ident[:, :])
                    last.then_inc(s["gturned"], 1)
                for h in range(HALVES):
                    last = pe.transpose(PS[0:NE1, 6, h * P:(h + 1) * P], gates[:, h, 0:NE1], ident[:, :])
                last.then_inc(s["g8"], 1)

            @block.scalar
            def _(act):
                act.wait_ge(s["shifted"], 1)
                act.activation(S8[:, :, :], S8[:, :, :], ACT.Exp).then_inc(s["exped"], 1)
                act.wait_ge(s["turned"], 1)
                act.activation(S8T[:, :], PS[0:NE1, 6, 0:N], ACT.Copy).then_inc(s["turned_out"], 1)
                for c in range(C):
                    act.wait_ge(s["gathered"], c + 1)
                    act.activation(exT[:, c, :], PS[:, c, :], ACT.Copy)
                for h in range(HALVES):
                    act.wait_ge(s["gturned"], h + 1)
                    act.activation(chosenT[:, :, h * P:(h + 1) * P],
                                   PS[:, 4 + h, :].rearrange("p (g n) -> p g n", g=4), ACT.Copy)
                act.wait_ge(s["g8"], 1)
                act.activation(gatesT[0:NE1, :], PS[0:NE1, 6, 0:N], ACT.Copy)

            @block.vector
            def _(dve):
                chain = Chain(dve, s["v"])
                wide = lambda a: a.unsqueeze(2).broadcast_to([P, HALVES, NE1])
                for h in range(HALVES):
                    dve.wait_ge(s["logits"], h + 1)
                    chain.link(dve.tensor_copy(S8[:, h, :], PS[:, 4 + h, 0:NE1]))
                chain.link(dve.tensor_reduce(best[:, :], S8[:, :, :], AX_X, ALU.max))
                dve.tensor_tensor(S8[:, :, :], S8[:, :, :], wide(best[:, :]), ALU.subtract).then_inc(s["shifted"], 1)
                dve.wait_ge(s["exped"], 1)
                chain.link(dve.tensor_reduce(best[:, :], S8[:, :, :], AX_X, ALU.add))
                chain.link(dve.reciprocal(best[:, :], best[:, :]))
                dve.tensor_tensor(S8[:, :, :], S8[:, :, :], wide(best[:, :]), ALU.mult).then_inc(s["probs"], HALVES)
                dve.wait_ge(s["ins"], 32)
                dve.wait_ge(s["spread_"], 1)
                dve.wait_ge(s["probs"], HALVES)
                for h in range(HALVES):
                    for e in range(NE1):
                        row = PS[:, e // 2, (e % 2) * N:(e % 2 + 1) * N]
                        chain.link(dve.tensor_scalar(junk, row, S8[:, h, e:e + 1], 0.0, ALU.is_gt, ALU.add,
                                                     accum_out=above[:, h, e:e + 1]))
                        chain.link(dve.scalar_tensor_tensor(junk, row, S8[:, h, e:e + 1], before[:, h, :],
                                                            ALU.is_equal, ALU.mult,
                                                            accum_out=level[:, h, e:e + 1]))
                chain.link(dve.tensor_tensor(above[:, :, :], above[:, :, :], level[:, :, :], ALU.add))
                chain.link(dve.scalar_tensor_tensor(gates[:, :, 0:NE1], above[:, :, :], float(CAP), S8[:, :, :],
                                                    ALU.is_lt, ALU.mult))
                for h in range(HALVES):
                    for e in range(NE1):
                        a = slice(e * CAP, (e + 1) * CAP)
                        dve.tensor_scalar(place[:, h, a], iota[:, 0:CAP], above[:, h, e:e + 1], None, ALU.is_equal)
                        last = dve.tensor_scalar(placeG[:, h, a], iota[:, 0:CAP], above[:, h, e:e + 1],
                                                 S8[:, h, e:e + 1], ALU.is_equal, ALU.mult)
                last.then_inc(s["placed"], 1)

        with Stage(nc, "ffn1_experts") as st:
            hid = st.sb("hid", [P, 2, FC1, CAP])
            names = ("h_done", "h_out", "y_done", "y_out")
            s = {n: st.sem(n) for n in names}
            b1c = small["ffn1_b1"]
            block = st.block()

            @block.sync
            def _(sp):
                for e in range(4, NE1):
                    for b, (w, used) in enumerate(((W1_1, s["h_done"]), (W2_1, s["y_done"]))):
                        sp.wait_ge(used, e - 3)
                        sp.dma_start(ring[2 * (e - 4) + b], w[e].rearrange("(c p) n -> p c n", p=P)).then_inc(
                            ring_in[2 * (e - 4) + b], 16)

            @block.tensor
            def _(pe):
                def expert(e):
                    j, W1 = e % 2, ring[2 * (e % 4)].rearrange("p (c n) -> p c n", c=C)
                    pe.wait_ge(ring_in[2 * (e % 4)], 16 * (e // 4) + 16)
                    if e >= 2:
                        pe.wait_ge(s["h_out"], e - 1)
                    for f in range(FC1):
                        for c in range(C):
                            last = pe.matmul(PS[:, j, f * CAP:(f + 1) * CAP], W1[:, c, f * P:(f + 1) * P],
                                             exT[:, c, e * CAP:(e + 1) * CAP], start=(c == 0),
                                             stop=(c == C - 1), skip_group_check=True)
                    last.then_inc(s["h_done"], 1)

                def result(e):
                    j, W2 = e % 2, ring[2 * (e % 4) + 1].rearrange("p (c n) -> p c n", c=FC1)
                    pe.wait_ge(ring_in[2 * (e % 4) + 1], 16 * (e // 4) + 16)
                    pe.wait_ge(s["h_out"], e + 1)
                    if e >= 2:
                        pe.wait_ge(s["y_out"], e - 1)
                    for f in range(FC1):
                        last = pe.matmul(PS[j * CAP:(j + 1) * CAP, 2 + j, :], hid[:, j, f, :], W2[:, f, :],
                                         start=(f == 0), stop=(f == FC1 - 1))
                    last.then_inc(s["y_done"], 1)

                expert(0)
                for e in range(NE1):
                    if e + 1 < NE1:
                        expert(e + 1)
                    result(e)

            @block.scalar
            def _(act):
                for e in range(NE1):
                    act.wait_ge(s["h_done"], e + 1)
                    if e >= 2:
                        act.wait_ge(s["y_done"], e - 1)
                    for f in range(FC1):
                        last = act.activation(hid[:, e % 2, f, :], PS[:, e % 2, f * CAP:(f + 1) * CAP], ACT.Gelu,
                                              bias=b1c[:, e, f:f + 1])
                    last.then_inc(s["h_out"], 1)

            @block.vector
            def _(dve):
                for e in range(NE1):
                    rows = slice(e % 2 * CAP, (e % 2 + 1) * CAP)
                    dve.wait_ge(s["y_done"], e + 1)
                    dve.tensor_copy(Yp[rows, e // 2, :], PS[rows, 2 + e % 2, :]).then_inc(s["y_out"], 1)

        with Stage(nc, "ffn1_out") as st:
            done, v = st.sem("done"), st.sem("v")
            block = st.block()

            @block.tensor
            def _(pe):
                for h in range(HALVES):
                    for g in range(4):
                        pe.matmul(PS[:, h, :], chosenT[:, g, h * P:(h + 1) * P], Yp[:, g, :], start=(g == 0), stop=False)
                    pe.matmul(PS[:, h, :], gatesT[0:NE1, h * P:(h + 1) * P], small["ffn1_b2"][:, :], start=False,
                              stop=True).then_inc(done, 1)

            @block.vector
            def _(dve):
                chain = Chain(dve, v)
                for h in range(HALVES):
                    dve.wait_ge(done, h + 1)
                    chain.link(dve.tensor_tensor(X[:, h, :], X[:, h, :], PS[:, h, :], ALU.add))
        keep1.close()
        weights.close()
        EF, NH2, HD2 = 128, 16, 32
        ROW = EF + 2

        def project(name, parts, bias, sink, waits=(), pool_program=None):
            with Stage(nc, name) as st:
                done = st.sem("done")
                block = st.block()
                if pool_program:
                    block.gpsimd(pool_program)

                @block.tensor
                def _(pe):
                    for w in waits:
                        pe.wait_ge(*w)
                    for h in range(HALVES):
                        every = [(a, W, c) for a, W, m in parts for c in range(m)]
                        for q, (a, W, c) in enumerate(every):
                            last = pe.matmul(PS[:, h, :], a[:, c, h * P:(h + 1) * P], W[:, c, :], start=(q == 0),
                                             stop=(q == len(every) - 1))
                        last.then_inc(done, 1)

                @block.vector
                def _(dve):
                    for h in range(HALVES):
                        dve.wait_ge(done, h + 1)
                        dve.tensor_tensor(sink[:, h, :], PS[:, h, :], bias, ALU.add)

        def split(name, pairs):
            with Stage(nc, name) as st:
                v = st.sem("v")
                block = st.block()

                @block.vector
                def _(dve):
                    chain = Chain(dve, v)
                    for a, hi, lo in pairs:
                        chain.link(dve.tensor_copy(hi, a))
                        chain.link(dve.tensor_tensor(lo, a, hi.bitcast(F32), ALU.subtract))

        weights = layer("gnn2")
        scratch = nc.dram_tensor("sorted_edges", (E, ROW), F32, kind="Internal").ap()
        pens = nc.dram_tensor("pens", (2, E), F32, kind="Internal").ap()
        at, W2 = 0, {}
        for name, n in (("hk_W1a", 4), ("hk_W1b", 1), ("hv_W1a", 4), ("hv_W1b", 1), ("hq_W1", 4), ("hk_W2", 4),
                        ("hv_W2", 4), ("hq_W2", 4), ("no_W1", 8), ("no_W2", 4)):
            W2[name] = r1(at, (n, D))
            at += n * D
        edges = R0[:, 0:TILES * ROW].rearrange("p (t r) -> p t r", r=ROW)
        with Stage(nc, "gnn2_rank") as st:
            BF = mybir.dt.bfloat16
            pos = st.sb("pos", [P, TILES])
            masks = st.sb("masks", [P, 2, P])
            strict = st.sb("strict", [P, 2, P], BF)
            onesb = st.sb("onesb", [P, P], BF)
            GROUPS = 4
            STEPS = TILES // GROUPS
            over = st.sb("over", [P, 4, 2, N], BF)
            hot = st.sb("hot", [P, 2, GROUPS, N], BF)
            iota_b = st.sb("iota_b", [P, N], BF)
            junk = st.sb("junk", [P, GROUPS, N])
            total = st.sb("total", [P, 2, N])
            names = ("ins", "small_in", "consts", "under", "counted", "first_out", "hots", "ranked", "read", "closed", "last_out",
                     "turned", "v")
            s = {n: st.sem(n) for n in names}
            block = st.block()

            @block.sync
            def _(sp):
                sp.dma_start(masks[:, :, :], t["masks"]).then_inc(s["ins"], 16)
                sp.dma_start(edges[:, :, 0:EF], t["attr128"]).then_inc(s["ins"], 16)
                load_small(sp, "gnn2", s["small_in"])
                for name, w in W2.items():
                    sp.dma_start(w, t["g2_" + name].rearrange("(c p) n -> p c n", p=P)).then_inc(w_gnn2, 16)
                sp.wait_ge(s["small_in"], 16 * len(SMALL_SHAPES["gnn2"]))

            @block.tensor
            def _(pe):
                def count(k, j, g, first):
                    pe.wait_ge(s["under"], k + 1)
                    for b in range(GROUPS):
                        last = pe.matmul(PS[:, b, 0:N], onesb[:, :], over[:, j, int(g < b), :], start=first, stop=False,
                                         skip_group_check=True)
                    last.then_inc(s["counted"], 1)

                pe.wait_ge(s["consts"], 1)
                for j in range(4):
                    count(j, j, 0, j == 0)
                for g in range(GROUPS):
                    with pe.Fori(max(g * STEPS // 4, 1), (g + 1) * STEPS // 4) as i:
                        for j in range(4):
                            count(4 * i + j, j, g, False)

                def ranked(i, p, g):
                    pe.wait_ge(s["hots"], GROUPS * i + (g + 1))
                    pe.matmul(PS[:, g, 0:N], strict[:, 0, :], hot[:, p, g, :], start=False, stop=False,
                              skip_group_check=True).then_inc(s["ranked"], 1)

                def closed(i, p, g):
                    pe.wait_ge(s["read"], GROUPS * i + (g + 1))
                    pe.matmul(PS[:, g, 0:N], strict[:, 1, :], hot[:, p, g, :], start=False, stop=False,
                              skip_group_check=True).then_inc(s["closed"], 1)

                pe.wait_ge(s["first_out"], 1)
                for g in range(GROUPS):
                    ranked(0, 0, g)
                with pe.Fori(0, STEPS // 2 - 1) as i:
                    for p in range(2):
                        for g in range(GROUPS):
                            closed(2 * i + p, p, g)
                            ranked(2 * i + p + 1, 1 - p, g)
                for g in range(GROUPS):
                    closed(STEPS - 2, 0, g)
                    ranked(STEPS - 1, 1, g)
                for g in range(GROUPS):
                    closed(STEPS - 1, 1, g)
                pe.wait_ge(s["last_out"], 1)
                for q in range(2):
                    for h in range(HALVES):
                        last = pe.transpose(PS[:, 4 + q, h * P:(h + 1) * P], total[:, q, h * P:(h + 1) * P], ident[:, :])
                last.then_inc(s["turned"], 1)

            @block.vector
            def _(dve):
                chain = Chain(dve, s["v"])
                dve.wait_ge(s["ins"], 32)
                dve.memset(onesb[:, :], 1.0)
                chain.link(dve.tensor_copy(iota_b[:, :], iota[:, :]))
                dve.tensor_copy(edges[:, :, EF], src_col[:, :])
                dve.tensor_copy(edges[:, :, EF + 1], dst_col[:, :])
                dve.tensor_copy(strict[:, :, :], masks[:, :, :]).then_inc(s["consts"], 1)

                def under(k, j, first):
                    if not first:
                        dve.wait_ge(s["counted"], k - 3)
                    for q, op in enumerate((ALU.is_gt, ALU.is_ge)):
                        last = dve.tensor_scalar(over[:, j, q, :], iota_b[:, :], dst_col[:, bass.ds(k, 1)], None, op)
                    last.then_inc(s["under"], 1)

                for j in range(4):
                    under(j, j, True)
                with dve.Fori(1, TILES // 4) as i:
                    for j in range(4):
                        under(4 * i + j, j, False)

                def hots(i, p, g, first):
                    if not first:
                        dve.wait_ge(s["closed"], GROUPS * i + (g + 1 - 2 * GROUPS))
                    dve.tensor_scalar(hot[:, p, g, :], iota_b[:, :], dst_col[:, bass.ds(i + g * STEPS, 1)], None,
                                      ALU.is_equal).then_inc(s["hots"], 1)

                for i in range(2):
                    for g in range(GROUPS):
                        hots(i, i, g, True)
                dve.wait_ge(s["counted"], TILES)
                dve.tensor_copy(total[:, 0, :], PS[:, 0, 0:N]).then_inc(s["first_out"], 1)

                def step(i, p, end):
                    for g in range(GROUPS):
                        dve.wait_ge(s["ranked"], GROUPS * i + (g + 1))
                        dve.scalar_tensor_tensor(junk[:, g, :], PS[:, g, 0:N], 1.0, hot[:, p, g, :], ALU.mult, ALU.mult,
                                                 accum_out=pos[:, bass.ds(i + g * STEPS, 1)]).then_inc(s["read"], 1)
                        if g and not end:
                            hots(i + 2, p, g - 1, False)
                    if not end:
                        hots(i + 2, p, GROUPS - 1, False)

                with dve.Fori(0, STEPS // 2 - 1) as i:
                    for p in range(2):
                        step(2 * i + p, p, False)
                for p in range(2):
                    step(STEPS - 2 + p, p, True)
                dve.wait_ge(s["read"], TILES)
                chain.link(dve.tensor_copy(pos_i[:, :], pos[:, :]))
                dve.wait_ge(s["closed"], TILES)
                dve.tensor_copy(total[:, 1, :], PS[:, GROUPS - 1, 0:N]).then_inc(s["last_out"], 1)
                dve.wait_ge(s["turned"], 1)
                for q in range(2):
                    dve.tensor_copy(bounds[:, :, q], PS[:, 4 + q, 0:N:P])

        q2 = ExitStack()
        sr = lambda name, shape: q2.enter_context(nc.sbuf_tensor(name, shape, F32R))
        A_hi, A_lo = sr("A_hi", [P, HALVES, D]), sr("A_lo", [P, HALVES, D])
        Q_hi, Q_lo = sr("Q_hi", [P, HALVES, D]), sr("Q_lo", [P, HALVES, D])
        NX = NH2 + 2
        X_hi, X_lo = sr("X_hi", [P, HALVES, NX]), sr("X_lo", [P, HALVES, NX])
        def sorts(a, b):
            def program(pool):
                for k in range(a, b):
                    pool.indirect_dma_start(scratch, bass.IndirectOffsetOnAxis(ap=pos_i[:, k:k + 1], axis=0),
                                            edges[:, k, :], None, bounds_check=E - 1).then_inc(moved, 16)
                if b == TILES:
                    pool.wait_ge(moved, 16 * TILES)
            return program

        def up(shape):
            upper_at[0] += int(np.prod(shape))
            v = R0[:, upper_at[0] - int(np.prod(shape)):upper_at[0]]
            return v.rearrange("p (a b) -> p a b", a=shape[0]) if len(shape) == 2 else v
        upper_at = [TILES * ROW]
        L = up((TILES, NH2))
        node_k, node_v, hid_no = up((HALVES, D)), up((HALVES, D)), up((HALVES, D))
        extra = q2.enter_context(nc.sbuf_tensor("extra", [P, HALVES, NX], F32))
        norm_and_turn("gnn2_norm", pool_program=sorts(0, 10))
        wait2 = [(w_gnn2, 16 * len(W2))]
        rows2 = {n: small["gnn2_rows"][:, k, :] for k, n in enumerate(("hk_b1", "hv_b1", "hq_b1", "hk_b2", "hv_b2",
                                                                      "hq_b2", "no_b1", "no_b2"))}
        cols2 = {n: (small["gnn2_cols"][:, 2 * k, :], small["gnn2_cols"][:, 2 * k + 1, :])
                 for k, n in enumerate(("hk", "hv", "hq", "no"))}
        mid = upper_at[0]
        qh, qb = up((HALVES, D)), up((HALVES, D))
        project("gnn2_nk", [(HT, W2["hk_W1a"], C)], rows2["hk_b1"], node_k, wait2, pool_program=sorts(10, 20))
        project("gnn2_nv", [(HT, W2["hv_W1a"], C)], rows2["hv_b1"], node_v, pool_program=sorts(20, 28))
        project("gnn2_nh", [(HT, W2["no_W1"][:, 4:8, :], C)], rows2["no_b1"], hid_no, pool_program=sorts(28, 35))
        project("gnn2_nq", [(HT, W2["hq_W1"], C)], rows2["hq_b1"], qh, pool_program=sorts(35, 42))
        norm_and_turn("gnn2_qnorm", affine=cols2["hq"], source=qh, into=qh, func=ACT.Relu, pool_program=sorts(42, 50))
        project("gnn2_q", [(HT, W2["hq_W2"], C)], rows2["hq_b2"], qh, pool_program=sorts(50, 56))
        with Stage(nc, "gnn2_tables") as st:
            v = st.sem("v")
            block = st.block()
            block.gpsimd(sorts(56, TILES))

            @block.vector
            def _(dve):
                chain = Chain(dve, v)
                chain.link(dve.tensor_scalar(flat(qh), flat(qh), HD2 ** -0.5, None, ALU.mult))
                for h in range(HALVES):
                    chain.link(dve.tensor_tensor(qb[:, h, :], qh[:, h, :], rows2["hk_b2"], ALU.mult))
                    chain.link(dve.tensor_reduce(extra[:, h, 0:NH2], qb[:, h, :].rearrange("p (a b) -> p a b", a=NH2),
                                                 AX_X, ALU.add))
                chain.link(dve.tensor_copy(extra[:, :, NH2:NX], bounds[:, :, :]))
                for a, hi, lo in ((qh, Q_hi, Q_lo), (extra, X_hi, X_lo)):
                    chain.link(dve.tensor_copy(hi[:, :, :], a[:, :, :]))
                    chain.link(dve.tensor_tensor(lo[:, :, :], a[:, :, :], hi[:, :, :].bitcast(F32), ALU.subtract))

        penF, penL = [q2.enter_context(nc.sbuf_tensor(f"pen{k}", [P, TILES], F32)) for k in range(2)]
        sdst = q2.enter_context(nc.sbuf_tensor("sdst", [P, TILES, 2], F32))

        def edge_pass(name, keys, W1b, W2e, gain, offset, table):
            with Stage(nc, name) as st:
                upper_at[0] = mid
                overlay = lambda label, at, shape: nc.alloc_sbuf_tensor_at(f"{name}_{label}", shape, F32R,
                                                                          offset=r0_at + at)
                W_hi, W_lo = overlay("W_hi", 0, [P, C, D]), overlay("W_lo", 8192, [P, C, D])
                B_hi, B_lo = overlay("B_hi", 16384, [P, D]), overlay("B_lo", 18432, [P, D])
                ef_hi, ef_lo = overlay("ef_hi", 20480, [P, 2, P]), overlay("ef_lo", 21504, [P, 2, P])
                r_hi, r_lo = overlay("r_hi", 24576, [P, 2, D]), overlay("r_lo", 28672, [P, 2, D])
                prod = R0[:, 5632:6144]
                hn = up((2, D))
                rT = up((2, D))
                n_hot = 4 if keys else 2
                WIDE = D + NH2
                if keys:
                    qs = r1(0, (2, D))
                    hots = r1(1024, (4, N))
                else:
                    hots = up((2, N))
                    to_dst = st.sb("to_dst", [P, 2, N], F32R)
                    full = up((2, WIDE))
                    m_hi, m_lo = st.sb("m_hi", [P, 2, WIDE], F32R), st.sb("m_lo", [P, 2, WIDE], F32R)
                rowt = st.sb("rowt", [P, 2, ROW])
                pick = st.sb("pick", [P, 2, n_hot * P], F32R)
                stats, mv = st.sb("stats", [P, 2, 6]), st.sb("mv", [P, 2, 2])
                rstd, shift = st.sb("rstd", [P, 2]), st.sb("shift", [P, 2])
                names = ("rows0", "rows1", "hot", "saved", "f1", "ef_hi", "ef_out", "ef_lo", "hidden", "varied", "rooted",
                         "scaled", "normed", "hn_turned", "relued", "r_hi", "r_lo", "f4", "q_out", "used", "m_hi", "m_lo",
                         "scattered", "q_done", "v", "stat", "split")
                s = {n: st.sem(n) for n in names}
                block = st.block()

                @block.sync
                def _(sp):
                    def body(k, j):
                        guard(sp, s["f1"], k, 2)
                        guard(sp, s["saved"], k, 2)
                        sp.dma_start(rowt[:, j, :], scratch[bass.ds(k * P, P), :]).then_inc(s[f"rows{j}"], 16)

                    over_tiles(sp, body)

                @block.tensor
                def _(pe):
                    def turn_hot(k, j):
                        pe.wait_ge(s["hot"], k + 1)
                        guard(pe, s["ef_out"], k, 1)
                        guard(pe, s["ef_lo"], k, 1)
                        pe.wait_ge(s[f"rows{j}"], 8 * (k - j) + 16)
                        pe.transpose(PS[:, 5, 0:P], rowt[:, j, 0:EF], ident[:, :])
                        for q in range(n_hot):
                            last = pe.transpose(PS[:, 4, q * P:(q + 1) * P],
                                                hots[:, 2 * (q // 2) + j, (q % 2) * P:(q % 2 + 1) * P], ident[:, :])
                        last.then_inc(s["f1"], 1)

                    def hidden(k, j):
                        pe.wait_ge(s["ef_out"], k + 1)
                        guard(pe, s["normed"], k, 1)
                        for h in range(HALVES):
                            pe.matmul(PS[:, 0, :], pick[:, j, h * P:(h + 1) * P], A_hi[:, h, :], start=(h == 0), stop=False)
                            pe.matmul(PS[:, 0, :], pick[:, j, h * P:(h + 1) * P], A_lo[:, h, :], start=False, stop=False)
                        pe.matmul(PS[:, 0, :], ef_hi[:, j, :], B_hi[:, :], start=False, stop=False)
                        pe.matmul(PS[:, 0, :], ef_hi[:, j, :], B_lo[:, :], start=False, stop=False)
                        pe.wait_ge(s["ef_lo"], k + 1)
                        pe.matmul(PS[:, 0, :], ef_lo[:, j, :], B_hi[:, :], start=False, stop=True).then_inc(s["hidden"], 1)
                        if keys:
                            guard(pe, s["q_out"], k, 1)
                            for h in range(HALVES):
                                a = pick[:, j, (2 + h) * P:(3 + h) * P]
                                pe.matmul(PS[:, 1, :], a, Q_hi[:, h, :], start=(h == 0), stop=False)
                                pe.matmul(PS[:, 1, :], a, Q_lo[:, h, :], start=False, stop=(h == 1))
                            guard(pe, s["used"], k, 2)
                            for h in range(HALVES):
                                a = pick[:, j, (2 + h) * P:(3 + h) * P]
                                pe.matmul(PS[:, 6 + j, 0:NX], a, X_hi[:, h, :], start=(h == 0), stop=False)
                                last = pe.matmul(PS[:, 6 + j, 0:NX], a, X_lo[:, h, :], start=False, stop=(h == 1))
                            last.then_inc(s["q_done"], 1)

                    def outer(k, j):
                        pe.wait_ge(s["r_hi"], k + 1)
                        guard(pe, s["used"], k, 1)
                        for c in range(C):
                            a = r_hi[:, j, c * P:(c + 1) * P]
                            pe.matmul(PS[:, 3, :], a, W_hi[:, c, :], start=(c == 0), stop=False)
                            pe.matmul(PS[:, 3, :], a, W_lo[:, c, :], start=False, stop=False)
                        pe.wait_ge(s["r_lo"], k + 1)
                        for c in range(C):
                            last = pe.matmul(PS[:, 3, :], r_lo[:, j, c * P:(c + 1) * P], W_hi[:, c, :], start=False,
                                             stop=(c == C - 1))
                        last.then_inc(s["f4"], 1)

                    def turn_normed(k, j):
                        pe.wait_ge(s["normed"], k + 1)
                        guard(pe, s["relued"], k, 1)
                        for c in range(C):
                            last = pe.transpose(PS[:, 2, c * P:(c + 1) * P], hn[:, j, c * P:(c + 1) * P], ident[:, :])
                        last.then_inc(s["hn_turned"], 1)

                    def scatter(k, j):
                        pe.wait_ge(s["m_lo"], k + 1)
                        first, end = isinstance(k, int) and k == 0, isinstance(k, int) and k == TILES - 1
                        for h in range(HALVES):
                            a = to_dst[:, j, h * P:(h + 1) * P]
                            for part in (m_hi, m_lo):
                                one, two = first and part is m_hi, end and part is m_lo
                                if h == 0:
                                    pe.matmul(PS[0:NH2, 1, 0:N], part[:, j, D:WIDE], to_dst[:, j, :], start=one,
                                              stop=two, skip_group_check=True)
                                last = pe.matmul(PS[:, 6 + h, :], a, part[:, j, 0:D], start=one, stop=two,
                                                 skip_group_check=True)
                        last.then_inc(s["scattered"], 1)

                    pe.wait_ge(s["split"], 1)
                    turn_hot(0, 0)

                    def body(k, j):
                        fixed = isinstance(k, int)
                        hidden(k, j)
                        if not (fixed and k == TILES - 1):
                            turn_hot(k + 1, 1 - j)
                        if not keys and not (fixed and k < 3):
                            scatter(k - 3, 1 - j)
                        if not (fixed and k == 0):
                            outer(k - 1, 1 - j)
                        turn_normed(k, j)

                    over_tiles(pe, body, head=4)
                    if not keys:
                        scatter(TILES - 3, 1)
                    outer(TILES - 1, 1)
                    if not keys:
                        scatter(TILES - 2, 0)
                        scatter(TILES - 1, 1)

                @block.scalar
                def _(act):
                    def leave(k, j):
                        act.wait_ge(s["f1"], k + 1)
                        guard(act, s["hidden"], k, 2)
                        act.activation(ef_hi[:, j, :], PS[:, 5, 0:P], ACT.Copy).then_inc(s["ef_hi"], 1)
                        if keys:
                            guard(act, s["q_done"], k, 2)
                        act.activation(pick[:, j, :], PS[:, 4, 0:n_hot * P], ACT.Copy).then_inc(s["ef_out"], 1)

                    def weigh(k, j):
                        act.wait_ge(s["used"], k + 1)
                        guard(act, s["scattered"], k, 2)
                        act.activation(m_hi[:, j, :], full[:, j, :], ACT.Copy).then_inc(s["m_hi"], 1)

                    leave(0, 0)

                    def body(k, j):
                        fixed = isinstance(k, int)
                        act.wait_ge(s["varied"], k + 1)
                        act.activation(rstd[:, j:j + 1], rstd[:, j:j + 1], ACT.Sqrt).then_inc(s["rooted"], 1)
                        if not (fixed and k == TILES - 1):
                            leave(k + 1, 1 - j)
                        act.wait_ge(s["scaled"], k + 1)
                        guard(act, s["hn_turned"], k, 2)
                        act.activation(hn[:, j, :], PS[:, 0, :], ACT.Identity, bias=shift[:, j:j + 1],
                                       scale=rstd[:, j:j + 1]).then_inc(s["normed"], 1)
                        if keys:
                            act.wait_ge(s["q_done"], k + 1)
                            guard(act, s["used"], k, 2)
                            act.activation(qs[:, j, :], PS[:, 1, :], ACT.Copy).then_inc(s["q_out"], 1)
                        act.wait_ge(s["hn_turned"], k + 1)
                        guard(act, s["r_lo"], k, 2)
                        for c in range(C):
                            last = act.activation(rT[:, j, c * P:(c + 1) * P], PS[:, 2, c * P:(c + 1) * P], ACT.Relu,
                                                  bias=offset[:, c:c + 1], scale=gain[:, c:c + 1])
                        last.then_inc(s["relued"], 1)
                        act.wait_ge(s["relued"], k + 1)
                        guard(act, s["f4"], k, 2)
                        act.activation(r_hi[:, j, :], rT[:, j, :], ACT.Copy).then_inc(s["r_hi"], 1)
                        if not keys and not (fixed and k == 0):
                            weigh(k - 1, 1 - j)

                    over_tiles(act, body, head=4)
                    if not keys:
                        weigh(TILES - 1, 1)

                @block.vector
                def _(dve):
                    chain = Chain(dve, s["v"])
                    for a, hi, lo in ((flat(W2e), flat(W_hi[:, :, :]), flat(W_lo[:, :, :])), (W1b, B_hi[:, :], B_lo[:, :]),
                                      (flat(table), flat(A_hi[:, :, :]), flat(A_lo[:, :, :]))):
                        chain.link(dve.tensor_copy(hi, a))
                        last = dve.tensor_tensor(lo, a, hi.bitcast(F32), ALU.subtract)
                    last.then_inc(s["split"], 1)
                    steps = chain.n

                    def hot(k, j):
                        dve.wait_ge(s[f"rows{j}"], 8 * (k - j) + 16)
                        guard(dve, s["f1"], k, 2)
                        if keys:
                            dve.tensor_scalar(hots[:, 2 + j, :], iota[:, :], rowt[:, j, EF + 1:ROW], None, ALU.is_equal)
                        dve.tensor_scalar(hots[:, j, :], iota[:, :], rowt[:, j, EF:EF + 1], None,
                                          ALU.is_equal).then_inc(s["hot"], 1)

                    def save(k, j):
                        dve.tensor_copy(sdst[:, bass.ds(k, 1), :].rearrange("p a b -> p (a b)"),
                                        rowt[:, j, EF:ROW]).then_inc(s["saved"], 1)

                    def low_ef(k, j):
                        dve.wait_ge(s["ef_hi"], k + 1)
                        guard(dve, s["hidden"], k, 2)
                        dve.tensor_tensor(ef_lo[:, j, :], PS[:, 5, 0:P], ef_hi[:, j, :].bitcast(F32),
                                          ALU.subtract).then_inc(s["ef_lo"], 1)

                    def low_r(k, j):
                        dve.wait_ge(s["r_hi"], k + 1)
                        guard(dve, s["f4"], k, 2)
                        dve.tensor_tensor(r_lo[:, j, :], rT[:, j, :], r_hi[:, j, :].bitcast(F32),
                                          ALU.subtract).then_inc(s["r_lo"], 1)

                    def low_m(k, j):
                        dve.wait_ge(s["m_hi"], k + 1)
                        guard(dve, s["scattered"], k, 2)
                        dve.tensor_tensor(m_lo[:, j, :], full[:, j, :], m_hi[:, j, :].bitcast(F32),
                                          ALU.subtract).then_inc(s["m_lo"], 1)

                    def use(k, j):
                        dve.wait_ge(s["f4"], k + 1)
                        Lk = L[:, bass.ds(k, 1), :].rearrange("p a b -> p (a b)")
                        if keys:
                            dve.wait_ge(s["q_out"], k + 1)
                            dve.tensor_tensor(prod, PS[:, 3, :], qs[:, j, :], ALU.mult).then_inc(s["v"], 1)
                            dve.wait_ge(s["v"], 2 * k + steps + 1)
                            dve.tensor_reduce(Lk, prod.rearrange("p (a b) -> p a b", a=NH2), AX_X,
                                              ALU.add).then_inc(s["v"], 1)
                            dve.tensor_scalar(penF[:, bass.ds(k, 1)], PS[:, 6 + j, NH2:NH2 + 1],
                                              small["place"][:, bass.ds(k, 1)], FAR, ALU.is_equal, ALU.mult)
                            dve.tensor_scalar(penL[:, bass.ds(k, 1)], PS[:, 6 + j, NH2 + 1:NX],
                                              small["place1"][:, bass.ds(k, 1)], FAR, ALU.is_equal, ALU.mult)
                            dve.wait_ge(s["v"], 2 * k + steps + 2)
                            dve.tensor_tensor(Lk, Lk, PS[:, 6 + j, 0:NH2], ALU.add).then_inc(s["used"], 1)
                        else:
                            guard(dve, s["scattered"], k, 2)
                            dve.wait_ge(s["saved"], k + 1)
                            dve.tensor_scalar(to_dst[:, j, :], iota[:, :], sdst[:, bass.ds(k, 1), 1], None, ALU.is_equal)
                            guard(dve, s["m_lo"], k, 2)
                            dve.tensor_copy(full[:, j, D:WIDE], Lk)
                            dve.tensor_tensor(full[:, j, 0:D].rearrange("p (a b) -> p a b", a=NH2),
                                              PS[:, 3, :].rearrange("p (a b) -> p a b", a=NH2),
                                              Lk.unsqueeze(2).broadcast_to([P, NH2, HD2]), ALU.mult).then_inc(s["used"], 1)

                    hot(0, 0)
                    hot(1, 1)
                    save(0, 0)
                    low_ef(0, 0)
                    stat = s["stat"]

                    def body(k, j):
                        fixed = isinstance(k, int)
                        dve.wait_ge(s["hidden"], k + 1)
                        guard(dve, s["normed"], k, 2)
                        dve.bn_stats(stats[:, j, :], PS[:, 0, :]).then_inc(stat, 1)
                        dve.wait_ge(stat, 3 * k + 1)
                        if not (fixed and k == TILES - 1):
                            save(k + 1, 1 - j)
                        dve.bn_aggr(mv[:, j, :], stats[:, j, :]).then_inc(stat, 1)
                        dve.wait_ge(stat, 3 * k + 2)
                        dve.tensor_scalar(rstd[:, j:j + 1], mv[:, j, 1:2], EPS, None, ALU.add).then_inc(s["varied"], 1)
                        if not (fixed and k == 0):
                            low_r(k - 1, 1 - j)
                        dve.wait_ge(s["rooted"], k + 1)
                        dve.reciprocal(rstd[:, j:j + 1], rstd[:, j:j + 1]).then_inc(stat, 1)
                        dve.wait_ge(stat, 3 * k + 3)
                        dve.tensor_scalar(shift[:, j:j + 1], mv[:, j, 0:1], rstd[:, j:j + 1], -1.0, ALU.mult,
                                          ALU.mult).then_inc(s["scaled"], 1)
                        if not (fixed and k == TILES - 1):
                            low_ef(k + 1, 1 - j)
                        if keys and not (fixed and k >= TILES - 2):
                            hot(k + 2, j)
                        if not keys and not (fixed and k < 2):
                            low_m(k - 2, j)
                        if not (fixed and k == 0):
                            use(k - 1, 1 - j)
                        if not keys and not (fixed and k >= TILES - 2):
                            hot(k + 2, j)

                    over_tiles(dve, body, head=4)
                    low_r(TILES - 1, 1)
                    if not keys:
                        low_m(TILES - 2, 0)
                    use(TILES - 1, 1)
                    if not keys:
                        low_m(TILES - 1, 1)

        edge_pass("gnn2_keys", True, W2["hk_W1b"][:, 0, :], W2["hk_W2"], *cols2["hk"], node_k)

        with Stage(nc, "gnn2_pens") as st:
            penT = st.sb("penT", [TILES, 2, P])
            turned, out_, stored = st.sem("turned"), st.sem("out"), st.sem("stored")
            block = st.block()

            @block.tensor
            def _(pe):
                pe.transpose(PS[0:TILES, 0, 0:P], penF[:, :], ident[:, :])
                pe.transpose(PS[0:TILES, 0, P:2 * P], penL[:, :], ident[:, :]).then_inc(turned, 1)

            @block.vector
            def _(dve):
                dve.wait_ge(turned, 1)
                dve.tensor_copy(flat(penT[:, :, :]), PS[0:TILES, 0, 0:2 * P]).then_inc(out_, 1)

            @block.sync
            def _(sp):
                sp.wait_ge(out_, 1)
                sp.dma_start(pens.rearrange("a (t p) -> t a p", p=P), penT[:, :, :]).then_inc(stored, 16)
                sp.wait_ge(stored, 16)

        with Stage(nc, "gnn2_max") as st:
            CK = 4 * P
            STEPS = E // CK
            F = R0[0:NH2, 0:E]
            pf = st.sb("pf", [NH2, 4, CK])
            back = st.sb("back", [NH2, 2, CK])
            names = ("pen_in0", "pen_in1", "pen_in2", "pen_in3", "turned", "scanned", "scanned_back", "returned", "shifted", "exped")
            s = {n: st.sem(n) for n in names}
            block = st.block()
            order = list(range(STEPS)) + list(reversed(range(STEPS)))

            @block.sync
            def _(sp):
                for q, chunk in enumerate(order):
                    if q >= 4:
                        if q - 4 < STEPS:
                            sp.wait_ge(s["scanned"], q - 3)
                        else:
                            sp.wait_ge(s["scanned_back"], q - 3 - STEPS)
                    sp.dma_start(pf[:, q % 4, :], pens[int(q >= STEPS):int(q >= STEPS) + 1, chunk * CK:(chunk + 1) * CK]
                                 .broadcast_to([NH2, CK])).then_inc(s[f"pen_in{q % 4}"], 16)

            @block.tensor
            def _(pe):
                for q in range(STEPS):
                    if q >= 2:
                        pe.wait_ge(s["scanned"], q - 1)
                    for m in range(4):
                        last = pe.transpose(PS[0:NH2, q % 2, m * P:(m + 1) * P], L[:, 4 * q + m, :], ident[:, :])
                    last.then_inc(s["turned"], 1)
                for q in range(STEPS):
                    pe.wait_ge(s["scanned_back"], q + 1)
                    if q >= 2:
                        pe.wait_ge(s["shifted"], q - 1)
                    for m in range(4):
                        last = pe.transpose(PS[:, 2 + q % 2, m * NH2:(m + 1) * NH2], back[:, q % 2, m * P:(m + 1) * P],
                                            ident[0:NH2, 0:NH2])
                    last.then_inc(s["returned"], 1)

            @block.vector
            def _(dve):
                for q in range(STEPS):
                    dve.wait_ge(s["turned"], q + 1)
                    dve.wait_ge(s[f"pen_in{q % 4}"], 16 * (q // 4) + 16)
                    if q:
                        dve.wait_ge(s["scanned"], q)
                    dve.tensor_tensor_scan(F[:, q * CK:(q + 1) * CK], pf[:, q % 4, :], PS[0:NH2, q % 2, :],
                                           0.0 if q == 0 else F[:, q * CK - 1:q * CK], ALU.add,
                                           ALU.max).then_inc(s["scanned"], 1)
                dve.wait_ge(s["scanned"], STEPS)

                def shift(q):
                    chunk = STEPS - 1 - q
                    dve.wait_ge(s["returned"], q + 1)
                    a = flat(L[:, 4 * chunk:4 * chunk + 4, :])
                    dve.tensor_tensor(a, a, PS[:, 2 + q % 2, 0:4 * NH2], ALU.subtract).then_inc(s["shifted"], 1)

                for q in range(STEPS):
                    chunk = STEPS - 1 - q
                    dve.wait_ge(s[f"pen_in{(STEPS + q) % 4}"], 16 * ((STEPS + q) // 4) + 16)
                    if q >= 2:
                        dve.wait_ge(s["returned"], q - 1)
                    if q:
                        dve.wait_ge(s["scanned_back"], q)
                    dve.tensor_tensor_scan(back[:, q % 2, ::-1], pf[:, (STEPS + q) % 4, ::-1],
                                           F[:, chunk * CK:(chunk + 1) * CK][:, ::-1],
                                           0.0 if q == 0 else back[:, 1 - q % 2, 0:1], ALU.add,
                                           ALU.max).then_inc(s["scanned_back"], 1)
                    if q:
                        shift(q - 1)
                shift(STEPS - 1)

            @block.scalar
            def _(act):
                act.wait_ge(s["shifted"], STEPS)
                act.activation(flat(L[:, :, :]), flat(L[:, :, :]), ACT.Exp)

        edge_pass("gnn2_values", False, W2["hv_W1b"][:, 0, :], W2["hv_W2"], *cols2["hv"], node_v)
        mixed = R0[:, 0:1024].rearrange("p (h d) -> p h d", h=2)
        mixedT = R0[:, 1024:2048].rearrange("p (c n) -> p c n", c=C)
        with Stage(nc, "gnn2_mean") as st:
            den, inv = st.sb("den", [P, HALVES, NH2]), st.sb("inv", [P, HALVES, NH2])
            denT = st.sb("denT", [NH2, N])
            v, ready, turned, den_out, den_turned = (st.sem(n) for n in ("v", "ready", "turned", "den_out", "den_turned"))
            block = st.block()
            spare = R0[:, 2048:3072].rearrange("p (h d) -> p h d", h=2)
            heads = lambda a: a.rearrange("p (a b) -> p a b", a=NH2)
            wide = lambda a: a.unsqueeze(2).broadcast_to([P, NH2, HD2])

            @block.vector
            def _(dve):
                chain = Chain(dve, v)
                dve.tensor_copy(denT[:, :], PS[0:NH2, 1, 0:N]).then_inc(den_out, 1)
                dve.wait_ge(den_turned, 1)
                chain.link(dve.tensor_copy(flat(den[:, :, :]), PS[:, 0, 0:2 * NH2]))
                chain.link(dve.tensor_scalar(flat(inv[:, :, :]), flat(den[:, :, :]), 1e-30, None, ALU.max))
                chain.link(dve.reciprocal(flat(inv[:, :, :]), flat(inv[:, :, :])))
                chain.link(dve.tensor_tensor(flat(den[:, :, :]), flat(den[:, :, :]), flat(inv[:, :, :]), ALU.mult))
                for h in range(HALVES):
                    chain.link(dve.tensor_tensor(heads(mixed[:, h, :]), heads(PS[:, 6 + h, :]), wide(inv[:, h, :]), ALU.mult))
                    chain.link(dve.tensor_tensor(heads(spare[:, h, :]), heads(rows2["hv_b2"]), wide(den[:, h, :]), ALU.mult))
                    dve.tensor_tensor(mixed[:, h, :], mixed[:, h, :], spare[:, h, :], ALU.add).then_inc(ready, 1)

            @block.tensor
            def _(pe):
                pe.wait_ge(den_out, 1)
                for h in range(HALVES):
                    last = pe.transpose(PS[:, 0, h * NH2:(h + 1) * NH2], denT[:, h * P:(h + 1) * P],
                                        ident[0:NH2, 0:NH2])
                last.then_inc(den_turned, 1)
                for h in range(HALVES):
                    pe.wait_ge(ready, h + 1)
                    for c in range(C):
                        last = pe.transpose(PS[:, 2 + h, c * P:(c + 1) * P], mixed[:, h, c * P:(c + 1) * P], ident[:, :])
                    last.then_inc(turned, 1)

            @block.scalar
            def _(act):
                for h in range(HALVES):
                    act.wait_ge(turned, h + 1)
                    act.activation(mixedT[:, :, h * P:(h + 1) * P], PS[:, 2 + h, :].rearrange("p (c n) -> p c n", c=C),
                                   ACT.Copy)

        with Stage(nc, "gnn2_no") as st:
            done, v = st.sem("done"), st.sem("v")
            block = st.block()

            @block.tensor
            def _(pe):
                for h in range(HALVES):
                    for c in range(C):
                        last = pe.matmul(PS[:, h, :], mixedT[:, c, h * P:(h + 1) * P], W2["no_W1"][:, c, :],
                                         start=(c == 0), stop=(c == C - 1))
                    last.then_inc(done, 1)

            @block.vector
            def _(dve):
                chain = Chain(dve, v)
                for h in range(HALVES):
                    chain.link(dve.tensor_tensor(X[:, h, :], X[:, h, :], XN[:, h, :], ALU.add))
                    dve.wait_ge(done, h + 1)
                    chain.link(dve.tensor_tensor(hid_no[:, h, :], hid_no[:, h, :], PS[:, h, :], ALU.add))

        norm_and_turn("gnn2_nonorm", affine=cols2["no"], source=hid_no, into=hid_no, func=ACT.Relu)
        project("gnn2_last", [(HT, W2["no_W2"], C)], rows2["no_b2"], mixed)
        with Stage(nc, "gnn2_add") as st:
            block = st.block()

            @block.vector
            def _(dve):
                dve.tensor_tensor(flat(X[:, :, :]), flat(X[:, :, :]), flat(mixed), ALU.add)
        q2.close()
        weights.close()
        NE2, F2 = 8, 32
        weights = layer("ffn2")
        norm_and_turn("ffn2_norm", loads="ffn2")
        route("ffn2_route", NE2, small["ffn2_Wg"], bias=small["ffn2_bg"])
        nC = NE2 * F2 // P
        mix("ffn2_mix", [(P, small["expand2"][:, k * P:(k + 1) * P], None) for k in range(nC)] + [(F2, None, 0.5)],
            r0(0, (3, N)), ACT.Relu, lambda c, k, u: small["ffn2_W1"][:, c, k * P:k * P + u], small["ffn2_b1"],
            lambda k, u: small["ffn2_W2"][0:u, k, :], small["ffn2_bs2"], 0.5, n_exp=NE2, b2=small["ffn2_b2"])
        weights.close()

        NE3, F3, UN = 8, 2048, 512
        Q3 = F3 // UN
        unit = [(r0(4096 * q, (C, UN)), r0(4096 * q + 2048, (UN // P, D))) for q in range(Q3)]

        def load_unit(sp, e, q):
            W1d, W2d = t["L3_ffn_W1"], t["L3_ffn_W2"]
            return ((unit[q][0], W1d[bass.ds(e, 1), :, q * UN:(q + 1) * UN].rearrange("e (c p) n -> p (e c) n", p=P)),
                    (unit[q][1], W2d[bass.ds(e, 1), q * UN:(q + 1) * UN, :].rearrange("e (c p) n -> p (e c) n", p=P)))

        weights = layer("gnn3")
        Wi, Wj = r1(0, (C, D)), r1(2048, (C, D))

        def own_and_next(sp):
            for w, name in ((Wi, "gnn3_Wi"), (Wj, "gnn3_Wj")):
                sp.dma_start(w, t[name].rearrange("(c p) n -> p c n", p=P)).then_inc(w_gnn3, 16)
            for q in range(Q3):
                for b, (w, a) in enumerate(load_unit(sp, 0, q)):
                    sp.dma_start(w, a).then_inc(unit_in[2 * q + b], 16)

        norm_and_turn("gnn3_norm", loads="gnn3", large=own_and_next)
        nodes = R1[:, 4096:6144].rearrange("p (a h d) -> p a h d", a=2, h=2)
        project("gnn3_i", [(HT, Wi, C)], small["gnn3_b"], nodes[:, 0], [(w_gnn3, 32)])
        project("gnn3_j", [(HT, Wj, C)], small["gnn3_zero"], nodes[:, 1])
        q3 = ExitStack()
        T_hi, T_lo = (q3.enter_context(nc.sbuf_tensor(n, [P, 4, D], F32R)) for n in ("T_hi", "T_lo"))
        split("gnn3_split", [(R1[:, 4096:6144], T_hi[:, :, :].rearrange("p a b -> p (a b)"),
                              T_lo[:, :, :].rearrange("p a b -> p (a b)"))])
        with Stage(nc, "gnn3_edges") as st:
            hots = R1[:, 6144:7168].rearrange("p (a n) -> p a n", a=4)
            overlay = lambda label, at, shape: nc.alloc_sbuf_tensor_at(f"gnn3_{label}", shape, F32R, offset=r1_at + at)
            pick = overlay("pick", 28672, [P, 2, 4 * P])
            m_hi, m_lo = overlay("m_hi", 32768, [P, 2, D]), overlay("m_lo", 36864, [P, 2, D])
            to_src = overlay("to_src", 40960, [P, 2, N])
            names = ("hot", "f1", "f1_out", "picked", "m_hi", "m_lo", "summed", "v")
            s = {n: st.sem(n) for n in names}
            block = st.block()

            @block.tensor
            def _(pe):
                def front(k, j):
                    pe.wait_ge(s["hot"], k + 1)
                    guard(pe, s["f1_out"], k, 1)
                    for q in range(4):
                        last = pe.transpose(PS[:, 4, q * P:(q + 1) * P],
                                            hots[:, 2 * (q // 2) + j, (q % 2) * P:(q % 2 + 1) * P], ident[:, :])
                    last.then_inc(s["f1"], 1)

                def gather(k, j):
                    pe.wait_ge(s["f1_out"], k + 1)
                    guard(pe, s["m_lo"], k, 2)
                    for q in range(4):
                        pe.matmul(PS[:, 2 + j, :], pick[:, j, q * P:(q + 1) * P], T_hi[:, q, :], start=(q == 0), stop=False)
                        last = pe.matmul(PS[:, 2 + j, :], pick[:, j, q * P:(q + 1) * P], T_lo[:, q, :], start=False,
                                         stop=(q == 3))
                    last.then_inc(s["picked"], 1)

                def back(k, j):
                    pe.wait_ge(s["m_lo"], k + 1)
                    first, end = isinstance(k, int) and k == 0, isinstance(k, int) and k == TILES - 1
                    for h in range(HALVES):
                        for part in (m_hi, m_lo):
                            last = pe.matmul(PS[:, 6 + h, :], to_src[:, j, h * P:(h + 1) * P], part[:, j, :],
                                             start=first and part is m_hi, stop=end and part is m_lo,
                                             skip_group_check=True)
                    last.then_inc(s["summed"], 1)

                def body(k, j):
                    if not (isinstance(k, int) and k == TILES - 1):
                        front(k + 1, 1 - j)
                    gather(k, j)
                    if not (isinstance(k, int) and k == 0):
                        back(k - 1, 1 - j)

                front(0, 0)
                over_tiles(pe, body)
                back(TILES - 1, 1)

            @block.scalar
            def _(act):
                def leave(k, j):
                    act.wait_ge(s["f1"], k + 1)
                    guard(act, s["picked"], k, 2)
                    act.activation(pick[:, j, :], PS[:, 4, :], ACT.Copy).then_inc(s["f1_out"], 1)

                def body(k, j):
                    if not (isinstance(k, int) and k == TILES - 1):
                        leave(k + 1, 1 - j)
                    act.wait_ge(s["picked"], k + 1)
                    guard(act, s["summed"], k, 2)
                    act.activation(m_hi[:, j, :], PS[:, 2 + j, :], ACT.Relu).then_inc(s["m_hi"], 1)

                leave(0, 0)
                over_tiles(act, body)

            @block.vector
            def _(dve):
                def hot(k, j):
                    guard(dve, s["f1"], k, 2)
                    dve.tensor_scalar(hots[:, j, :], iota[:, :], src_col[:, bass.ds(k, 1)], None, ALU.is_equal)
                    dve.tensor_scalar(hots[:, 2 + j, :], iota[:, :], dst_col[:, bass.ds(k, 1)], None,
                                      ALU.is_equal).then_inc(s["hot"], 1)

                def body(k, j):
                    if not (isinstance(k, int) and k >= TILES - 2):
                        hot(k + 2, j)
                    guard(dve, s["summed"], k, 2)
                    dve.tensor_scalar(to_src[:, j, :], iota[:, :], src_col[:, bass.ds(k, 1)], None, ALU.is_equal)
                    dve.wait_ge(s["m_hi"], k + 1)
                    dve.scalar_tensor_tensor(m_lo[:, j, :], PS[:, 2 + j, :], 0.0, m_hi[:, j, :].bitcast(F32), ALU.max,
                                             ALU.subtract).then_inc(s["m_lo"], 1)

                hot(0, 0)
                hot(1, 1)
                over_tiles(dve, body)
                chain = Chain(dve, s["v"])
                dve.wait_ge(s["summed"], TILES)
                for h in range(HALVES):
                    chain.link(dve.tensor_tensor(X[:, h, :], X[:, h, :], PS[:, 6 + h, :], ALU.add))
        q3.close()
        weights.close()

        weights = layer("ffn3")
        norm_and_turn("ffn3_norm", passes=2, affine=(small["ffn3_ln"][:, 0:C], small["ffn3_ln"][:, C:2 * C]),
                      loads="ffn3")
        route("ffn3_route", NE3, small["ffn3_wr"], bias=small["ffn3_br"])
        H_hi, H_lo = (weights.enter_context(nc.sbuf_tensor(n, [P, C, N], F32R)) for n in ("H_hi", "H_lo"))
        split("ffn3_split", [(flat(HT[:, :, :]), flat(H_hi[:, :, :]), flat(H_lo[:, :, :]))])
        with Stage(nc, "ffn3_experts") as st:
            FU = UN // P
            overlay = lambda label, at, shape: nc.alloc_sbuf_tensor_at(f"ffn3_{label}", shape, F32R, offset=at)
            sel = R1[0:NE3, 0:NE3 * P].rearrange("p (e n) -> p e n", e=NE3)
            spread_gates = R1[:, 1024:3072].rearrange("p (e n) -> p e n", e=NE3)
            hid = R1[:, 3072:3072 + 2 * FU * N].rearrange("p (j f n) -> p j f n", j=2, f=FU)
            hid_hi = overlay("hid_hi", r1_at + 4 * 5120, [P, 2, FU, N])
            hid_lo = overlay("hid_lo", r1_at + 4 * 7168, [P, 2, FU, N])
            low = [(overlay(f"W1_lo{q}", r0_at + 16384 * q, [P, C, UN]),
                    overlay(f"W2_lo{q}", r0_at + 16384 * q + 8192, [P, FU, D])) for q in range(Q3)]
            high = [(overlay(f"W1_hi{j}", r1_at + 4 * 9216 + 16384 * j, [P, C, UN]),
                     overlay(f"W2_hi{j}", r1_at + 4 * 9216 + 16384 * j + 8192, [P, FU, D])) for j in range(2)]
            names = ("ins", "spread_", "spread_out", "w1_hi", "w1_lo", "w2_hi", "w2_lo", "h_done", "h_out", "gated",
                     "hid_hi", "hid_lo", "y_done", "all_done", "v")
            s = {n: st.sem(n) for n in names}
            b1c = small["ffn3_b1"]
            block = st.block()

            def unit_guard(eng, semaphore, e, q, back):
                if not (isinstance(e, int) and Q3 * e + q < back):
                    eng.wait_ge(semaphore, Q3 * e + (q + 1 - back))

            def over_units(eng, expert):
                expert(0)
                with eng.Fori(1, NE3 - 1) as e:
                    expert(e)
                expert(NE3 - 1)

            def following(e, q, ahead):
                e2, q2 = e + (q + ahead) // Q3, (q + ahead) % Q3
                return None if isinstance(e, int) and e2 >= NE3 else (e2, q2)

            @block.sync
            def _(sp):
                sp.dma_start(sel, t["select8"]).then_inc(s["ins"], 16)
                with sp.Fori(1, NE3) as e:
                    for q in range(Q3):
                        for b, (w, a) in enumerate(load_unit(sp, e, q)):
                            sp.wait_ge(s["y_done"] if b else s["h_done"], 4 * e + (q - 3))
                            sp.dma_start(w, a).then_inc(unit_in[2 * q + b], 16)

            @block.tensor
            def _(pe):
                pe.wait_ge(s["ins"], 16)
                for e in range(NE3):
                    last = pe.matmul(PS[:, e // 2, (e % 2) * N:(e % 2 + 1) * N], sel[:, e, :], gatesT[0:NE3, :],
                                     start=True, stop=True, skip_group_check=True)
                last.then_inc(s["spread_"], 1)
                pe.wait_ge(s["spread_out"], 1)

                def hidden(e, q):
                    W_hi, W_lo = high[q % 2][0], low[q][0]
                    pe.wait_ge(s["w1_lo"], Q3 * e + (q + 1))
                    unit_guard(pe, s["h_out"], e, q, 2)
                    for f in range(FU):
                        out = PS[:, 2 * (q % 2) + f // 2, (f % 2) * N:(f % 2 + 1) * N]
                        for c in range(C):
                            a, b = W_hi[:, c, f * P:(f + 1) * P], W_lo[:, c, f * P:(f + 1) * P]
                            pe.matmul(out, a, H_hi[:, c, :], start=(c == 0), stop=False, skip_group_check=True)
                            pe.matmul(out, a, H_lo[:, c, :], start=False, stop=False, skip_group_check=True)
                            last = pe.matmul(out, b, H_hi[:, c, :], start=False, stop=(c == C - 1), skip_group_check=True)
                    last.then_inc(s["h_done"], 1)

                def outer(e, q):
                    W_hi, W_lo = high[q % 2][1], low[q][1]
                    pe.wait_ge(s["w2_lo"], Q3 * e + (q + 1))
                    pe.wait_ge(s["hid_lo"], Q3 * e + (q + 1))
                    first = isinstance(e, int) and e == 0 and q == 0
                    for h in range(HALVES):
                        for f in range(FU):
                            a, b = (x[:, q % 2, f, h * P:(h + 1) * P] for x in (hid_hi, hid_lo))
                            pe.matmul(PS[:, 6 + h, :], a, W_hi[:, f, :], start=first and f == 0, stop=False,
                                      skip_group_check=True)
                            pe.matmul(PS[:, 6 + h, :], a, W_lo[:, f, :], start=False, stop=False, skip_group_check=True)
                            last = pe.matmul(PS[:, 6 + h, :], b, W_hi[:, f, :], start=False, stop=False,
                                             skip_group_check=True)
                    last.then_inc(s["y_done"], 1)

                def expert(e):
                    for q in range(Q3):
                        if following(e, q, 1):
                            hidden(*following(e, q, 1))
                        outer(e, q)

                hidden(0, 0)
                over_units(pe, expert)
                for h in range(HALVES):
                    last = pe.matmul(PS[:, 6 + h, :], gatesT[0:NE3, h * P:(h + 1) * P], small["ffn3_b2"][:, :],
                                     start=False, stop=True, skip_group_check=True)
                last.then_inc(s["all_done"], 1)

            @block.scalar
            def _(act):
                def high_of(e, q, b):
                    act.wait_ge(unit_in[2 * q + b], 16 * e + 16)
                    unit_guard(act, s["y_done"] if b else s["h_done"], e, q, 2)
                    act.activation(flat(high[q % 2][b][:, :, :]), flat(unit[q][b]), ACT.Copy).then_inc(
                        s["w2_hi"] if b else s["w1_hi"], 1)

                def expert(e):
                    for q in range(Q3):
                        act.wait_ge(s["h_done"], Q3 * e + (q + 1))
                        unit_guard(act, s["hid_lo"], e, q, 2)
                        for f in range(FU):
                            last = act.activation(hid[:, q % 2, f, :],
                                                  PS[:, 2 * (q % 2) + f // 2, (f % 2) * N:(f % 2 + 1) * N], ACT.Gelu,
                                                  bias=b1c[:, bass.ds(e, 1), q * FU + f])
                        last.then_inc(s["h_out"], 1)
                        if following(e, q, 2):
                            high_of(*following(e, q, 2), 0)
                        act.wait_ge(s["gated"], Q3 * e + (q + 1))
                        unit_guard(act, s["y_done"], e, q, 2)
                        act.activation(flat(hid_hi[:, q % 2, :, :]), flat(hid[:, q % 2, :, :]), ACT.Copy).then_inc(s["hid_hi"], 1)
                        if following(e, q, 1):
                            high_of(*following(e, q, 1), 1)

                high_of(0, 0, 0)
                high_of(0, 0, 1)
                high_of(0, 1, 0)
                over_units(act, expert)

            @block.vector
            def _(dve):
                chain = Chain(dve, s["v"])
                for h in range(HALVES):
                    chain.link(dve.tensor_tensor(X[:, h, :], X[:, h, :], XN[:, h, :], ALU.add))
                dve.wait_ge(s["spread_"], 1)
                for b in range(4):
                    last = dve.tensor_copy(flat(spread_gates[:, 2 * b:2 * b + 2, :]), PS[:, b, :])
                last.then_inc(s["spread_out"], 1)

                def low_of(e, q, b):
                    dve.wait_ge(s["w2_hi"] if b else s["w1_hi"], Q3 * e + (q + 1))
                    dve.tensor_tensor(flat(low[q][b][:, :, :]), flat(unit[q][b]),
                                      flat(high[q % 2][b][:, :, :]).bitcast(F32), ALU.subtract).then_inc(
                        s["w2_lo"] if b else s["w1_lo"], 1)

                def expert(e):
                    for q in range(Q3):
                        a = hid[:, q % 2, :, :]
                        dve.wait_ge(s["h_out"], Q3 * e + (q + 1))
                        dve.tensor_tensor(a, a, spread_gates[:, bass.ds(e, 1), :].broadcast_to([P, FU, N]),
                                          ALU.mult).then_inc(s["gated"], 1)
                        if following(e, q, 2):
                            low_of(*following(e, q, 2), 0)
                        dve.wait_ge(s["hid_hi"], Q3 * e + (q + 1))
                        unit_guard(dve, s["y_done"], e, q, 2)
                        dve.tensor_tensor(flat(hid_lo[:, q % 2, :, :]), flat(a), flat(hid_hi[:, q % 2, :, :]).bitcast(F32),
                                          ALU.subtract).then_inc(s["hid_lo"], 1)
                        if following(e, q, 1):
                            low_of(*following(e, q, 1), 1)

                low_of(0, 0, 0)
                low_of(0, 0, 1)
                low_of(0, 1, 0)
                dve.wait_ge(s["spread_out"], 1)
                over_units(dve, expert)
                dve.wait_ge(s["all_done"], 1)
                for h in range(HALVES):
                    chain.link(dve.tensor_tensor(X[:, h, :], X[:, h, :], PS[:, 6 + h, :], ALU.add))
        weights.close()
        with Stage(nc, "result") as st:
            stored = st.sem("stored")
            block = st.block()

            @block.sync
            def _(sp):
                sp.dma_start(out.rearrange("(h p) d -> p h d", p=P), X[:, :, :]).then_inc(stored, 16)
                sp.wait_ge(stored, 16)


def _columns(a):
    return np.ascontiguousarray(np.moveaxis(a.reshape(-1, P, *a.shape[1:]), 0, 1))


def _constants():
    n = np.arange(P)
    return {
        "ident": np.eye(P, dtype=np.float32),
        "iota": np.broadcast_to(np.arange(N, dtype=np.float32), (P, N)).copy(),
        "pair": np.where(n[:, None] // 8 == n[None, :] // 8, 0.0, FAR).astype(np.float32),
    }


def _laid_out(i):
    f = lambda a: np.ascontiguousarray(np.asarray(a))
    o = {k: f(v) for k, v in i.items()}
    arrays = dict(_constants())
    arrays["x"] = o["x"]
    arrays["src"], arrays["dst"] = _columns(o["src"]), _columns(o["dst"])
    def diagonal(a, n):
        m = np.zeros((n * a.shape[0], n * a.shape[1]), a.dtype)
        for k in range(n):
            m[k * a.shape[0]:(k + 1) * a.shape[0], k * a.shape[1]:(k + 1) * a.shape[1]] = a
        return m

    attr17 = np.concatenate([o["edge_attr_16"].T, np.ones((1, E), np.float32)])
    arrays["attr16"] = f(attr17.reshape(17, TILES // 4, 4, P).transpose(2, 0, 1, 3).reshape(4 * 17, -1))
    arrays["We17"] = diagonal(np.concatenate([o["L0_gnn_We"], o["L0_gnn_be"][None]]), 4)
    arrays["qk_bias"] = f(np.stack([_columns(o["L0_gnn_bq"]), _columns(o["L0_gnn_bk"])], 1))
    for k in ("L0_gnn_Wq", "L0_gnn_Wk", "L0_gnn_Wv", "L0_gnn_Wo", "L0_gnn_bv", "L0_gnn_bo"):
        arrays[k] = o[k]
    twice = lambda a, axis: f(np.concatenate([a, a], axis))
    rows = lambda a: f(np.broadcast_to(a, (P, a.shape[-1])))
    chunks = lambda a: f(np.moveaxis(a.reshape(-1, P, a.shape[-1]), 0, 1))
    n = np.arange(2048)
    arrays |= {
        "ffn0_W1": f(np.moveaxis(o["L0_ffn_W1"], 0, 1).reshape(D, -1)), "L0_ffn_W2": f(o["L0_ffn_W2"].reshape(-1, D)),
        "expand0": (n[None] // 32 == np.arange(64)[:, None]).astype(np.float32),
        "L0_ffn_Ws1": o["L0_ffn_Ws1"], "L0_ffn_Ws2": o["L0_ffn_Ws2"],
        "ffn0_ln": f(np.concatenate([_columns(o["L0_ffn_" + k]) for k in ("ln1_g", "ln1_b", "ffln_g", "ffln_b")], 1)),
        "Wr": chunks(o["L0_ffn_Wr"]), "codebookT": f(o["L0_ffn_codebook"].T),
        "ffn0_b1": f(np.concatenate([_columns(o["L0_ffn_b1"].reshape(-1)), _columns(o["L0_ffn_bs1"])], 1)),
        "ffn0_bs2": rows(o["L0_ffn_bs2"]), "ffn0_b2": o["L0_ffn_b2"], "Wf1": chunks(o["L0_ffn_Wf1"]),
        "bf1": o["L0_ffn_bf1"][:, None], "Wf2": o["L0_ffn_Wf2"], "bf2": rows(o["L0_ffn_bf2"]),
    }
    arrays |= {
        "up0": o["L1_gnn_W_up0"], "up1": o["L1_gnn_W_up1"], "mlp1": diagonal(o["L1_gnn_W_mlp1"], 2),
        "mlp2": diagonal(o["L1_gnn_W_mlp2"], 2), "mlp3": diagonal(o["L1_gnn_W_mlp3"], 2), "mlp4": twice(o["L1_gnn_W_mlp4"], 0), "out0": chunks(o["L1_gnn_W_out0"]),
        "out1": chunks(o["L1_gnn_W_out1"]), "attr4": _columns(o["edge_attr_4"]), "attr8": f(o["edge_attr_8"].reshape(-1, 2, D, 8).transpose(1, 3, 0, 2).reshape(16, -1)),
        "L1_ffn_W1": o["L1_ffn_W1"], "L1_ffn_W2": o["L1_ffn_W2"],
    }
    node = _columns(np.arange(N))
    arrays |= {
        "ffn1_Wg": chunks(o["L1_ffn_Wg"]), "ffn1_b1": f(o["L1_ffn_b1"].reshape(8, 8, P).transpose(2, 0, 1)),
        "ffn1_b2": o["L1_ffn_b2"], "before": (np.arange(N) < node[..., None]).astype(np.float32),
        "select8": np.repeat(np.eye(8, dtype=np.float32)[:, :, None], P, 2),
    }
    g2 = lambda k: o["L2_gnn_" + k]
    place = (np.arange(TILES)[None] * P + np.arange(P)[:, None]).astype(np.float32)
    later = (n[:P, None] < n[None, :P]).astype(np.float32)
    arrays |= {
        "attr128": _columns(o["edge_attr_128"]), "place": place, "place1": place + 1,
        "masks": f(np.stack([later, 1 - later], 1)),
        "gnn2_rows": f(np.broadcast_to(np.stack([g2(k) for k in ("hk_b1", "hv_b1", "hq_b1", "hk_b2", "hv_b2", "hq_b2",
                                                                "no_b1", "no_b2")]), (P, 8, D))),
        "gnn2_cols": f(np.stack([_columns(g2(f"{m}_{k}")) for m in ("hk", "hv", "hq", "no") for k in ("g", "be")], 1)),
        "g2_hk_W1a": f(g2("hk_W1")[:D]), "g2_hk_W1b": f(g2("hk_W1")[D:]), "g2_hv_W1a": f(g2("hv_W1")[:D]),
        "g2_hv_W1b": f(g2("hv_W1")[D:]),
    } | {"g2_" + k: g2(k) for k in ("hq_W1", "hk_W2", "hv_W2", "hq_W2", "no_W1", "no_W2")}
    pad = lambda a: np.concatenate([a, np.zeros((P - a.shape[0], *a.shape[1:]), np.float32)])
    side = lambda a: np.moveaxis(a, 0, 1).reshape(D, -1)
    arrays |= {
        "ffn2_Wg": chunks(o["L2_ffn_Wg"]), "ffn2_bg": rows(o["L2_ffn_bg"]),
        "ffn2_W1": chunks(np.concatenate([side(o["L2_ffn_W1"]), o["L2_ffn_Ws1"]], 1)),
        "ffn2_b1": _columns(np.concatenate([o["L2_ffn_b1"].reshape(-1), pad(o["L2_ffn_bs1"])])),
        "ffn2_W2": chunks(np.concatenate([o["L2_ffn_W2"].reshape(-1, D), pad(o["L2_ffn_Ws2"])])),
        "ffn2_bs2": rows(o["L2_ffn_bs2"]), "ffn2_b2": o["L2_ffn_b2"],
        "expand2": (n[None, :N] // 32 == np.arange(8)[:, None]).astype(np.float32),
        "gnn3_Wi": f(o["L3_gnn_W"][:, :D].T), "gnn3_Wj": f(o["L3_gnn_W"][:, D:].T), "gnn3_b": rows(o["L3_gnn_b"]),
        "gnn3_zero": np.zeros((P, D), np.float32),
        "ffn3_ln": f(np.concatenate([_columns(o["L3_ffn_ln_g"]), _columns(o["L3_ffn_ln_b"])], 1)),
        "ffn3_wr": chunks(o["L3_ffn_w_r"].T), "ffn3_br": rows(o["L3_ffn_b_r"]),
        "ffn3_b1": f(o["L3_ffn_b1"].reshape(8, 16, P).transpose(2, 0, 1)), "ffn3_b2": o["L3_ffn_b2"],
        "L3_ffn_W1": o["L3_ffn_W1"], "L3_ffn_W2": o["L3_ffn_W2"],
    }
    return arrays


def kernel(**inputs):
    import concourse.bacc as _bacc
    from concourse.bass_utils import run_bass_kernel_spmd as _run

    nc = _bacc.Bacc("TRN2", target_bir_lowering=False, num_devices=1)
    arrays = _laid_out(inputs)
    t = {k: nc.dram_tensor(f"in_{k}", a.shape, mybir.dt.from_np(a.dtype), kind="ExternalInput").ap()
         for k, a in arrays.items()}
    out = nc.dram_tensor("out_0", (N, D), F32, kind="ExternalOutput").ap()
    build(nc, t, out)
    r = _run(nc, [{f"in_{k}": a for k, a in arrays.items()}], core_ids=[0])
    return r.results[0]["out_0"]
```
